# Optimizing a Trainium2 kernel written in Bass

```python
import numpy as np
import jax
import jax.numpy as jnp

def _softmax(x, axis=-1):
    return jax.nn.softmax(x, axis=axis)

def _gelu(x):
    return jax.nn.gelu(x, approximate=True)

def _silu(x):
    return jax.nn.silu(x)

def _sigmoid(x):
    return jax.nn.sigmoid(x)

def _layernorm(x, axis=-1, eps=1e-05):
    m = jnp.mean(x, axis=axis, keepdims=True)
    v = jnp.var(x, axis=axis, keepdims=True)
    return (x - m) / jnp.sqrt(v + eps)

def _scatter_add(tgt, idx, src, axis=0):
    return tgt.at[idx].add(src)

def _segment_sum(src, seg, n):
    return jax.ops.segment_sum(src, seg, n)
kernel_name = 'mk_adaln_d2_jaxref_r8_86e89a'

def setup_inputs(seed: int=0):
    np.random.seed(seed)
    _w = jnp.asarray

    def _L0_attn_setup():
        import jax, jax.numpy as jnp
        import numpy as np
        D_MODEL = 256
        NUM_HEADS = 16
        D_KV = D_MODEL // NUM_HEADS
        THETA = 10000.0
        N_LORA = 4
        RANK = 16
        BATCH = 2
        SEQ = 256

        def _adapter_ids(starts, batch):
            ids = jnp.searchsorted(starts, jnp.arange(batch), side='right') - 1
            return jnp.clip(ids, 0, starts.shape[0] - 1)

        def _multilora(x, ids, W, A, B):
            base = jnp.einsum('bsd,od->bso', x, W)
            Ai, Bi = (A[ids], B[ids])
            low = jnp.einsum('bsd,brd->bsr', x, Ai)
            return base + jnp.einsum('bsr,bor->bso', low, Bi)

        def _rope(x):
            d = x.shape[-1]
            pos = jnp.arange(x.shape[-2], dtype=jnp.float32)
            inv_freq = THETA ** (-jnp.arange(0, d, 2, dtype=jnp.float32) / d)
            ang = pos[:, None] * inv_freq[None, :]
            cos, sin = (jnp.cos(ang), jnp.sin(ang))
            x1, x2 = (x[..., 0::2], x[..., 1::2])
            o1 = x1 * cos - x2 * sin
            o2 = x1 * sin + x2 * cos
            return jnp.stack([o1, o2], axis=-1).reshape(x.shape)
        key = jax.random.key(seed)
        ks = jax.random.split(key, 16)
        s = 0.02
        inp = {'x': jax.random.normal(ks[0], (BATCH, SEQ, D_MODEL), jnp.float32), 'lora_start_indices': jnp.sort(jax.random.randint(ks[1], (N_LORA,), 0, BATCH)), 'Wq': jax.random.normal(ks[2], (D_MODEL, D_MODEL), jnp.float32) * s, 'Aq': jax.random.normal(ks[3], (N_LORA, RANK, D_MODEL), jnp.float32) * s, 'Bq': jax.random.normal(ks[4], (N_LORA, D_MODEL, RANK), jnp.float32) * s, 'Wk': jax.random.normal(ks[5], (D_MODEL, D_MODEL), jnp.float32) * s, 'Ak': jax.random.normal(ks[6], (N_LORA, RANK, D_MODEL), jnp.float32) * s, 'Bk': jax.random.normal(ks[7], (N_LORA, D_MODEL, RANK), jnp.float32) * s, 'Wv': jax.random.normal(ks[8], (D_MODEL, D_MODEL), jnp.float32) * s, 'Av': jax.random.normal(ks[9], (N_LORA, RANK, D_MODEL), jnp.float32) * s, 'Bv': jax.random.normal(ks[10], (N_LORA, D_MODEL, RANK), jnp.float32) * s, 'Wo': jax.random.normal(ks[11], (D_MODEL, D_MODEL), jnp.float32) * s, 'Ao': jax.random.normal(ks[12], (N_LORA, RANK, D_MODEL), jnp.float32) * s, 'Bo': jax.random.normal(ks[13], (N_LORA, D_MODEL, RANK), jnp.float32) * s}
        return inp
    _L0_attn_in = _L0_attn_setup()

    def _L0_ffn_setup():
        import jax, jax.numpy as jnp
        import numpy as np
        HIDDEN = 256
        INTER = 176
        NUM_EXPERTS = 16
        TOP_K = 2
        BATCH, SEQ = (2, 256)
        key = jax.random.key(seed)
        ks = jax.random.split(key, 5)
        scale_h = 1.0 / np.sqrt(HIDDEN)
        scale_i = 1.0 / np.sqrt(INTER)
        return {'hidden_states': jax.random.normal(ks[0], (BATCH, SEQ, HIDDEN), jnp.float32), 'gate_w': jax.random.normal(ks[1], (NUM_EXPERTS, HIDDEN), jnp.float32) * scale_h, 'w_gate': jax.random.normal(ks[2], (NUM_EXPERTS, INTER, HIDDEN), jnp.float32) * scale_h, 'w_up': jax.random.normal(ks[3], (NUM_EXPERTS, INTER, HIDDEN), jnp.float32) * scale_h, 'w_down': jax.random.normal(ks[4], (NUM_EXPERTS, HIDDEN, INTER), jnp.float32) * scale_i}
    _L0_ffn_in = _L0_ffn_setup()
    _L0_c = _w((lambda *s: np.random.randn(*s).astype(np.float32) * 0.05)(4, 256))
    _L0_wmod = _w((lambda *s: np.random.randn(*s).astype(np.float32) * 0.05)(256, 6 * 256) * 256 ** (-0.5))

    def _L1_attn_setup():
        import jax, jax.numpy as jnp
        import numpy as np
        B_, S_, E_ = (2, 256, 256)
        H_, P_, N_, G_, K_, CH_ = (64, 64, 128, 1, 4, 32)
        INTER = H_ * P_
        CONV_DIM = INTER + 2 * G_ * N_
        PROJ = INTER + CONV_DIM + H_
        EPS = 1e-05

        def segsum(x):
            T = x.shape[-1]
            xe = jnp.broadcast_to(x[..., None], x.shape + (T,))
            m_excl = jnp.tril(jnp.ones((T, T), bool), -1)
            s = jnp.cumsum(jnp.where(m_excl, xe, 0.0), axis=-2)
            m_incl = jnp.tril(jnp.ones((T, T), bool), 0)
            return jnp.where(m_incl, s, -jnp.inf)

        def ssm_forward(input_states, in_proj_w, conv_w, conv_b, A_log, dt_bias, D, norm_w, out_proj_w):
            b, s, _ = input_states.shape
            proj = input_states @ in_proj_w.T
            gate, hBC, dt = jnp.split(proj, [INTER, INTER + CONV_DIM], axis=-1)
            x = hBC.transpose(0, 2, 1)
            x = jax.lax.conv_general_dilated(x, conv_w, (1,), [(K_ - 1, 0)], dimension_numbers=('NCH', 'OIH', 'NCH'), feature_group_count=CONV_DIM)
            hBC = jax.nn.silu((x + conv_b[None, :, None]).transpose(0, 2, 1))
            hs, Bmat, Cmat = jnp.split(hBC, [INTER, INTER + G_ * N_], axis=-1)
            A = -jnp.exp(A_log)
            dt = jax.nn.softplus(dt + dt_bias)
            xh = hs.reshape(b, s, H_, P_)
            Bf = jnp.repeat(Bmat.reshape(b, s, G_, N_), H_ // G_, axis=2)
            Cf = jnp.repeat(Cmat.reshape(b, s, G_, N_), H_ // G_, axis=2)
            D_res = D[:, None] * xh
            xh = xh * dt[..., None]
            Adt = A[None, None, :] * dt
            nch = s // CH_
            xc = xh.reshape(b, nch, CH_, H_, P_)
            Bc = Bf.reshape(b, nch, CH_, H_, N_)
            Cc = Cf.reshape(b, nch, CH_, H_, N_)
            Ac = Adt.reshape(b, nch, CH_, H_).transpose(0, 3, 1, 2)
            A_cum = jnp.cumsum(Ac, axis=-1)
            L = jnp.exp(segsum(Ac))
            Gm = jnp.einsum('bclhn,bcshn->bclsh', Cc, Bc)
            M = Gm * L.transpose(0, 2, 3, 4, 1)
            Y_diag = jnp.einsum('bclsh,bcshp->bclhp', M, xc)
            decay_states = jnp.exp(A_cum[..., -1:] - A_cum)
            states = jnp.einsum('bclhn,bhcl,bclhp->bchpn', Bc, decay_states, xc)
            states = jnp.concatenate([jnp.zeros_like(states[:, :1]), states], axis=1)
            A_last = jnp.pad(A_cum[..., -1], ((0, 0), (0, 0), (1, 0)))
            decay_chunk = jnp.exp(segsum(A_last))
            new_states = jnp.einsum('bhij,bjhpn->bihpn', decay_chunk, states)
            states = new_states[:, :-1]
            state_decay = jnp.exp(A_cum)
            Y_off = jnp.einsum('bclhn,bchpn,bhcl->bclhp', Cc, states, state_decay)
            y = (Y_diag + Y_off).reshape(b, s, H_, P_) + D_res
            y = y.reshape(b, s, INTER)
            yg = y * jax.nn.silu(gate)
            var = jnp.mean(yg * yg, axis=-1, keepdims=True)
            yn = norm_w * (yg * jax.lax.rsqrt(var + EPS))
            return yn @ out_proj_w.T
        key = jax.random.key(seed)
        ks = jax.random.split(key, 4)
        return {'input_states': jax.random.normal(ks[0], (B_, S_, E_), jnp.float32), 'mask': jnp.ones((B_, 1, S_), jnp.int32), 'in_proj_w': jax.random.normal(ks[1], (PROJ, E_), jnp.float32) * 0.02, 'conv_w': jax.random.normal(ks[2], (CONV_DIM, 1, K_), jnp.float32) * 0.2, 'conv_b': jnp.zeros((CONV_DIM,), jnp.float32), 'A_log': jnp.log(jnp.arange(1, H_ + 1, dtype=jnp.float32)), 'dt_bias': jnp.ones((H_,), jnp.float32), 'D': jnp.ones((H_,), jnp.float32), 'norm_w': jnp.ones((INTER,), jnp.float32), 'out_proj_w': jax.random.normal(ks[3], (E_, INTER), jnp.float32) * 0.02}
    _L1_attn_in = _L1_attn_setup()

    def _L1_ffn_setup():
        import jax, jax.numpy as jnp
        import numpy as np
        HID = 256
        N_EXP = 32
        F_EXP = 96
        TOP_K = 6
        F_SH = 192
        B, S = (1, 128)
        key = jax.random.key(seed)
        ks = jax.random.split(key, 8)
        s = 0.02
        return {'hidden_states': jax.random.normal(ks[0], (B, S, HID), dtype=jnp.float32), 'gate_w': jax.random.normal(ks[1], (HID, N_EXP), dtype=jnp.float32) * s, 'wg': jax.random.normal(ks[2], (N_EXP, HID, F_EXP), dtype=jnp.float32) * s, 'wu': jax.random.normal(ks[3], (N_EXP, HID, F_EXP), dtype=jnp.float32) * s, 'wd': jax.random.normal(ks[4], (N_EXP, F_EXP, HID), dtype=jnp.float32) * s, 'sg': jax.random.normal(ks[5], (HID, F_SH), dtype=jnp.float32) * s, 'su': jax.random.normal(ks[6], (HID, F_SH), dtype=jnp.float32) * s, 'sd': jax.random.normal(ks[7], (F_SH, HID), dtype=jnp.float32) * s}
    _L1_ffn_in = _L1_ffn_setup()
    _L1_c = _w((lambda *s: np.random.randn(*s).astype(np.float32) * 0.05)(4, 256))
    _L1_wmod = _w((lambda *s: np.random.randn(*s).astype(np.float32) * 0.05)(256, 6 * 256) * 256 ** (-0.5))
    _d = {'L0_attn_x': _L0_attn_in['x'], 'L0_attn_lora_start_indices': _L0_attn_in['lora_start_indices'], 'L0_attn_Wq': _L0_attn_in['Wq'], 'L0_attn_Aq': _L0_attn_in['Aq'], 'L0_attn_Bq': _L0_attn_in['Bq'], 'L0_attn_Wk': _L0_attn_in['Wk'], 'L0_attn_Ak': _L0_attn_in['Ak'], 'L0_attn_Bk': _L0_attn_in['Bk'], 'L0_attn_Wv': _L0_attn_in['Wv'], 'L0_attn_Av': _L0_attn_in['Av'], 'L0_attn_Bv': _L0_attn_in['Bv'], 'L0_attn_Wo': _L0_attn_in['Wo'], 'L0_attn_Ao': _L0_attn_in['Ao'], 'L0_attn_Bo': _L0_attn_in['Bo'], 'L0_ffn_gate_w': _L0_ffn_in['gate_w'], 'L0_ffn_w_gate': _L0_ffn_in['w_gate'], 'L0_ffn_w_up': _L0_ffn_in['w_up'], 'L0_ffn_w_down': _L0_ffn_in['w_down'], 'L0_c': _L0_c, 'L0_wmod': _L0_wmod, 'L1_attn_mask': _L1_attn_in['mask'], 'L1_attn_in_proj_w': _L1_attn_in['in_proj_w'], 'L1_attn_conv_w': _L1_attn_in['conv_w'], 'L1_attn_conv_b': _L1_attn_in['conv_b'], 'L1_attn_A_log': _L1_attn_in['A_log'], 'L1_attn_dt_bias': _L1_attn_in['dt_bias'], 'L1_attn_D': _L1_attn_in['D'], 'L1_attn_norm_w': _L1_attn_in['norm_w'], 'L1_attn_out_proj_w': _L1_attn_in['out_proj_w'], 'L1_ffn_gate_w': _L1_ffn_in['gate_w'], 'L1_ffn_wg': _L1_ffn_in['wg'], 'L1_ffn_wu': _L1_ffn_in['wu'], 'L1_ffn_wd': _L1_ffn_in['wd'], 'L1_ffn_sg': _L1_ffn_in['sg'], 'L1_ffn_su': _L1_ffn_in['su'], 'L1_ffn_sd': _L1_ffn_in['sd'], 'L1_c': _L1_c, 'L1_wmod': _L1_wmod}
    _x0 = _d['L0_attn_x']
    _d['L0_attn_x'] = jax.random.normal(jax.random.fold_in(jax.random.key(seed), 1), (4, 512, 256), dtype=_x0.dtype)
    del _x0
    return _d

def reference(L0_attn_x, L0_attn_lora_start_indices, L0_attn_Wq, L0_attn_Aq, L0_attn_Bq, L0_attn_Wk, L0_attn_Ak, L0_attn_Bk, L0_attn_Wv, L0_attn_Av, L0_attn_Bv, L0_attn_Wo, L0_attn_Ao, L0_attn_Bo, L0_ffn_gate_w, L0_ffn_w_gate, L0_ffn_w_up, L0_ffn_w_down, L0_c, L0_wmod, L1_attn_mask, L1_attn_in_proj_w, L1_attn_conv_w, L1_attn_conv_b, L1_attn_A_log, L1_attn_dt_bias, L1_attn_D, L1_attn_norm_w, L1_attn_out_proj_w, L1_ffn_gate_w, L1_ffn_wg, L1_ffn_wu, L1_ffn_wd, L1_ffn_sg, L1_ffn_su, L1_ffn_sd, L1_c, L1_wmod):

    def _L0_attn_ref(x, lora_start_indices, Wq, Aq, Bq, Wk, Ak, Bk, Wv, Av, Bv, Wo, Ao, Bo):
        import jax, jax.numpy as jnp
        import numpy as np
        D_MODEL = 256
        NUM_HEADS = 16
        D_KV = D_MODEL // NUM_HEADS
        THETA = 10000.0
        N_LORA = 4
        RANK = 16
        BATCH = 2
        SEQ = 256

        def _adapter_ids(starts, batch):
            ids = jnp.searchsorted(starts, jnp.arange(batch), side='right') - 1
            return jnp.clip(ids, 0, starts.shape[0] - 1)

        def _multilora(x, ids, W, A, B):
            base = jnp.einsum('bsd,od->bso', x, W)
            Ai, Bi = (A[ids], B[ids])
            low = jnp.einsum('bsd,brd->bsr', x, Ai)
            return base + jnp.einsum('bsr,bor->bso', low, Bi)

        def _rope(x):
            d = x.shape[-1]
            pos = jnp.arange(x.shape[-2], dtype=jnp.float32)
            inv_freq = THETA ** (-jnp.arange(0, d, 2, dtype=jnp.float32) / d)
            ang = pos[:, None] * inv_freq[None, :]
            cos, sin = (jnp.cos(ang), jnp.sin(ang))
            x1, x2 = (x[..., 0::2], x[..., 1::2])
            o1 = x1 * cos - x2 * sin
            o2 = x1 * sin + x2 * cos
            return jnp.stack([o1, o2], axis=-1).reshape(x.shape)
        b, s, _ = x.shape
        ids = _adapter_ids(lora_start_indices, b)
        Q = _multilora(x, ids, Wq, Aq, Bq)
        K = _multilora(x, ids, Wk, Ak, Bk)
        V = _multilora(x, ids, Wv, Av, Bv)
        split = lambda t: t.reshape(b, s, NUM_HEADS, D_KV).transpose(0, 2, 1, 3)
        Q, K, V = (split(Q), split(K), split(V))
        Q, K = (_rope(Q), _rope(K))
        scores = jnp.einsum('bhqd,bhkd->bhqk', Q, K) / jnp.sqrt(jnp.asarray(D_KV, x.dtype))
        causal = jnp.tril(jnp.ones((s, s), bool))
        scores = jnp.where(causal, scores, jnp.asarray(-jnp.inf, scores.dtype))
        attn = jax.nn.softmax(scores, axis=-1)
        out = jnp.einsum('bhqk,bhkd->bhqd', attn, V)
        out = out.transpose(0, 2, 1, 3).reshape(b, s, D_MODEL)
        return _multilora(out, ids, Wo, Ao, Bo)

    def _L0_ffn_ref(hidden_states, gate_w, w_gate, w_up, w_down):
        import jax, jax.numpy as jnp
        import numpy as np
        HIDDEN = 256
        INTER = 176
        NUM_EXPERTS = 16
        TOP_K = 2
        BATCH, SEQ = (2, 256)
        B, S, H = hidden_states.shape
        E = gate_w.shape[0]
        x = hidden_states.reshape(-1, H)
        T = x.shape[0]
        logits = jnp.dot(x.astype(jnp.float32), gate_w.astype(jnp.float32).T)
        probs = jax.nn.softmax(logits, axis=-1)
        topk_w, topk_idx = jax.lax.top_k(probs, TOP_K)
        topk_w = topk_w / (jnp.sum(topk_w, axis=-1, keepdims=True) + 1e-20)
        combine = jnp.zeros((T, E), dtype=x.dtype).at[jnp.arange(T)[:, None], topk_idx].add(topk_w.astype(x.dtype))
        g = jnp.einsum('th,eih->tei', x, w_gate)
        u = jnp.einsum('th,eih->tei', x, w_up)
        h = jax.nn.silu(g) * u
        expert_out = jnp.einsum('tei,ehi->teh', h, w_down)
        y = jnp.einsum('te,teh->th', combine, expert_out)
        return y.reshape(B, S, H)

    def _L1_attn_ref(input_states, mask, in_proj_w, conv_w, conv_b, A_log, dt_bias, D, norm_w, out_proj_w):
        import jax, jax.numpy as jnp
        import numpy as np
        B_, S_, E_ = (2, 256, 256)
        H_, P_, N_, G_, K_, CH_ = (64, 64, 128, 1, 4, 32)
        INTER = H_ * P_
        CONV_DIM = INTER + 2 * G_ * N_
        PROJ = INTER + CONV_DIM + H_
        EPS = 1e-05

        def segsum(x):
            T = x.shape[-1]
            xe = jnp.broadcast_to(x[..., None], x.shape + (T,))
            m_excl = jnp.tril(jnp.ones((T, T), bool), -1)
            s = jnp.cumsum(jnp.where(m_excl, xe, 0.0), axis=-2)
            m_incl = jnp.tril(jnp.ones((T, T), bool), 0)
            return jnp.where(m_incl, s, -jnp.inf)

        def ssm_forward(input_states, in_proj_w, conv_w, conv_b, A_log, dt_bias, D, norm_w, out_proj_w):
            b, s, _ = input_states.shape
            proj = input_states @ in_proj_w.T
            gate, hBC, dt = jnp.split(proj, [INTER, INTER + CONV_DIM], axis=-1)
            x = hBC.transpose(0, 2, 1)
            x = jax.lax.conv_general_dilated(x, conv_w, (1,), [(K_ - 1, 0)], dimension_numbers=('NCH', 'OIH', 'NCH'), feature_group_count=CONV_DIM)
            hBC = jax.nn.silu((x + conv_b[None, :, None]).transpose(0, 2, 1))
            hs, Bmat, Cmat = jnp.split(hBC, [INTER, INTER + G_ * N_], axis=-1)
            A = -jnp.exp(A_log)
            dt = jax.nn.softplus(dt + dt_bias)
            xh = hs.reshape(b, s, H_, P_)
            Bf = jnp.repeat(Bmat.reshape(b, s, G_, N_), H_ // G_, axis=2)
            Cf = jnp.repeat(Cmat.reshape(b, s, G_, N_), H_ // G_, axis=2)
            D_res = D[:, None] * xh
            xh = xh * dt[..., None]
            Adt = A[None, None, :] * dt
            nch = s // CH_
            xc = xh.reshape(b, nch, CH_, H_, P_)
            Bc = Bf.reshape(b, nch, CH_, H_, N_)
            Cc = Cf.reshape(b, nch, CH_, H_, N_)
            Ac = Adt.reshape(b, nch, CH_, H_).transpose(0, 3, 1, 2)
            A_cum = jnp.cumsum(Ac, axis=-1)
            L = jnp.exp(segsum(Ac))
            Gm = jnp.einsum('bclhn,bcshn->bclsh', Cc, Bc)
            M = Gm * L.transpose(0, 2, 3, 4, 1)
            Y_diag = jnp.einsum('bclsh,bcshp->bclhp', M, xc)
            decay_states = jnp.exp(A_cum[..., -1:] - A_cum)
            states = jnp.einsum('bclhn,bhcl,bclhp->bchpn', Bc, decay_states, xc)
            states = jnp.concatenate([jnp.zeros_like(states[:, :1]), states], axis=1)
            A_last = jnp.pad(A_cum[..., -1], ((0, 0), (0, 0), (1, 0)))
            decay_chunk = jnp.exp(segsum(A_last))
            new_states = jnp.einsum('bhij,bjhpn->bihpn', decay_chunk, states)
            states = new_states[:, :-1]
            state_decay = jnp.exp(A_cum)
            Y_off = jnp.einsum('bclhn,bchpn,bhcl->bclhp', Cc, states, state_decay)
            y = (Y_diag + Y_off).reshape(b, s, H_, P_) + D_res
            y = y.reshape(b, s, INTER)
            yg = y * jax.nn.silu(gate)
            var = jnp.mean(yg * yg, axis=-1, keepdims=True)
            yn = norm_w * (yg * jax.lax.rsqrt(var + EPS))
            return yn @ out_proj_w.T
        return ssm_forward(input_states, in_proj_w, conv_w, conv_b, A_log, dt_bias, D, norm_w, out_proj_w)

    def _L1_ffn_ref(hidden_states, gate_w, wg, wu, wd, sg, su, sd):
        import jax, jax.numpy as jnp
        import numpy as np
        HID = 256
        N_EXP = 32
        F_EXP = 96
        TOP_K = 6
        F_SH = 192
        B, S = (1, 128)
        orig_shape = hidden_states.shape
        x = hidden_states.reshape(-1, HID)
        scores = jax.nn.sigmoid(x @ gate_w)
        topk_w, topk_i = jax.lax.top_k(scores, TOP_K)
        topk_w = topk_w / (jnp.sum(topk_w, axis=-1, keepdims=True) + 1e-20)
        combine = jnp.sum(jax.nn.one_hot(topk_i, N_EXP, dtype=topk_w.dtype) * topk_w[..., None], axis=1)
        g = jnp.einsum('td,edf->tef', x, wg)
        u = jnp.einsum('td,edf->tef', x, wu)
        act = jax.nn.silu(g) * u
        routed = jnp.einsum('tef,efd,te->td', act, wd, combine)
        routed = routed.reshape(orig_shape)
        shared = jax.nn.silu(hidden_states @ sg) * (hidden_states @ su) @ sd
        return routed + shared
    x = L0_attn_x
    mod = (_silu(L0_c) @ L0_wmod).reshape(L0_c.shape[0], 6, 1, -1)
    sa, ca, ga, sb, cb, gb = (mod[:, 0], mod[:, 1], mod[:, 2], mod[:, 3], mod[:, 4], mod[:, 5])
    ga = (2 * (ga >= 0) - 1) * jnp.maximum(jnp.abs(ga), 0.25)
    gb = (2 * (gb >= 0) - 1) * jnp.maximum(jnp.abs(gb), 0.25)
    h = _layernorm(x, axis=-1) * (1 + ca) + sa
    x = x + ga * _L0_attn_ref(h, L0_attn_lora_start_indices, L0_attn_Wq, L0_attn_Aq, L0_attn_Bq, L0_attn_Wk, L0_attn_Ak, L0_attn_Bk, L0_attn_Wv, L0_attn_Av, L0_attn_Bv, L0_attn_Wo, L0_attn_Ao, L0_attn_Bo)
    h = _layernorm(x, axis=-1) * (1 + cb) + sb
    x = x + gb * _L0_ffn_ref(h, L0_ffn_gate_w, L0_ffn_w_gate, L0_ffn_w_up, L0_ffn_w_down)
    mod = (_silu(L1_c) @ L1_wmod).reshape(L1_c.shape[0], 6, 1, -1)
    sa, ca, ga, sb, cb, gb = (mod[:, 0], mod[:, 1], mod[:, 2], mod[:, 3], mod[:, 4], mod[:, 5])
    ga = (2 * (ga >= 0) - 1) * jnp.maximum(jnp.abs(ga), 0.25)
    gb = (2 * (gb >= 0) - 1) * jnp.maximum(jnp.abs(gb), 0.25)
    h = _layernorm(x, axis=-1) * (1 + ca) + sa
    x = x + ga * _L1_attn_ref(h, L1_attn_mask, L1_attn_in_proj_w, L1_attn_conv_w, L1_attn_conv_b, L1_attn_A_log, L1_attn_dt_bias, L1_attn_D, L1_attn_norm_w, L1_attn_out_proj_w)
    h = _layernorm(x, axis=-1) * (1 + cb) + sb
    x = x + gb * _L1_ffn_ref(h, L1_ffn_gate_w, L1_ffn_wg, L1_ffn_wu, L1_ffn_wd, L1_ffn_sg, L1_ffn_su, L1_ffn_sd)
    return x

_drawn_inputs = setup_inputs


def setup_inputs(seed=0):
    import zlib

    import numpy as np

    out = dict(_drawn_inputs(seed))
    spreads = {'L1_attn_conv_b': (0.0, 0.1),
     'L1_attn_dt_bias': (1.0, 0.6),
     'L1_attn_D': (1.0, 0.2),
     'L1_attn_norm_w': (1.0, 0.2)}
    factors = {'L0_attn_Wq': 8.0,
     'L0_attn_Aq': 8.0,
     'L0_attn_Bq': 8.0,
     'L0_attn_Wk': 8.0,
     'L0_attn_Ak': 8.0,
     'L0_attn_Bk': 8.0,
     'L0_attn_Wv': 8.0,
     'L0_attn_Av': 8.0,
     'L0_attn_Bv': 8.0,
     'L0_attn_Wo': 8.0,
     'L0_attn_Ao': 8.0,
     'L0_attn_Bo': 8.0,
     'L1_attn_A_log': 8.0,
     'L1_ffn_gate_w': 8.0,
     'L1_ffn_wg': 8.0,
     'L1_ffn_wu': 8.0,
     'L1_ffn_wd': 8.0,
     'L1_ffn_sg': 8.0,
     'L1_ffn_su': 8.0,
     'L1_ffn_sd': 8.0}
    for name, (base, spread) in spreads.items():
        noise = np.random.default_rng([zlib.crc32(name.encode()), seed]).standard_normal(out[name].shape)
        drawn = base * np.exp(spread * noise) if base else spread * noise
        out[name] = jnp.asarray(drawn.astype(out[name].dtype))
    for name, factor in factors.items():
        out[name] = (out[name] * factor).astype(out[name].dtype)
    return out
```

```python
from contextlib import ExitStack

import numpy as np
import concourse.bass as bass
from concourse import mybir

FP32 = mybir.dt.float32
F32R = mybir.dt.float32r
BF16 = mybir.dt.bfloat16
I32 = mybir.dt.int32
U32 = mybir.dt.uint32
ALU = mybir.AluOpType
ACT = mybir.ActivationFunctionType
AX = mybir.AxisListType

P = 128
D = 256
KD = D // P
GROUPS = 4
SEQ = 512
TT = SEQ // P
HEADS, DK = 16, 16
SLOT = 64
RANK, LORAS = 16, 4
EPS = 1e-5
NEG = -3.0e38
SSM_HEADS, SSM_P, SSM_N = 64, 64, 128
INNER = SSM_HEADS * SSM_P
FT = INNER // P
TAPS = 4
E0, TOP0, I0 = 16, 2, 176
E1, TOP1, I1, SHARED = 32, 6, 96, 192
ROWS0 = E0 * I0
ROWS1 = E1 * I1 + SHARED
J0 = ROWS0 // P
J1 = -(-ROWS1 // (2 * P)) * 2
PART = 32


class Tally:

    def __init__(self, sem, base=0):
        self.sem, self.n, self.turn, self.each = sem, base, None, 0

    def add(self, ins):
        self.n += 1
        ins.then_inc(self.sem, 1)

    def now(self):
        return self.n if self.turn is None else self.turn * self.each + self.n

    def enter(self, turn, each):
        self.turn, self.each, self.first = turn, each, self.n

    def leave(self, turns):
        assert self.n - self.first == self.each, (self.n - self.first, self.each)
        self.turn, self.n = None, self.first + turns * self.each


ORDER = ("attn", "moe0", "ssm", "moe1")


def build(nc, io, order=ORDER):
    ctx = ExitStack()
    with ctx:
        program(nc, io, ctx, order)


def program(nc, io, ctx, order):
    def sb(name, shape, dt=FP32, where=ctx):
        return where.enter_context(nc.sbuf_tensor(name, shape, dt))

    sems = {}

    def sem(name):
        if name not in sems:
            sems[name] = ctx.enter_context(nc.semaphore(name))
        return sems[name]

    bank = [ctx.enter_context(nc.psum_tensor(f"bank{i}", [P, 512], FP32)) for i in range(8)]

    x = sb("x", [P, GROUPS * TT, D])
    ht_hi = sb("ht_hi", [P, KD, GROUPS * SEQ], F32R)
    ht_lo = sb("ht_lo", [P, KD, GROUPS * SEQ], F32R)
    hb_hi = sb("hb_hi", [P, KD, SEQ], F32R)
    hb_lo = sb("hb_lo", [P, KD, SEQ], F32R)
    mod_t = sb("mod_t", [P, 2, 6, KD, GROUPS])
    gates = sb("gates", [P, 4, GROUPS, D])
    comb_t = sb("comb_t", [P, GROUPS * SEQ], BF16)
    ident = sb("ident", [P, P])
    ident_b = sb("ident_b", [P, P], BF16)
    zero_b = sb("zero_b", [P, P], BF16)
    zero_r = sb("zero_r", [P, 512], BF16)
    ones_c = sb("ones_c", [P, 1])
    iota_e = sb("iota_e", [P, TT, E1])
    stats = sb("stats", [P, TT, 6])
    mv = sb("mv", [P, TT, 2])
    rs = sb("rs", [P, 5, TT])
    xn = sb("xn", [P, TT, D])
    h32 = sb("h32", [P, KD, SEQ])
    outs = sb("outs", [P, 4, SEQ])
    tail_tmp = outs[:, KD:4, :].rearrange("p a (c d) -> p (a c) d", d=D)
    rnorm = sb("rnorm", [P, TT])
    gw = sb("gw", [P, KD, 2 * P])
    gw_hi = sb("gw_hi", [P, KD, 2 * P], F32R)
    gw_lo = sb("gw_lo", [P, KD, 2 * P], F32R)
    lg_t = sb("lg_t", [E1, SEQ])
    lg = sb("lg", [P, TT, E1])
    pr = sb("pr", [P, TT, E1])
    msk = sb("msk", [P, TT, E1])
    eq = sb("eq", [P, TT, E1])
    top = sb("top", [P, TT, 8])
    top_i = sb("top_i", [P, TT, 8], U32)
    top_f = sb("top_f", [P, TT, 8])
    wsum = sb("wsum", [P, 2, TT])
    part_b = sb("part_b", [P, 2, TT, E1], BF16)
    comb = sb("comb", [P, TT, P])

    met, s_dve, s_act, s_pool = sem("met"), sem("dve_chain"), sem("act_chain"), sem("pool_chain")
    s_in, s_out = sem("inputs_in"), sem("x_out")

    class Engine:

        def __init__(self, e, name, chain):
            self.e, self.name, self.meet = e, name, Tally(met)
            self.own = Tally(chain) if chain is not None else None
            self.calls = {stage: Tally(None) for stage in ("norm", "route")}
            self.passes, self.waited = sem("waits_passed_" + name), False

        def together(self):
            if self.waited:
                self.passed()
            self.e.drain().then_inc(met, 1)
            self.meet.n += 4
            self.e.wait_ge(met, self.meet.now())
            self.passed()

        def passed(self):
            self.e.sem_inc(self.passes, 1)
            self.waited = False

        def step(self, ins):
            self.own.add(ins)
            self.e.wait_ge(self.own.sem, self.own.now())
            self.waited = True

        def call(self, stage):
            self.calls[stage].n += 1
            return self.calls[stage].now()

        def enter(self, turn, meets, steps, calls):
            self.meet.enter(turn, 4 * meets)
            for stage, tally in self.calls.items():
                tally.enter(turn, calls[stage])
            if self.own is not None:
                self.own.enter(turn, steps)

        def leave(self, turns):
            self.meet.leave(turns)
            for tally in self.calls.values():
                tally.leave(turns)
            if self.own is not None:
                self.own.leave(turns)

    block = ctx.enter_context(nc.Block())


    n_var, n_root, n_rows, n_turned, n_high, n_full = (
        sem("norm_" + n) for n in ("variance", "root", "rows", "turned", "high", "full"))

    def norm_dve(v, b, layer, half, meanwhile=None, last=None):
        c = v.call("norm")
        for i in range(TT):
            v.own.add(v.e.bn_stats(stats[:, i, :], x[:, bass.ds(b * TT + i, 1), :]))
        v.e.wait_ge(s_dve, v.own.now())
        v.passed()
        for i in range(TT):
            v.own.add(v.e.bn_aggr(mv[:, i, :], stats[:, i, :]))
        v.e.wait_ge(s_dve, v.own.now())
        v.e.tensor_scalar(rs[:, 0, :], mv[:, :, 1], EPS, None, ALU.add).then_inc(n_var, 1)
        v.e.wait_ge(n_root, c)
        rsqrt_dve(v)
        for i in range(TT):
            v.e.tensor_scalar(xn[:, i, :], x[:, bass.ds(b * TT + i, 1), :], mv[:, i, 0:1],
                              rs[:, 2, i:i + 1], ALU.subtract, ALU.mult).then_inc(n_rows, 1)
        if meanwhile:
            meanwhile()
        v.e.wait_ge(n_turned, c)
        for k in (1, 0):
            if k == 0:
                v.e.wait_ge(n_high, c * KD - 1)
            scale, shift = modulation(b, layer, half, k)
            v.e.tensor_scalar(h32[:, k, :], bank[k][:, :], scale, shift, ALU.mult, ALU.add).then_inc(n_full, 1)
        v.e.wait_ge(n_full, c * KD)
        hi, lo, off = (hb_hi, hb_lo, 0) if half == 0 else (ht_hi, ht_lo, b * SEQ)
        for k in range(KD):
            v.e.wait_ge(n_high, c * KD + (k + 1 - KD))
            v.own.add(v.e.tensor_tensor(lo[:, k, bass.ds(off, SEQ)], h32[:, k, :],
                                        hi[:, k, bass.ds(off, SEQ)].bitcast(FP32), ALU.subtract))
        if last:
            last()
        v.together()

    def modulation(b, layer, half, k):
        return (mod_t[:, layer, 3 * half + 1, k, bass.ds(b, 1)], mod_t[:, layer, 3 * half + 0, k, bass.ds(b, 1)])

    def rsqrt_dve(v):
        v.step(v.e.reciprocal(rs[:, 2, :], rs[:, 1, :]))
        v.step(v.e.tensor_tensor(rs[:, 3, :], rs[:, 0, :], rs[:, 2, :], ALU.mult))
        v.step(v.e.tensor_tensor(rs[:, 3, :], rs[:, 3, :], rs[:, 2, :], ALU.mult))
        v.step(v.e.tensor_scalar(rs[:, 3, :], rs[:, 3, :], -0.5, 1.5, ALU.mult, ALU.add))
        v.step(v.e.tensor_tensor(rs[:, 2, :], rs[:, 2, :], rs[:, 3, :], ALU.mult))

    def norm_act(a, b, layer, half, last=None):
        c = a.call("norm")
        a.e.wait_ge(n_var, c)
        a.e.activation(rs[:, 1, :], rs[:, 0, :], ACT.Sqrt).then_inc(n_root, 1)
        a.e.wait_ge(n_turned, c)
        hi, off = (hb_hi, 0) if half == 0 else (ht_hi, b * SEQ)
        for k in range(KD):
            scale, shift = modulation(b, layer, half, k)
            if k == 1:
                a.e.wait_ge(n_full, c * KD - 1)
            a.e.activation(hi[:, k, bass.ds(off, SEQ)], bank[k][:, :], ACT.Identity, bias=shift,
                           scale=scale).then_inc(n_high, 1)
        if last:
            last()
        a.together()

    def norm_pe(t):
        c = t.call("norm")
        for i in range(TT):
            t.e.wait_ge(n_rows, c * TT + (i + 1 - TT))
            for k in range(KD):
                mm = t.e.transpose(bank[k][:, i * P:(i + 1) * P], xn[:, i, k * P:(k + 1) * P], ident[:, :])
        mm.then_inc(n_turned, 1)
        t.together()

    def norm_pool(g):
        g.call("norm")
        g.together()

    NORM_MEETS, NORM_STEPS = 1, TT * 2 + 5 + KD

    r_turn = sem("route_handed_on")
    LOGITS, LOGITS_OUT, LOGITS_TURNED, SCORES_IN, SCORES, COMBINE, COMBINE_TURNED = range(1, 8)

    def handed(c, what):
        return c * COMBINE_TURNED + (what - COMBINE_TURNED)

    def route_pe(t, b, layer):
        c = t.call("route")
        w = slice(layer * P, layer * P + P)
        n = 0
        for k in range(KD):
            rh, rl = ht_hi[:, k, bass.ds(b * SEQ, SEQ)], ht_lo[:, k, bass.ds(b * SEQ, SEQ)]
            for lw, r in ((gw_hi, rh), (gw_hi, rl), (gw_lo, rh)):
                mm = t.e.matmul(bank[0][:, :], lw[:, k, w], r, start=(n == 0), stop=(n == 3 * KD - 1))
                n += 1
        mm.then_inc(r_turn, 1)
        t.e.wait_ge(r_turn, handed(c, LOGITS_OUT))
        t.passed()
        for i in range(TT):
            mm = t.e.transpose(bank[1][:, i * E1:(i + 1) * E1], lg_t[:, i * P:(i + 1) * P], ident[0:E1, 0:E1])
        mm.then_inc(r_turn, 1)
        t.e.wait_ge(r_turn, handed(c, COMBINE))
        for i in range(TT):
            mm = t.e.transpose(bank[2][:, i * P:(i + 1) * P], comb[:, i, :], ident[:, :])
        mm.then_inc(r_turn, 1)
        t.together()

    def route_act(a, b, layer):
        c = a.call("route")
        a.e.wait_ge(r_turn, handed(c, LOGITS))
        a.e.activation(lg_t[:, :], bank[0][0:E1, :], ACT.Copy).then_inc(r_turn, 1)
        a.e.wait_ge(r_turn, handed(c, SCORES_IN))
        if layer == 0:
            for i in range(TT):
                last = a.e.activation(pr[:, i, 0:E0], lg[:, i, 0:E0], ACT.Exp, bias=wsum[:, 0, i:i + 1])
        else:
            last = a.e.activation(pr[:, :, :], lg[:, :, :], ACT.Exp, scale=-1.0)
        last.then_inc(r_turn, 1)
        a.e.wait_ge(r_turn, handed(c, COMBINE_TURNED))
        a.e.activation(comb_t[:, bass.ds(b * SEQ, SEQ)], bank[2][:, :], ACT.Copy)
        a.together()

    def route_pool(g):
        g.call("route")
        g.together()

    def route_dve(v, b, layer):
        ne, k_top = (E0, TOP0) if layer == 0 else (E1, TOP1)
        e = v.e
        c = v.call("route")
        e.wait_ge(r_turn, handed(c, LOGITS_TURNED))
        v.step(e.tensor_copy(lg[:, :, :], bank[1][:, 0:TT * E1].rearrange("p (i e) -> p i e", i=TT)))
        if layer == 0:
            v.step(e.tensor_reduce(wsum[:, 0, :], lg[:, :, 0:ne], AX.X, ALU.max, negate=True))
        v.passed()
        e.sem_inc(r_turn, 1)
        e.wait_ge(r_turn, handed(c, SCORES))
        if layer == 0:
            v.step(e.tensor_reduce(wsum[:, 1, :], pr[:, :, 0:ne], AX.X, ALU.add))
            v.step(e.reciprocal(wsum[:, 1, :], wsum[:, 1, :]))
            v.step(e.tensor_tensor(pr[:, :, 0:ne], pr[:, :, 0:ne],
                                   wsum[:, 1, :].unsqueeze(2).broadcast_to([P, TT, ne]), ALU.mult))
        else:
            v.step(e.tensor_scalar(pr[:, :, :], pr[:, :, :], 1.0, None, ALU.add))
            v.step(e.reciprocal(pr[:, :, :], pr[:, :, :]))
        e.wait_ge(s_dve, v.own.now())
        v.passed()
        for i in range(TT):
            v.own.add(e.max(top[:, i, :], pr[:, i, 0:ne]))
        e.wait_ge(s_dve, v.own.now())
        v.passed()
        for i in range(TT):
            v.own.add(e.max_index(top_i[:, i, :], top[:, i, :], pr[:, i, 0:ne]))
        e.wait_ge(s_dve, v.own.now())
        v.step(e.tensor_copy(top_f[:, :, :], top_i[:, :, :]))
        v.step(e.tensor_reduce(wsum[:, 1, :], top[:, :, 0:k_top], AX.X, ALU.add))
        v.step(e.tensor_scalar(wsum[:, 1, :], wsum[:, 1, :], 1e-20, None, ALU.add))
        v.step(e.reciprocal(wsum[:, 1, :], wsum[:, 1, :]))
        v.step(e.tensor_scalar(wsum[:, 1, :], wsum[:, 1, :], 0.5, None, ALU.mult))
        for k in range(k_top):
            chosen = top_f[:, :, k:k + 1].broadcast_to([P, TT, ne])
            dst = msk if k == 0 else eq
            v.step(e.tensor_tensor(dst[:, :, 0:ne], iota_e[:, :, 0:ne], chosen, ALU.is_equal))
            if k:
                v.step(e.tensor_tensor(msk[:, :, 0:ne], msk[:, :, 0:ne], eq[:, :, 0:ne], ALU.add))
        v.step(e.tensor_tensor(msk[:, :, 0:ne], msk[:, :, 0:ne], pr[:, :, 0:ne], ALU.mult))
        v.step(e.tensor_tensor(msk[:, :, 0:ne], msk[:, :, 0:ne],
                               wsum[:, 1, :].unsqueeze(2).broadcast_to([P, TT, ne]), ALU.mult))
        v.step(e.tensor_copy(part_b[:, 0, :, 0:ne], msk[:, :, 0:ne]))
        v.step(e.tensor_copy(comb[:, :, 0:ne], part_b[:, 0, :, 0:ne]))
        v.step(e.tensor_tensor(msk[:, :, 0:ne], msk[:, :, 0:ne], comb[:, :, 0:ne], ALU.subtract))
        v.step(e.tensor_copy(part_b[:, 1, :, 0:ne], msk[:, :, 0:ne]))
        v.step(e.tensor_copy(comb[:, :, PART:PART + ne], part_b[:, 1, :, 0:ne]))
        e.tensor_tensor(comb[:, :, 2 * PART:2 * PART + ne], msk[:, :, 0:ne],
                        comb[:, :, PART:PART + ne], ALU.subtract).then_inc(r_turn, 1)
        v.together()

    ROUTE_MEETS = 1
    ROUTE_STEPS = (2 + 3 + 2 * TT + 5 + (2 * TOP0 - 1) + 2 + 5, 1 + 2 + 2 * TT + 5 + (2 * TOP1 - 1) + 2 + 5)

    def token_major(banks, i):
        return banks[i // 2][:, (i % 2) * D:(i % 2 + 1) * D]

    def tail_other(en):
        for _ in range(TAIL_MEETS):
            en.together()

    def tail_dve(v, b, acc, gate, scaled):
        v.together()
        for i in range(TT):
            got = token_major(acc, i)
            g = gates[:, gate, bass.ds(b, 1), :]
            if scaled:
                v.own.add(v.e.scalar_tensor_tensor(out=tail_tmp[:, i, :], in0=got, scalar=rnorm[:, i:i + 1],
                                                   in1=g, op0=ALU.mult, op1=ALU.mult))
            else:
                v.own.add(v.e.tensor_tensor(tail_tmp[:, i, :], got, g, ALU.mult))
        v.e.wait_ge(s_dve, v.own.now())
        for i in range(TT):
            xi = x[:, bass.ds(b * TT + i, 1), :]
            v.own.add(v.e.tensor_tensor(xi, xi, tail_tmp[:, i, :], ALU.add))
        v.together()

    TAIL_MEETS, TAIL_STEPS = 2, 2 * TT
    ONE_GROUP = {"norm": 2, "route": 1}

    setup = ExitStack()
    ct = sb("ct", [P, KD, 2, GROUPS], where=setup)
    cth = sb("cth", [P, KD, 2, GROUPS], where=setup)
    cs = sb("cs", [P, KD, 2, GROUPS], where=setup)
    csb = sb("csb", [P, KD, 2, GROUPS, P], where=setup)
    wmod = sb("wmod", [P, 2, KD, 6 * D], where=setup)
    ga = sb("ga", [P, 2, GROUPS, D], where=setup)
    gs = sb("gs", [P, GROUPS, D], where=setup)
    setup.close()

    s_wmod = [sem("wmod0_in"), sem("wmod1_in")]
    s_x_in, c_tanh, c_read = sem("x_in"), sem("condition_tanh"), sem("condition_ready")
    m_done, m_out, m_gate = sem("modulation_products"), sem("gates_out_of_psum"), sem("gates_done")
    FEATURES = [0, 1, 3, 4]
    FEATURE_BANK = [bank[0], bank[7]]
    GATE_BANKS = [(bank[1], bank[2]), (bank[3], bank[4]), (bank[5], bank[6]), (bank[1], bank[2])]
    MOD_UNITS = [("features", 0), ("gate", 0), ("gate", 1), ("features", 1), ("gate", 2), ("gate", 3)]

    def setup_sync(e):
        small = [(ct[:, :, :, :], io["ct"]), (gw[:, :, :], io["gw"]), (ident[:, :], io["ident"]),
                 (ident_b[:, :], io["ident_b"]), (iota_e[:, :, :], io["iota_e"])]
        assert SETUP_IN == 16 * len(small)
        for dst, src in small:
            e.dma_start(dst, src).then_inc(s_in, 16)
        for layer in range(2):
            e.dma_start(wmod[:, layer, :, :], io[f"wmod{layer}"]).then_inc(s_wmod[layer], 16)
        e.dma_start(x[:, :, :], io["x"].rearrange("b (i p) d -> p (b i) d", p=P)).then_inc(s_x_in, 16)

    SETUP_IN = 16 * 5
    SETUP_MEETS = 1

    def setup_dve(v):
        e = v.e
        v.own.add(e.memset(zero_b[:, :], 0.0))
        v.own.add(e.memset(zero_r[:, :], 0.0))
        v.own.add(e.memset(ones_c[:, :], 1.0))
        v.own.add(e.memset(comb[:, :, :], 0.0))
        e.wait_ge(s_dve, v.own.now())
        v.step(e.memset(comb[:, :, 3 * PART:3 * PART + 1], 0.5))
        e.wait_ge(s_in, SETUP_IN)
        e.wait_ge(c_tanh, 1)
        v.step(e.scalar_tensor_tensor(out=cs[:, :, :, :], in0=cth[:, :, :, :], scalar=1.0, in1=ct[:, :, :, :],
                                      op0=ALU.add, op1=ALU.mult))
        v.step(e.tensor_scalar(cs[:, :, :, :], cs[:, :, :, :], 0.5, None, ALU.mult))
        for k in range(KD):
            e.tensor_copy(csb[:, k, :, :, :],
                          cs[:, k, :, :].unsqueeze(3).broadcast_to([P, 2, GROUPS, P])).then_inc(c_read, 1)
        v.step(e.tensor_copy(gw_hi[:, :, :], gw[:, :, :]))
        v.step(e.tensor_tensor(gw_lo[:, :, :], gw[:, :, :], gw_hi[:, :, :].bitcast(FP32), ALU.subtract))
        for unit, (what, n) in enumerate(MOD_UNITS):
            if what == "features":
                e.wait_ge(m_done, unit + 1)
                got = FEATURE_BANK[n][:, 0:6 * KD * GROUPS].rearrange("p (c k b) -> p c k b", c=6, k=KD)
                for c in FEATURES:
                    v.own.add(e.tensor_scalar(mod_t[:, n, c, :, :], got[:, c, :, :],
                                              1.0 if c in (1, 4) else 0.0, None, ALU.add))
            else:
                g1 = ga[:, n % 2, :, :]
                e.wait_ge(m_out, n + 1)
                v.step(e.scalar_tensor_tensor(out=gs[:, :, :], in0=g1, scalar=-1.0, in1=g1,
                                              op0=ALU.mult, op1=ALU.max))
                v.own.add(e.tensor_scalar(gs[:, :, :], gs[:, :, :], 0.25, None, ALU.max))
                v.step(e.tensor_scalar(g1, g1, 0.0, 2.0, ALU.is_ge, ALU.mult))
                e.scalar_tensor_tensor(out=gates[:, n, :, :], in0=g1, scalar=-1.0, in1=gs[:, :, :],
                                       op0=ALU.add, op1=ALU.mult).then_inc(m_gate, 1)
                e.wait_ge(m_gate, n + 1)
        e.wait_ge(s_x_in, 16)
        v.together()

    def setup_act(a):
        e = a.e
        e.wait_ge(s_in, SETUP_IN)
        e.activation(cth[:, :, :, :], ct[:, :, :, :], ACT.Tanh, scale=0.5).then_inc(c_tanh, 1)
        for unit, (what, n) in enumerate(MOD_UNITS):
            if what == "gate":
                e.wait_ge(m_done, unit + 1)
                if n >= 2:
                    e.wait_ge(m_gate, n - 1)
                for b2, src in enumerate(GATE_BANKS[n]):
                    last = e.activation(ga[:, n % 2, 2 * b2:2 * b2 + 2, :],
                                        src[:, :].rearrange("p (b d) -> p b d", b=2), ACT.Copy)
                last.then_inc(m_out, 1)
        a.together()

    def setup_pool(g):
        g.together()

    def setup_pe(t):
        e = t.e
        e.wait_ge(s_in, SETUP_IN)
        e.wait_ge(c_read, KD)
        for what, n in MOD_UNITS:
            if what == "features":
                e.wait_ge(s_wmod[n], 16)
                for c in FEATURES:
                    for m in range(KD):
                        col = (c * KD + m) * GROUPS
                        for k in range(KD):
                            mm = e.matmul(FEATURE_BANK[n][:, col:col + GROUPS],
                                          wmod[:, n, k, c * D + m * P:c * D + (m + 1) * P],
                                          cs[:, k, n, :], start=(k == 0), stop=(k == KD - 1))
            else:
                layer, c = n // 2, (2, 5)[n % 2]
                if n == 3:
                    e.wait_ge(m_out, 1)
                for b in range(GROUPS):
                    dst = GATE_BANKS[n][b // 2][:, (b % 2) * D:(b % 2 + 1) * D]
                    for k in range(KD):
                        mm = e.matmul(dst, csb[:, k, layer, b, :], wmod[:, layer, k, c * D:(c + 1) * D],
                                      start=(k == 0), stop=(k == KD - 1))
            mm.then_inc(m_done, 1)
        t.together()

    atn = ExitStack()
    QKV = 3 * D
    wt = sb("wt", [P, KD, 4 * D], where=atn)
    la = sb("la", [LORAS * RANK, 4, D], where=atn)
    lb = sb("lb", [LORAS * RANK, 4, D], where=atn)
    lbm = h32[0:LORAS * RANK, :, :].rearrange("p a (c d) -> p (a c) d", d=D)
    starts_i = sb("starts_i", [LORAS * RANK, LORAS], I32, where=atn)
    starts = sb("starts", [LORAS * RANK, LORAS], where=atn)
    cnt = sb("cnt", [LORAS * RANK, GROUPS, LORAS], where=atn)
    pick = sb("pick", [LORAS * RANK, GROUPS], where=atn)
    own_id = sb("own_id", [LORAS * RANK, 1], where=atn)
    bnum = sb("bnum", [LORAS * RANK, GROUPS, LORAS], where=atn)
    work = sb("work", [P, 2 * 1280], where=atn)
    we = work[:, 0:KD * 4 * D].rearrange("p (k n) -> p k n", k=KD)
    we_hi = sb("we_hi", [P, KD, 4 * D], F32R, where=atn)
    we_lo = sb("we_lo", [P, KD, 4 * D], F32R, where=atn)
    trig = sb("trig", [P, 2, TT, DK // 2], where=atn)
    rot_t = h32[:, :, :].rearrange("p k (n h f) -> p (k n) h f", n=2, f=DK // 2)
    rot = gw[:, :, :].rearrange("p k (h f) -> p (k h) f", f=DK)
    qt = sb("qt", [P, HEADS // 2, SEQ], F32R, where=atn)
    kt = sb("kt", [P, HEADS // 2, SEQ], F32R, where=atn)
    vv = sb("vv", [P, TT, HEADS, 32], where=atn)
    pp = work[:, :].rearrange("p (a n) -> p a n", a=2)
    pt_all = sb("pt_all", [P, 2 * 1280], where=atn)
    pt = pt_all[:, :].rearrange("p (a n) -> p a n", a=2)
    stack = pt_all[:, 0:2 * HEADS * SLOT].rearrange("p (h s) -> p h s", s=SLOT)
    nmax = sb("nmax", [P, HEADS, TT], where=atn)
    ssum = sb("ssum", [P, HEADS, TT], where=atn)
    rsum = sb("rsum", [P, HEADS, TT], where=atn)
    ot = outs
    on = xn
    mask_a = sb("mask_a", [P, P], BF16, where=atn)
    atn.close()
    s_atn = sem("attention_in")
    ATN_IN = 16 * 8
    w_b, w_ba, w_sum, w_high = (sem("adapter_" + n) for n in ("b_chosen", "product", "added", "high"))
    s_qkv, s_vout, s_qkread = sem("qkv_done"), sem("values_out"), sem("qk_read")
    s_stack, s_tr, s_trout = sem("stack_ready"), sem("stack_turned"), sem("turned_out")
    PROJ = (0, 6)
    s_s, s_max = sem("scores_done"), sem("max_done")
    s_exp, s_turn, s_ptev, s_pv = sem("probs_done"), sem("probs_turned"), sem("probs_out"), sem("pv_done")
    s_otev = sem("heads_out")

    QOFF = [0, 128, 384, 768]
    UNITS = [[(3, 0)], [(0, 0), (2, 128)], [(1, 0)]]
    TUNITS = [[(0, 0)], [(1, 0), (3, 384)], [(2, 0)]]
    KOFF = {0: 0, 1: 512, 3: 896, 2: 1024}
    TOFF = [(0, 512), (512, 512), (1024, 256)]

    def attn_sync(e, over):
        loads = [(wt[:, :, :], io["wt"]), (la[:, :, :], io["la"]), (lb[:, :, :], io["lb"]),
                 (starts_i[:, :], io["starts"].rearrange("(o n) -> o n", o=1).broadcast_to([LORAS * RANK, LORAS])),
                 (own_id[:, :], io["own_id"]), (bnum[:, :, :], io["bnum"]), (trig[:, :, :, :], io["trig"]),
                 (mask_a[:, :], io["mask_a"])]
        e.wait_ge(met, over)
        for dst, src in loads:
            e.dma_start(dst, src).then_inc(s_atn, 16)

    def attn_dve(v):
        e = v.e
        e.wait_ge(s_atn, ATN_IN)
        v.step(e.tensor_copy(starts[:, :], starts_i[:, :]))
        v.step(e.tensor_tensor(cnt[:, :, :], bnum[:, :, :],
                               starts[:, :].unsqueeze(1).broadcast_to([LORAS * RANK, GROUPS, LORAS]), ALU.is_ge))
        v.step(e.tensor_reduce(pick[:, :], cnt[:, :, :], AX.X, ALU.add))
        v.step(e.tensor_scalar(pick[:, :], pick[:, :], -1.0, 0.0, ALU.add, ALU.max))
        v.step(e.tensor_scalar(pick[:, :], pick[:, :], own_id[:, 0:1], None, ALU.is_equal))
        v.own.add(e.memset(vv[:, :, :, :], 0.0))
        e.wait_ge(s_dve, v.own.now())
        with e.Fori(0, GROUPS) as b:
            v.enter(b, ATTN_MEETS, ATTN_STEPS, ONE_GROUP)
            e.tensor_scalar(lbm[:, :, :], lb[:, :, :], pick[:, bass.ds(b, 1)], None, ALU.mult).then_inc(w_b, 1)
            v.own.add(e.memset(stack[:, :, 3 * DK:SLOT], 0.0))

            def effective():
                e.wait_ge(w_ba, b + 1)
                for k in range(KD):
                    for n in range(2):
                        last = e.tensor_tensor(we[:, k, n * 512:(n + 1) * 512], bank[2 + 2 * k + n][:, :],
                                               wt[:, k, n * 512:(n + 1) * 512], ALU.add)
                last.then_inc(w_sum, 1)

            def effective_low():
                e.wait_ge(w_high, b + 1)
                v.own.add(e.tensor_tensor(we_lo[:, :, :], we[:, :, :], we_hi[:, :, :].bitcast(FP32), ALU.subtract))

            norm_dve(v, b, 0, 0, effective, effective_low)
            for i in range(TT):
                g = b * TT + i
                qk = bank[PROJ[i % 2]][:, :].rearrange("p (h f two) -> p h f two", f=DK // 2, two=2)
                cos = trig[:, 0, i, :].unsqueeze(1).broadcast_to([P, 2 * HEADS, DK // 2])
                sin = trig[:, 1, i, :].unsqueeze(1).broadcast_to([P, 2 * HEADS, DK // 2])
                e.wait_ge(s_qkv, g + 1)
                e.wait_ge(s_dve, v.own.now())
                for n, (half, fac) in enumerate(((0, cos), (1, sin), (0, sin), (1, cos))):
                    last = e.tensor_tensor(rot_t[:, n, :, :], qk[:, :, :, half], fac, ALU.mult)
                last.then_inc(s_qkread, 1)
                e.wait_ge(s_qkread, g + 1)
                v.own.add(e.tensor_tensor(rot[:, :, 0:DK // 2], rot_t[:, 0, :, :], rot_t[:, 1, :, :], ALU.subtract))
                v.own.add(e.tensor_tensor(rot[:, :, DK // 2:DK], rot_t[:, 2, :, :], rot_t[:, 3, :, :], ALU.add))
                e.wait_ge(s_dve, v.own.now())
                if i:
                    e.wait_ge(s_tr, g)
                v.step(e.tensor_copy(stack[:, :, 0:DK].bitcast(F32R), rot[:, :, :]))
                v.own.add(e.tensor_tensor(stack[:, 0:HEADS, 2 * DK:3 * DK].bitcast(F32R), rot[:, 0:HEADS, :],
                                          stack[:, 0:HEADS, 0:DK], ALU.subtract))
                v.own.add(e.tensor_tensor(stack[:, HEADS:, DK:2 * DK].bitcast(F32R), rot[:, HEADS:, :],
                                          stack[:, HEADS:, 0:DK], ALU.subtract))
                v.own.add(e.tensor_copy(stack[:, 0:HEADS, DK:2 * DK], stack[:, 0:HEADS, 0:DK]))
                last = e.tensor_copy(stack[:, HEADS:, 2 * DK:3 * DK], stack[:, HEADS:, 0:DK])
                last.then_inc(s_stack, 1)
            v.together()
            for h in range(HEADS):
                for u, unit in enumerate(UNITS):
                    n = 3 * h + u
                    e.wait_ge(s_s, b * (3 * HEADS) + n + 1)
                    for q, col in unit:
                        last = e.tensor_reduce(nmax[:, h, q:q + 1], bank[n % 3][:, col:col + P * (q + 1)],
                                               AX.X, ALU.max, negate=True)
                    last.then_inc(s_max, 1)
                if h >= 1:
                    attn_evac(e, b, h - 1, 0)
            attn_evac(e, b, HEADS - 1, 0)
            v.together()
            v.step(e.reciprocal(rsum[:, :, :], ssum[:, :, :]))
            v.together()
            for i in range(TT):
                src = bank[i][:, :].rearrange("p (h s) -> p h s", s=32)[:, :, 0:DK]
                v.own.add(e.tensor_tensor(on[:, i, :].rearrange("p (h s) -> p h s", s=DK), src,
                                          rsum[:, :, i:i + 1].broadcast_to([P, HEADS, DK]), ALU.mult))
            v.together()
            v.together()
            for k in range(KD):
                v.own.add(e.tensor_copy(h32[:, k, :], bank[4 + k][:, :]))
            v.together()
            v.together()
            for k in range(KD):
                v.own.add(e.tensor_tensor(hb_lo[:, k, :], h32[:, k, :], hb_hi[:, k, :].bitcast(FP32), ALU.subtract))
            v.together()
            tail_dve(v, b, (bank[0], bank[1]), 0, False)
            norm_dve(v, b, 0, 1)
            route_dve(v, b, 0)
            v.leave(GROUPS)

    def attn_evac(e, b, h, who):
        for u in ((0, 2), (1,))[who]:
            n = 3 * h + u
            e.wait_ge(s_turn, b * (3 * HEADS) + n + 1)
            if h >= 2:
                e.wait_ge(s_pv, b * HEADS + h - 1)
            off, size = TOFF[u]
            src, dst = bank[3 + u][:, 0:size], pt[:, h % 2, off:off + size]
            if who == 0:
                e.tensor_copy(dst, src).then_inc(s_ptev, 1)
            else:
                e.activation(dst, src, ACT.Copy).then_inc(sem("probs_out_act"), 1)

    ATTN_MEETS = NORM_MEETS + 1 + 2 + 2 + 2 + 1 + TAIL_MEETS + NORM_MEETS + ROUTE_MEETS
    ATTN_STEPS = (NORM_STEPS * 2 + 1 + 1 + TT * (2 + 1 + 3) + 1 + TT + 2 * KD
                  + TAIL_STEPS + ROUTE_STEPS[0])

    def attn_act(a):
        e = a.e
        with e.Fori(0, GROUPS) as b:
            a.enter(b, ATTN_MEETS, 0, ONE_GROUP)
            def effective_high():
                e.wait_ge(w_sum, b + 1)
                e.activation(we_hi[:, :, :], we[:, :, :], ACT.Copy).then_inc(w_high, 1)

            norm_act(a, b, 0, 0, effective_high)

            def values(i):
                e.wait_ge(s_qkv, b * TT + i + 1)
                e.activation(vv[:, i, :, 0:DK], bank[PROJ[i % 2] + 1][:, 0:D].rearrange("p (h s) -> p h s", s=DK),
                             ACT.Copy).then_inc(s_vout, 1)

            values(0)
            for i in range(TT):
                if i + 1 < TT:
                    values(i + 1)
                e.wait_ge(s_tr, b * TT + i + 1)
                for n in range(2):
                    e.activation(qt[:, 4 * n:4 * n + 4, i * P:(i + 1) * P],
                                 bank[2 + n][:, :].rearrange("p (h t) -> p h t", h=4), ACT.Copy, scale=0.25)
                for n in range(2):
                    last = e.activation(kt[:, 4 * n:4 * n + 4, i * P:(i + 1) * P],
                                        bank[4 + n][:, :].rearrange("p (h t) -> p h t", h=4), ACT.Copy)
                last.then_inc(s_trout, 1)
            a.together()
            for h in range(HEADS):
                if h >= 2:
                    e.wait_ge(s_turn, b * (3 * HEADS) + 3 * (h - 1))
                for u, unit in enumerate(UNITS):
                    e.wait_ge(s_max, b * (3 * HEADS) + 3 * h + u + 1)
                    for q, col in unit:
                        w = P * (q + 1)
                        last = e.activation(pp[:, h % 2, QOFF[q]:QOFF[q] + w], bank[u][:, col:col + w], ACT.Exp,
                                            bias=nmax[:, h, q:q + 1], accum_out=ssum[:, h, q:q + 1])
                    last.then_inc(s_exp, 1)
                if h >= 1:
                    attn_evac(e, b, h - 1, 1)
                if h >= 4 and h % 4 == 2:
                    attn_out(e, b, h // 4 - 1)
            attn_evac(e, b, HEADS - 1, 1)
            attn_out(e, b, HEADS // 4 - 1)
            a.together()
            a.together()
            a.together()
            a.together()
            a.together()
            for k in range(KD):
                e.activation(hb_hi[:, k, :], h32[:, k, :], ACT.Copy)
            a.together()
            a.together()
            tail_other(a)
            norm_act(a, b, 0, 1)
            route_act(a, b, 0)
            a.leave(GROUPS)

    def attn_out(e, b, g):
        e.wait_ge(s_pv, b * HEADS + 4 * g + 4)
        e.activation(ot[:, g, :], bank[6 + g % 2][:, :], ACT.Copy).then_inc(s_otev, 1)

    def attn_pe(t):
        e = t.e
        with e.Fori(0, GROUPS) as b:
            t.enter(b, ATTN_MEETS, 0, ONE_GROUP)
            e.wait_ge(w_b, b + 1)
            for k in range(KD):
                for n in range(2):
                    for w in range(2):
                        mm = e.matmul(bank[2 + 2 * k + n][:, w * D:(w + 1) * D], la[:, 2 * n + w, k * P:(k + 1) * P],
                                      lbm[:, 2 * n + w, :], start=True, stop=True)
            mm.then_inc(w_ba, 1)
            norm_pe(t)

            def project(i):
                tok = slice(i * P, (i + 1) * P)
                if i >= 2:
                    e.wait_ge(s_qkread, b * TT + i - 1)
                    e.wait_ge(s_vout, b * TT + i - 1)
                for dst, cols in ((bank[PROJ[i % 2]][:, :], slice(0, 512)),
                                  (bank[PROJ[i % 2] + 1][:, 0:D], slice(512, QKV))):
                    n = 0
                    for k in range(KD):
                        for l, r in ((hb_hi, we_hi), (hb_hi, we_lo), (hb_lo, we_hi)):
                            mm = e.matmul(dst, l[:, k, tok], r[:, k, cols], start=(n == 0), stop=(n == 3 * KD - 1))
                            n += 1
                mm.then_inc(s_qkv, 1)

            project(0)
            for i in range(TT):
                if i + 1 < TT:
                    project(i + 1)
                e.wait_ge(s_stack, b * TT + i + 1)
                if i:
                    e.wait_ge(s_trout, b * TT + i)
                for h in range(HEADS):
                    mm = e.transpose(bank[2 + h // 4][:, (h % 4) * P:(h % 4 + 1) * P],
                                     stack[:, 2 * h:2 * h + 2, :].rearrange("p a s -> p (a s)"), ident[:, :])
                mm.then_inc(s_tr, 1)
            t.together()
            for h in range(HEADS + 2):
                if h < HEADS:
                    rows = slice(SLOT * (h % 2), SLOT * (h % 2) + SLOT)
                    for u, unit in enumerate(UNITS):
                        if h >= 1:
                            e.wait_ge(s_exp, b * (3 * HEADS) + 3 * (h - 1) + u + 1)
                        for q, col in unit:
                            w = P * (q + 1)
                            e.matmul(bank[u][:, col:col + w], qt[rows, h // 2, q * P:(q + 1) * P],
                                     kt[rows, h // 2, 0:w], start=True, stop=False)
                            last = e.matmul(bank[u][:, col + w - P:col + w], ident_b[:, :], mask_a[:, :],
                                            start=False, stop=True)
                        last.then_inc(s_s, 1)
                if 1 <= h <= HEADS:
                    g = h - 1
                    for u, unit in enumerate(TUNITS):
                        e.wait_ge(s_exp, b * (3 * HEADS) + 3 * g + 3)
                        if g >= 1:
                            if u == 1:
                                e.wait_ge(sem("probs_out_act"), b * HEADS + g)
                            else:
                                e.wait_ge(s_ptev, b * (2 * HEADS) + 2 * (g - 1) + (1 if u == 0 else 2))
                        for k, col in unit:
                            for q in range(k, TT):
                                last = e.transpose(bank[3 + u][:, col + (q - k) * P:col + (q - k + 1) * P],
                                                   pp[:, g % 2, QOFF[q] + k * P:QOFF[q] + (k + 1) * P], ident[:, :])
                        last.then_inc(s_turn, 1)
                if h >= 2:
                    g = h - 2
                    e.wait_ge(s_ptev, b * (2 * HEADS) + 2 * g + 2)
                    e.wait_ge(sem("probs_out_act"), b * HEADS + g + 1)
                    if g % 4 == 0 and g >= 8:
                        e.wait_ge(s_otev, b * 4 + g // 4 - 1)
                    rows = slice(32 * (g % 4), 32 * (g % 4) + 32)
                    for k in range(TT):
                        last = e.matmul(bank[6 + (g // 4) % 2][rows, k * P:512], vv[:, k, g, :],
                                        pt[:, g % 2, KOFF[k]:KOFF[k] + SEQ - k * P],
                                        start=(k == 0), stop=(k == TT - 1), tile_position=(0, 32 * (g % 4)))
                    last.then_inc(s_pv, 1)
            t.together()
            for i in range(TT):
                for g in range(4):
                    e.transpose(bank[i][:, g * P:(g + 1) * P], ot[:, g, i * P:(i + 1) * P], ident[:, :])
            t.together()
            t.together()
            for k in range(KD):
                for i in range(TT):
                    e.transpose(bank[4 + k][:, i * P:(i + 1) * P], on[:, i, k * P:(k + 1) * P], ident[:, :])
            for _ in range(4):
                t.together()
            for i in range(TT):
                n = 0
                for k in range(KD):
                    for l, r in ((hb_hi, we_hi), (hb_lo, we_hi), (hb_hi, we_lo)):
                        e.matmul(token_major((bank[0], bank[1]), i), l[:, k, i * P:(i + 1) * P], r[:, k, QKV:4 * D],
                                 start=(n == 0), stop=(n == 3 * KD - 1))
                        n += 1
            tail_other(t)
            norm_pe(t)
            route_pe(t, b, 0)
            t.leave(GROUPS)

    def attn_pool(g):
        with g.e.Fori(0, GROUPS) as b:
            g.enter(b, ATTN_MEETS, 0, ONE_GROUP)
            norm_pool(g)
            for _ in range(ATTN_MEETS - 2 * NORM_MEETS - TAIL_MEETS - ROUTE_MEETS):
                g.together()
            tail_other(g)
            norm_pool(g)
            route_pool(g)
            g.leave(GROUPS)

    def moe(layer):
        name, J = f"moe{layer}", (J0, J1)[layer]
        JJ = J // 2
        own = ExitStack()
        WC = 2 * D + D
        sel = sb(name + "_sel", [P, J * P], BF16, where=own)
        raw = sb(name + "_raw", [P, 2, WC], where=own)
        w_hi = sb(name + "_whi", [P, 2, WC], F32R, where=own)
        w_lo = sb(name + "_wlo", [P, 2, WC], F32R, where=own)
        th = sb(name + "_th", [P, 2, SEQ], where=own)
        sg = sb(name + "_sg", [P, 2, SEQ], where=own)
        sc = sb(name + "_sc", [P, 2, SEQ], where=own)
        h = sb(name + "_h", [P, 2, SEQ], where=own)
        h_hi = sb(name + "_hhi", [P, 2, SEQ], F32R, where=own)
        h_lo = sb(name + "_hlo", [P, 2, SEQ], F32R, where=own)
        own.close()
        s_sel = sem(name + "_sel_in")
        s_raw = [sem(f"{name}_raw_in{u}") for u in range(2)]
        s_whi, s_wlo = sem(name + "_w_hi"), sem(name + "_w_lo")
        s_g, s_u, s_c = sem(name + "_gate_done"), sem(name + "_up_done"), sem(name + "_comb_done")
        s_th, s_hhi, s_hlo = sem(name + "_tanh"), sem(name + "_h_hi"), sem(name + "_h_lo")
        s_gu, s_cu, s_h = sem(name + "_gate_used"), sem(name + "_comb_used"), sem(name + "_h")
        s_d = sem(name + "_down_done")
        acc = [[bank[0], bank[1]], [bank[2], bank[3]]]
        B_G, B_U, B_C = bank[4], bank[5], bank[6]
        MEETS = 2 * TAIL_MEETS

        def sync(e, over):
            e.wait_ge(met, over)
            e.dma_start(sel[:, :], io[f"sel{layer}"]).then_inc(s_sel, 16)
            with e.Fori(0, 2) as half:
                with e.Fori(0, JJ) as jj:
                    for u in range(2):
                        w = (half * JJ + jj) * 2 + u
                        e.wait_ge(s_whi, w + 1)
                        e.wait_ge(s_wlo, w + 1)
                        e.dma_start(raw[:, u, :], io[f"w{layer}"][bass.ds(jj * 2 + u, 1), :, :]
                                    .rearrange("o p n -> p (o n)")).then_inc(s_raw[u], 16)

        def loop(en, body, finish, meets, steps):
            with en.e.Fori(0, 2) as half:
                en.enter(half, MEETS, steps, {"norm": 0, "route": 0})
                body(half, 0, True, False)
                with en.e.Fori(1, JJ - 1) as jj:
                    body(half, jj, False, False)
                body(half, JJ - 1, False, True)
                finish(half)
                en.leave(2)

        def act(a):
            e = a.e
            e.drain().then_inc(s_whi, 2)

            def high(half, m_step, m):
                e.wait_ge(s_h, m + 3)
                e.wait_ge(s_d, m + 2)
                e.activation(h_hi[:, m_step % 2, :], h[:, m_step % 2, :], ACT.Copy).then_inc(s_hhi, 1)

            def split(pair, u):
                e.wait_ge(s_raw[u], pair * 16 + 16)
                e.wait_ge(s_d, pair * 4 + (2 * u + 1))
                e.activation(w_hi[:, u, :], raw[:, u, :], ACT.Copy).then_inc(s_whi, 1)

            def body(half, jj, first, last):
                if first:
                    split(half * JJ, 0)
                for s in range(4):
                    u, tg = s // 2, s % 2
                    m = half * (4 * JJ) + jj * 4 + s
                    if s == 1:
                        split(half * JJ + jj, 1)
                    if s == 3 and not last:
                        split(half * JJ + jj + 1, 0)
                    if not (first and s == 0):
                        high(half, s + 1, m - 1)
                    e.wait_ge(s_g, m + 1)
                    e.wait_ge(s_gu, m + 1)
                    e.activation(th[:, tg, :], B_G[:, :], ACT.Tanh, scale=0.5).then_inc(s_th, 1)

            def finish(half):
                high(half, 3, half * (4 * JJ) + 4 * JJ - 1)
                for tg in range(2):
                    tail_other(a)

            loop(a, body, finish, MEETS, 0)

        def pool(g):
            e = g.e
            e.drain().then_inc(s_wlo, 2)

            def body(half, jj, first, last):
                for u in range(2):
                    w = (half * JJ + jj) * 2 + u
                    e.wait_ge(s_whi, w + 3)
                    e.tensor_tensor(w_lo[:, u, :], raw[:, u, :], w_hi[:, u, :].bitcast(FP32),
                                    ALU.subtract).then_inc(s_wlo, 1)

            def finish(half):
                for tg in range(2):
                    tail_other(g)

            loop(g, body, finish, MEETS, 0)

        def dve(v):
            e = v.e
            e.drain().then_inc(s_gu, 2)
            e.drain().then_inc(s_cu, 2)
            e.drain().then_inc(s_h, 2)

            def low(s, m):
                e.wait_ge(s_hhi, m + 1)
                e.wait_ge(s_d, m + 2)
                e.tensor_tensor(h_lo[:, s % 2, :], h[:, s % 2, :], h_hi[:, s % 2, :].bitcast(FP32),
                                ALU.subtract).then_inc(s_hlo, 1)

            def body(half, jj, first, last):
                for s in range(4):
                    tg = s % 2
                    m = half * (4 * JJ) + jj * 4 + s
                    if not (first and s == 0):
                        low(s + 1, m - 1)
                    e.wait_ge(s_th, m + 1)
                    e.wait_ge(s_cu, m + 1)
                    e.scalar_tensor_tensor(out=sg[:, tg, :], in0=th[:, tg, :], scalar=1.0, in1=B_G[:, :],
                                           op0=ALU.add, op1=ALU.mult).then_inc(s_gu, 1)
                    e.wait_ge(s_c, m + 1)
                    e.wait_ge(s_gu, m + 3)
                    e.wait_ge(s_h, m + 1)
                    e.tensor_tensor(sc[:, tg, :], sg[:, tg, :], B_C[:, :], ALU.mult).then_inc(s_cu, 1)
                    e.wait_ge(s_u, m + 1)
                    e.wait_ge(s_cu, m + 3)
                    if not (first and s < 2):
                        e.wait_ge(s_hlo, m - 1)
                    e.tensor_tensor(h[:, tg, :], sc[:, tg, :], B_U[:, :], ALU.mult).then_inc(s_h, 1)

            def finish(half):
                low(3, half * (4 * JJ) + 4 * JJ - 1)
                for tg in range(2):
                    tail_dve(v, half * 2 + tg, acc[tg], 2 * layer + 1, False)

            loop(v, body, finish, MEETS, 2 * TAIL_STEPS)

        def pe(t):
            e = t.e
            e.drain().then_inc(s_d, 3)
            e.wait_ge(s_sel, 16)

            def down(s, m, u):
                e.wait_ge(s_hhi, m + 1)
                e.wait_ge(s_hlo, m + 1)
                tg = s % 2
                for i in range(TT):
                    rows = slice(i * P, (i + 1) * P)
                    for l, r in ((h_hi, w_hi), (h_lo, w_hi), (h_hi, w_lo)):
                        mm = e.matmul(token_major(acc[tg], i), l[:, tg, rows], r[:, u, 2 * D:3 * D],
                                      start=False, stop=False, skip_group_check=True)
                mm.then_inc(s_d, 1)

            def body(half, jj, first, last):
                if first:
                    for a2 in acc:
                        for o in range(KD):
                            e.matmul(a2[o][:, :], zero_b[:, :], zero_r[:, :], start=True, stop=False,
                                     skip_group_check=True)
                for s in range(4):
                    u, tg = s // 2, s % 2
                    m = half * (4 * JJ) + jj * 4 + s
                    w = (half * JJ + jj) * 2 + u
                    col = half * (2 * SEQ) + tg * SEQ
                    if tg == 0:
                        e.wait_ge(s_whi, w + 3)
                        e.wait_ge(s_wlo, w + 3)
                    for dst, base, used, done in ((B_G, 0, s_gu, s_g), (B_U, D, s_h, s_u)):
                        e.wait_ge(used, m + 2)
                        n = 0
                        for k in range(KD):
                            rh, rl = ht_hi[:, k, bass.ds(col, SEQ)], ht_lo[:, k, bass.ds(col, SEQ)]
                            cols = slice(base + k * P, base + (k + 1) * P)
                            for l, r in ((w_hi, rh), (w_hi, rl), (w_lo, rh)):
                                mm = e.matmul(dst[:, :], l[:, u, cols], r, start=(n == 0), stop=(n == 3 * KD - 1))
                                n += 1
                        mm.then_inc(done, 1)
                    e.wait_ge(s_cu, m + 2)
                    e.matmul(B_C[:, :], sel[:, bass.ds((jj * 2 + u) * P, P)], comb_t[:, bass.ds(col, SEQ)],
                             start=True, stop=True).then_inc(s_c, 1)
                    if not (first and s == 0):
                        down(s + 1, m - 1, ((s + 3) % 4) // 2)

            def finish(half):
                down(3, half * (4 * JJ) + 4 * JJ - 1, 1)
                for a2 in acc:
                    for o in range(KD):
                        e.matmul(a2[o][:, :], zero_b[:, :], zero_r[:, :], start=False, stop=True,
                                 skip_group_check=True)
                for tg in range(2):
                    tail_other(t)

            loop(t, body, finish, MEETS, 0)

        return (sync, act, pool, dve, pe), 4 * 2 * MEETS

    ssm_mem = ExitStack()

    def sm(name, shape, dt=FP32):
        return sb(name, shape, dt, where=ssm_mem)

    NC = TT
    cw = sm("cw", [P, FT + 2, TAPS + 1])
    nw = sm("nw", [P, FT])
    dsk = sm("dsk", [P, FT])
    a_neg = sm("a_neg", [P, 2])
    dtb = sm("dtb", [P, 2])
    wb = sm("wb", [P, 4, D])
    wb_hi, wb_lo = sm("wb_hi", [P, 4, D], F32R), sm("wb_lo", [P, 4, D], F32R)
    sel_p = sm("sel_p", [P, 2, FT], BF16)
    last_r = sm("last_r", [P, P], F32R)
    last_f = sm("last_f", [P, P])
    reset = sm("reset", [P, SEQ])
    mask_s = sm("mask_s", [P, SEQ], BF16)
    raw_i, raw_o = sm("raw_i", [P, 2, 2 * D]), sm("raw_o", [P, 2, D])
    wi_hi, wi_lo = sm("wi_hi", [P, 2, 2 * D], F32R), sm("wi_lo", [P, 2, 2 * D], F32R)
    wo_hi, wo_lo = sm("wo_hi", [P, 2, D], F32R), sm("wo_lo", [P, 2, D], F32R)
    cv = sm("cv", [P, 2, SEQ])
    thx, thg = sm("thx", [P, SEQ]), sm("thg", [P, SEQ])
    xc = sm("xc", [P, 2, SEQ])
    sgt = sm("sgt", [P, 2, SEQ])
    bc = sm("bc", [P, 2, SEQ])
    c_t = sm("c_t", [P, SEQ])
    b_tok = sm("b_tok", [P, NC, P])
    g_mat = sm("g_mat", [P, NC, P])
    cum_b = sm("cum_b", [P, 2, SEQ], BF16)
    cum_tok = sm("cum_tok", [P, NC, SSM_HEADS])
    ct_hi, ct_lo = sm("ct_hi", [P, NC, SSM_HEADS], F32R), sm("ct_lo", [P, NC, SSM_HEADS], F32R)
    dt_tok = sm("dt_tok", [P, NC, 2, FT])
    dec_tok = sm("dec_tok", [P, NC, 2, FT])
    e_last = sm("e_last", [P, NC, 2, FT])
    e_in = h32
    l_mat = sm("l_mat", [P, 2, SEQ])
    m_mat = outs[:, :, :].rearrange("p (s h) t -> p s h t", s=2)
    ce = sm("ce", [P, 2, 2, SEQ - P])
    xdt = xn[:, :, :].rearrange("p (s a) (b f) -> p s (a b) f", s=2, f=P)
    xdec = sm("xdec", [P, NC - 1, P])
    st = sm("st", [P, 2, NC - 1, P])
    yd, yg = sm("yd", [P, SEQ]), sm("yg", [P, SEQ])
    y_hi, y_lo = sm("y_hi", [P, 2, SEQ], F32R), sm("y_lo", [P, 2, SEQ], F32R)
    sq, sq_sum = sm("sq", [P, SEQ]), sm("sq_sum", [P, SEQ])
    dt_t, dt_u, dt_v = outs[:, 0:2, :], outs[:, 2:4, :], l_mat
    cum_t = xn[:, :, :].rearrange("p (n a) d -> p n (a d)", n=2)
    low_p = h32[:, :, :].bitcast(BF16)[:, :, 0:SEQ]
    ssm_mem.close()

    s_ssm = sem("mixer_in")
    s_ri = [sem(f"in_weights_in{u}") for u in range(2)]
    s_ro = [sem(f"out_weights_in{u}") for u in range(2)]
    (s_wih, s_wil, s_woh, s_wol, s_x, s_z, s_cb, s_mk, s_cv, s_thx, s_thz, s_xc, s_sg, s_e, s_l, s_m, s_ce, s_t,
     s_xdt, s_xdec, s_ss, s_y, s_yd, s_yg, s_sq, s_acc, s_yhi, s_ylo, s_o) = [sem("mix_" + n) for n in (
         "in_hi", "in_lo", "out_hi", "out_lo", "x", "z", "cum_bcast", "cum_masked", "conv_first", "tanh_x", "tanh_z",
         "x_conv", "silu_z", "decay_in", "decay_mat", "m_mat", "c_decayed", "x_turned", "x_dt", "x_decayed",
         "state_sums", "y", "y_skip", "y_gated", "squares", "squares_summed", "y_hi", "y_lo", "out")]
    s_tap, s_st = sem("mix_taps"), sem("mix_states")
    PSZ, PSX, PCB, PT, PY = bank[2], bank[3], (bank[4], bank[5]), bank[6], bank[7]
    SSM_IN = 16 * 10
    SSM_PRE = 1
    (g_proj, g_dt, g_bias, g_abs, g_log, g_taps, g_tanh, g_cum, g_turned, g_bc, g_bc_out, g_ct, g_last, g_dec) = [
        sem("group_" + n) for n in ("projected", "dt_in", "bc_bias", "minus_abs", "log", "bc_taps", "bc_tanh",
                                    "running_sums", "turned", "bc", "bc_products", "sums_split", "last_sums",
                                    "decays")]
    SSM_POST = 1 + 2 + TAIL_MEETS + NORM_MEETS + ROUTE_MEETS
    SSM_MEETS = NORM_MEETS + SSM_PRE + SSM_POST
    AHEAD = 3

    def done(g, each=1):
        return each * g + (each + 3)

    class Tile:

        def __init__(self, b, it, u, back, static):
            self.f = it * 2 + (u - back)
            self.slot = (u - back) % 2
            self.half = it + (u - back) // 2
            self.g = b * FT + self.f
            self.one = slice(self.f, self.f + 1) if static else bass.ds(self.f, 1)
            self.live = not static or 0 <= self.f < FT
            self.b = b

    def ssm_steps(en, b, step):
        def run(it, u, static):
            step(en, [Tile(b, it, u, back, static) for back in range(AHEAD + 1)])

        for ft in range(4):
            run(ft // 2, ft % 2, True)
        with en.e.Fori(2, FT // 2) as it:
            for u in range(2):
                run(it, u, False)
        for ft in range(FT, FT + AHEAD):
            run(ft // 2, ft % 2, True)

    def ssm_sync(e, over):
        e.wait_ge(met, over)
        loads = [(cw[:, :, :], io["cw"]), (nw[:, :], io["nw"]), (dsk[:, :], io["dsk"]), (a_neg[:, :], io["a_log"]),
                 (dtb[:, :], io["dt_bias"]), (wb[:, :, :], io["wb"]), (sel_p[:, :, :], io["sel_p"]),
                 (last_f[:, :], io["last_f"]), (reset[:, :], io["reset"]), (mask_s[:, :], io["mask_s"])]
        for dst, src in loads:
            e.dma_start(dst, src).then_inc(s_ssm, 16)
        def step(_, tiles):
            w = tiles[0]
            if w.live:
                e.wait_ge(s_wih, done(w.g - 2))
                e.wait_ge(s_wil, done(w.g - 2))
                e.dma_start(raw_i[:, w.slot, :], io["wi"][w.one, :, :]
                            .rearrange("o p n -> p (o n)")).then_inc(s_ri[w.slot], 16)
            w = tiles[1]
            if w.live:
                e.wait_ge(s_woh, done(w.g - 2))
                e.wait_ge(s_wol, done(w.g - 2))
                e.dma_start(raw_o[:, w.slot, :], io["wo"][w.one, :, :]
                            .rearrange("o p n -> p (o n)")).then_inc(s_ro[w.slot], 16)

        with e.Fori(0, GROUPS) as b:
            ssm_steps(Engine(e, "sync", None), b, step)

    def ssm_pe_step(t, tiles):
        e = t.e

        def project(w, dst, base, sem_done):
            n = 0
            for k in range(KD):
                cols = slice(base + k * P, base + (k + 1) * P)
                for l, r in ((wi_hi, hb_hi), (wi_hi, hb_lo), (wi_lo, hb_hi)):
                    mm = e.matmul(dst[:, :], l[:, w.slot, cols], r[:, k, :], start=(n == 0), stop=(n == 3 * KD - 1))
                    n += 1
            mm.then_inc(sem_done, 1)

        w = tiles[0]
        if w.live:
            e.wait_ge(s_wih, done(w.g))
            e.wait_ge(s_wil, done(w.g))
            e.wait_ge(s_tap, done(w.g - 1, 3))
            project(w, PSX, D, s_x)
        w = tiles[1]
        if w.live:
            e.wait_ge(s_xc, done(w.g))
            e.wait_ge(s_st, done(w.g - 1, 3))
            for c in range(NC):
                mm = e.transpose(PT[:, c * P:(c + 1) * P], xc[:, w.slot, c * P:(c + 1) * P], ident[:, :])
            mm.then_inc(s_t, 1)
        w = tiles[0]
        if w.live:
            e.wait_ge(s_l, done(w.g - 1))
            for hh in range(2):
                mm = e.matmul(PCB[hh][:, :], sel_p[:, 0, bass.ds(w.f, 1)].broadcast_to([P, P]), cum_b[:, hh, :],
                              start=True, stop=False, skip_group_check=True)
            mm.then_inc(s_cb, 1)
        w = tiles[2]
        if w.live:
            e.wait_ge(s_m, done(w.g))
            e.wait_ge(s_ce, done(w.g))
            e.wait_ge(s_st, done(w.g, 3))
            e.wait_ge(s_yd, done(w.g - 1))
            for c in range(NC):
                for hh in range(2):
                    rows = slice(hh * SSM_P, (hh + 1) * SSM_P)
                    mm = e.matmul(PY[rows, c * P:(c + 1) * P], xdt[:, w.slot, c, rows],
                                  m_mat[:, w.slot, hh, c * P:(c + 1) * P],
                                  start=True, stop=(c == 0), skip_group_check=True)
                for hh in range(2):
                    rows = slice(hh * SSM_P, (hh + 1) * SSM_P)
                    if c:
                        mm = e.matmul(PY[rows, c * P:(c + 1) * P], st[:, w.slot, c - 1, rows],
                                      ce[:, w.slot, hh, (c - 1) * P:c * P], start=False, stop=True,
                                      skip_group_check=True)
            mm.then_inc(s_y, 1)
        w = tiles[0]
        if w.live:
            e.wait_ge(s_sg, done(w.g - 1))
            project(w, PSZ, 0, s_z)
        w = tiles[0]
        if w.live:
            e.wait_ge(s_e, done(w.g))
            for hh in range(2):
                for c in range(NC):
                    cols = slice(c * P, (c + 1) * P)
                    e.matmul(PCB[hh][:, cols], cum_b[:, hh, cols],
                             sel_p[:, 1, bass.ds(w.f, 1)].broadcast_to([P, P]), start=False, stop=False,
                             skip_group_check=True)
                mm = e.matmul(PCB[hh][:, :], ident_b[:, :], mask_s[:, :], start=False, stop=True,
                              skip_group_check=True)
            mm.then_inc(s_mk, 1)
        w = tiles[1]
        if w.live:
            e.wait_ge(s_xdec, done(w.g))
            for c in range(NC - 1):
                mm = e.matmul(PT[:, c * P:(c + 1) * P], b_tok[:, c, :], xdec[:, c, :], start=True, stop=True)
            mm.then_inc(s_ss, 1)
        w = tiles[3]
        if w.live:
            e.wait_ge(s_yhi, done(w.g))
            e.wait_ge(s_ylo, done(w.g))
            e.wait_ge(s_woh, done(w.g))
            e.wait_ge(s_wol, done(w.g))
            for i in range(TT):
                for l, r in ((y_hi, wo_hi), (y_lo, wo_hi), (y_hi, wo_lo)):
                    mm = e.matmul(token_major((bank[0], bank[1]), i), l[:, w.slot, i * P:(i + 1) * P],
                                  r[:, w.slot, :], start=False, stop=False, skip_group_check=True)
            mm.then_inc(s_o, 1)

    def ssm_act_step(a, tiles):
        e = a.e
        w = tiles[0]
        if w.live:
            e.wait_ge(s_ri[w.slot], (w.b * (FT // 2) + w.half) * 16 + 16)
            e.wait_ge(s_x, done(w.g - 2))
            e.wait_ge(s_z, done(w.g - 2))
            e.activation(wi_hi[:, w.slot, :], raw_i[:, w.slot, :], ACT.Copy).then_inc(s_wih, 1)
        w = tiles[1]
        if w.live:
            e.wait_ge(s_mk, done(w.g))
            e.wait_ge(s_m, done(w.g - 1))
            for hh in range(2):
                last = e.activation(l_mat[:, hh, :], PCB[hh][:, :], ACT.Exp)
            last.then_inc(s_l, 1)
        w = tiles[1]
        if w.live:
            e.wait_ge(s_tap, done(w.g, 3))
            e.wait_ge(s_xc, done(w.g - 1))
            e.activation(thx[:, :], cv[:, w.slot, :], ACT.Tanh, scale=0.5).then_inc(s_thx, 1)
        w = tiles[2]
        if w.live:
            e.wait_ge(s_ro[w.slot], (w.b * (FT // 2) + w.half) * 16 + 16)
            e.wait_ge(s_o, done(w.g - 2))
            e.activation(wo_hi[:, w.slot, :], raw_o[:, w.slot, :], ACT.Copy).then_inc(s_woh, 1)
        w = tiles[3]
        if w.live:
            e.wait_ge(s_yg, done(w.g))
            e.wait_ge(s_acc, done(w.g - 1))
            e.activation(sq[:, :], yg[:, :], ACT.Square).then_inc(s_sq, 1)
        w = tiles[1]
        if w.live:
            e.wait_ge(s_z, done(w.g))
            e.wait_ge(s_sg, done(w.g - 1))
            e.activation(thg[:, :], PSZ[:, :], ACT.Tanh, scale=0.5).then_inc(s_thz, 1)
        w = tiles[3]
        if w.live:
            e.wait_ge(s_yg, done(w.g))
            e.wait_ge(s_o, done(w.g - 2))
            e.activation(y_hi[:, w.slot, :], yg[:, :], ACT.Identity,
                         scale=nw[:, bass.ds(w.f, 1)]).then_inc(s_yhi, 1)
        w = tiles[0]
        if w.live:
            e.wait_ge(s_cb, done(w.g))
            e.wait_ge(s_ce, done(w.g - 1))
            for hh in range(2):
                last = e.activation(e_in[:, hh, P:SEQ], PCB[hh][:, P:SEQ], ACT.Exp)
            last.then_inc(s_e, 1)
        w = tiles[0]
        if w.live:
            e.wait_ge(s_x, done(w.g))
            e.wait_ge(s_xc, done(w.g - 2))
            e.activation(cv[:, w.slot, :], PSX[:, :], ACT.Identity, bias=cw[:, bass.ds(w.f, 1), TAPS],
                         scale=cw[:, bass.ds(w.f, 1), TAPS - 1]).then_inc(s_cv, 1)

    def ssm_dve_step(v, tiles):
        e = v.e
        w = tiles[1]
        if w.live:
            e.wait_ge(s_cv, done(w.g))
            for n in range(1, TAPS):
                if n > 1:
                    e.wait_ge(s_tap, 3 * w.g + 2 + n)
                e.scalar_tensor_tensor(out=cv[:, w.slot, n:SEQ], in0=PSX[:, 0:SEQ - n],
                                       scalar=cw[:, bass.ds(w.f, 1), TAPS - 1 - n], in1=cv[:, w.slot, n:SEQ],
                                       op0=ALU.mult, op1=ALU.add).then_inc(s_tap, 1)
        w = tiles[2]
        if w.live:
            e.wait_ge(s_ss, done(w.g))
            e.wait_ge(s_y, done(w.g - 2))
            e.tensor_copy(st[:, w.slot, 0, :], PT[:, 0:P]).then_inc(s_st, 1)
            for c in (1, 2):
                e.wait_ge(s_st, 3 * w.g + 3 + c)
                for hh in range(2):
                    cols = slice(hh * SSM_P, (hh + 1) * SSM_P)
                    last = e.scalar_tensor_tensor(out=st[:, w.slot, c, cols], in0=st[:, w.slot, c - 1, cols],
                                                  scalar=e_last[:, c, hh, bass.ds(w.f, 1)],
                                                  in1=PT[:, c * P + hh * SSM_P:c * P + (hh + 1) * SSM_P],
                                                  op0=ALU.mult, op1=ALU.add)
                last.then_inc(s_st, 1)
        w = tiles[1]
        if w.live:
            e.wait_ge(s_thx, done(w.g))
            e.wait_ge(s_yd, done(w.g - 2))
            e.scalar_tensor_tensor(out=xc[:, w.slot, :], in0=thx[:, :], scalar=1.0, in1=cv[:, w.slot, :],
                                   op0=ALU.add, op1=ALU.mult).then_inc(s_xc, 1)
        w = tiles[1]
        if w.live:
            e.wait_ge(s_l, done(w.g))
            e.wait_ge(s_y, done(w.g - 2))
            for hh in range(2):
                last = e.tensor_tensor(m_mat[:, w.slot, hh, :], l_mat[:, hh, :],
                                       g_mat[:, :, :].rearrange("p c l -> p (c l)"), ALU.mult)
            last.then_inc(s_m, 1)
        w = tiles[1]
        if w.live:
            e.wait_ge(s_thz, done(w.g))
            e.wait_ge(s_yg, done(w.g - 2))
            e.scalar_tensor_tensor(out=sgt[:, w.slot, :], in0=thg[:, :], scalar=1.0, in1=PSZ[:, :],
                                   op0=ALU.add, op1=ALU.mult).then_inc(s_sg, 1)
        w = tiles[1]
        if w.live:
            e.wait_ge(s_t, done(w.g))
            e.wait_ge(s_y, done(w.g - 2))
            e.tensor_tensor(xdt[:, w.slot, :, :].rearrange("p c (h f) -> p c h f", h=2),
                            PT[:, :].rearrange("p (c h f) -> p c h f", c=NC, h=2),
                            dt_tok[:, :, :, bass.ds(w.f, 1)].broadcast_to([P, NC, 2, SSM_P]),
                            ALU.mult).then_inc(s_xdt, 1)
        w = tiles[3]
        if w.live:
            e.wait_ge(s_yhi, done(w.g))
            e.wait_ge(s_o, done(w.g - 2))
            e.scalar_tensor_tensor(out=y_lo[:, w.slot, :], in0=yg[:, :], scalar=nw[:, bass.ds(w.f, 1)],
                                   in1=y_hi[:, w.slot, :].bitcast(FP32), op0=ALU.mult,
                                   op1=ALU.subtract).then_inc(s_ylo, 1)
        w = tiles[2]
        if w.live:
            e.wait_ge(s_y, done(w.g))
            e.wait_ge(s_yg, done(w.g - 1))
            e.scalar_tensor_tensor(out=yd[:, :], in0=xc[:, w.slot, :], scalar=dsk[:, bass.ds(w.f, 1)], in1=PY[:, :],
                                   op0=ALU.mult, op1=ALU.add).then_inc(s_yd, 1)

    def ssm_pool_step(q, tiles):
        e = q.e
        w = tiles[0]
        if w.live:
            e.wait_ge(s_wih, done(w.g))
            e.tensor_tensor(wi_lo[:, w.slot, :], raw_i[:, w.slot, :], wi_hi[:, w.slot, :].bitcast(FP32),
                            ALU.subtract).then_inc(s_wil, 1)
        w = tiles[3]
        if w.live:
            e.wait_ge(s_yd, done(w.g))
            e.wait_ge(s_sg, done(w.g))
            e.wait_ge(s_sq, done(w.g - 1))
            e.wait_ge(s_ylo, done(w.g - 1))
            e.tensor_tensor(yg[:, :], yd[:, :], sgt[:, w.slot, :], ALU.mult).then_inc(s_yg, 1)
        w = tiles[1]
        if w.live:
            e.wait_ge(s_e, done(w.g))
            e.wait_ge(s_y, done(w.g - 2))
            for hh in range(2):
                last = e.tensor_tensor(ce[:, w.slot, hh, :], e_in[:, hh, P:SEQ], c_t[:, P:SEQ], ALU.mult)
            last.then_inc(s_ce, 1)
        w = tiles[1]
        if w.live:
            e.wait_ge(s_xdt, done(w.g))
            e.wait_ge(s_ss, done(w.g - 1))
            e.tensor_tensor(xdec[:, :, :].rearrange("p c (h f) -> p c h f", h=2),
                            xdt[:, w.slot, 0:NC - 1, :].rearrange("p c (h f) -> p c h f", h=2),
                            dec_tok[:, 0:NC - 1, :, bass.ds(w.f, 1)].broadcast_to([P, NC - 1, 2, SSM_P]),
                            ALU.mult).then_inc(s_xdec, 1)
        w = tiles[2]
        if w.live:
            e.wait_ge(s_woh, done(w.g))
            e.tensor_tensor(wo_lo[:, w.slot, :], raw_o[:, w.slot, :], wo_hi[:, w.slot, :].bitcast(FP32),
                            ALU.subtract).then_inc(s_wol, 1)
        w = tiles[3]
        if w.live:
            e.wait_ge(s_sq, done(w.g))
            e.wait_ge(s_acc, done(w.g - 1))
            e.tensor_tensor(sq_sum[:, :], sq_sum[:, :], sq[:, :], ALU.add).then_inc(s_acc, 1)

    def three_products(e, dst, pairs, start, stop):
        for n, (l, r) in enumerate(pairs):
            mm = e.matmul(dst, l, r, start=start and n == 0, stop=stop and n == len(pairs) - 1)
        return mm

    def ssm_pe(t):
        e = t.e
        for s in (s_x, s_z, s_cb, s_mk, s_t, s_ss, s_y, s_o):
            e.drain().then_inc(s, 3)
        t.together()
        t.together()
        with e.Fori(0, GROUPS) as b:
            t.enter(b, SSM_MEETS, 0, ONE_GROUP)
            norm_pe(t)
            for w in (2, 3, 0, 1):
                pairs = [(l[:, w, k * P:(k + 1) * P], r[:, k, :]) for k in range(KD)
                         for l, r in ((wb_hi, hb_hi), (wb_hi, hb_lo), (wb_lo, hb_hi))]
                three_products(e, bank[2 + w][:, :], pairs, True, True).then_inc(g_proj, 1)
            for o in range(KD):
                e.matmul(bank[o][:, :], zero_b[:, :], zero_r[:, :], start=True, stop=False, skip_group_check=True)
            e.wait_ge(g_cum, b + 1)
            t.passed()
            for c in range(NC):
                cols = slice(c * P, (c + 1) * P)
                for hh in range(2):
                    hc = slice((c * 2 + hh) * FT, (c * 2 + hh + 1) * FT)
                    e.transpose(bank[5][:, hc], cum_t[0:FT, hh, cols], ident[0:FT, 0:FT])
                    mm = e.transpose(bank[4][:, hc], dt_t[0:FT, hh, cols], ident[0:FT, 0:FT])
            mm.then_inc(g_turned, 1)
            e.wait_ge(g_bc, b + 1)
            for c in range(NC):
                cols = slice(c * P, (c + 1) * P)
                e.matmul(bank[7][:, cols], bc[:, 0, cols], bc[:, 1, cols], start=True, stop=True)
                mm = e.transpose(bank[2][:, cols], bc[:, 0, cols], ident[:, :])
            mm.then_inc(g_bc_out, 1)
            e.wait_ge(g_ct, b + 1)
            three_products(e, bank[6][:, 0:NC * SSM_HEADS],
                           [(last_r[:, :], part[:, :, :].rearrange("p c h -> p (c h)")) for part in (ct_hi, ct_lo)],
                           True, True).then_inc(g_last, 1)
            t.together()
            ssm_steps(t, b, ssm_pe_step)
            for o in range(KD):
                e.matmul(bank[o][:, :], zero_b[:, :], zero_r[:, :], start=False, stop=True, skip_group_check=True)
            e.wait_ge(s_acc, done(b * FT + (FT - 1)))
            for i in range(TT):
                e.matmul(bank[2][:, i:i + 1], sq_sum[:, i * P:(i + 1) * P], ones_c[:, :], start=True, stop=True)
            for _ in range(3):
                t.together()
            tail_other(t)
            norm_pe(t)
            route_pe(t, b, 1)
            t.leave(GROUPS)

    def ssm_act(a):
        e = a.e
        for s in (s_wih, s_woh, s_e, s_l, s_cv, s_thx, s_thz, s_sq, s_yhi):
            e.drain().then_inc(s, 3)
        e.wait_ge(s_ssm, SSM_IN)
        a.step(e.activation(a_neg[:, :], a_neg[:, :], ACT.Exp))
        e.activation(wb_hi[:, :, :], wb[:, :, :], ACT.Copy)
        a.together()
        a.together()
        with e.Fori(0, GROUPS) as b:
            a.enter(b, SSM_MEETS, 1, ONE_GROUP)
            norm_act(a, b, 1, 0)
            for n in range(2):
                e.wait_ge(g_proj, b * 4 + n + 1)
                e.activation(dt_u[:, n, :], bank[4 + n][:, :], ACT.Identity, bias=dtb[:, n:n + 1]).then_inc(g_dt, 1)
            for n in range(2):
                e.wait_ge(g_proj, b * 4 + n + 3)
                e.activation(bc[:, n, :], bank[2 + n][:, :], ACT.Identity, bias=cw[:, FT + n, TAPS:TAPS + 1],
                             scale=cw[:, FT + n, TAPS - 1:TAPS]).then_inc(g_bias, 1)
            e.wait_ge(g_abs, b + 1)
            a.step(e.activation(dt_v[:, :, :], dt_v[:, :, :], ACT.Exp))
            e.activation(dt_v[:, :, :], dt_v[:, :, :], ACT.Ln, bias=1.0).then_inc(g_log, 1)
            e.wait_ge(g_taps, b + 1)
            for n, th in enumerate((thx, thg)):
                e.activation(th[:, :], bc[:, n, :], ACT.Tanh, scale=0.5).then_inc(g_tanh, 1)
            e.wait_ge(g_dec, b + 1)
            e.activation(e_last[:, :, :, :].rearrange("p c h f -> p (c h f)"), bank[6][:, 0:NC * SSM_HEADS], ACT.Exp)
            e.activation(dec_tok[:, :, :, :], dec_tok[:, :, :, :], ACT.Exp)
            a.together()
            ssm_steps(a, b, ssm_act_step)
            a.together()
            a.together()
            e.activation(rs[:, 1, :], rs[:, 0, :], ACT.Sqrt)
            a.together()
            tail_other(a)
            norm_act(a, b, 1, 1)
            route_act(a, b, 1)
            a.leave(GROUPS)

    def ssm_dve(v):
        e = v.e
        for s in (s_tap, s_st, s_sg, s_yd, s_xc, s_m, s_xdt, s_ylo):
            e.drain().then_inc(s, 3)
        e.wait_ge(s_ssm, SSM_IN)
        v.together()
        e.tensor_scalar(a_neg[:, :], a_neg[:, :], -1.0, None, ALU.mult)
        e.tensor_scalar(dsk[:, :], dsk[:, :], 0.5, None, ALU.mult)
        e.tensor_tensor(wb_lo[:, :, :], wb[:, :, :], wb_hi[:, :, :].bitcast(FP32), ALU.subtract)
        e.tensor_copy(last_r[:, :], last_f[:, :])
        v.together()
        with e.Fori(0, GROUPS) as b:
            v.enter(b, SSM_MEETS, SSM_STEPS, ONE_GROUP)
            norm_dve(v, b, 1, 0)
            e.wait_ge(g_dt, b * 2 + 2)
            e.scalar_tensor_tensor(out=dt_v[:, :, :], in0=dt_u[:, :, :], scalar=-1.0, in1=dt_u[:, :, :],
                                   op0=ALU.mult, op1=ALU.min).then_inc(g_abs, 1)
            e.wait_ge(g_bias, b * 2 + 2)
            for n in range(1, TAPS):
                for w in range(2):
                    last = e.scalar_tensor_tensor(out=bc[:, w, n:SEQ], in0=bank[2 + w][:, 0:SEQ - n],
                                                  scalar=cw[:, FT + w, TAPS - 1 - n:TAPS - n],
                                                  in1=bc[:, w, n:SEQ], op0=ALU.mult, op1=ALU.add)
                    if n < TAPS - 1:
                        v.own.add(last)
                if n < TAPS - 1:
                    e.wait_ge(s_dve, v.own.now())
            last.then_inc(g_taps, 1)
            e.wait_ge(g_log, b + 1)
            v.step(e.scalar_tensor_tensor(out=dt_t[:, :, :], in0=dt_u[:, :, :], scalar=0.0, in1=dt_v[:, :, :],
                                          op0=ALU.max, op1=ALU.add))
            for hh in range(2):
                v.own.add(e.tensor_scalar(dt_u[:, hh, :], dt_t[:, hh, :], a_neg[:, hh:hh + 1], None, ALU.mult))
            e.wait_ge(s_dve, v.own.now())
            for hh in range(2):
                last = e.tensor_tensor_scan(cum_t[:, hh, :], reset[:, :], dt_u[:, hh, :], 0.0, ALU.mult, ALU.add)
            last.then_inc(g_cum, 1)
            for w, th in enumerate((thx, thg)):
                e.wait_ge(g_tanh, b * 2 + w + 1)
                last = e.scalar_tensor_tensor(out=bc[:, w, :], in0=th[:, :], scalar=1.0, in1=bc[:, w, :],
                                              op0=ALU.add, op1=ALU.mult)
            last.then_inc(g_bc, 1)
            v.own.add(e.memset(sq_sum[:, :], 0.0))
            flat, flat_h = "p c h -> p (c h)", "p c h f -> p (c h f)"
            n = NC * SSM_HEADS
            e.wait_ge(g_turned, b + 1)
            v.step(e.tensor_copy(cum_tok[:, :, :].rearrange(flat), bank[5][:, 0:n]))
            v.step(e.tensor_copy(ct_hi[:, :, :], cum_tok[:, :, :]))
            e.tensor_tensor(ct_lo[:, :, :], cum_tok[:, :, :], ct_hi[:, :, :].bitcast(FP32),
                            ALU.subtract).then_inc(g_ct, 1)
            v.own.add(e.tensor_scalar(dt_tok[:, :, :, :].rearrange(flat_h), bank[4][:, 0:n], 0.5, None, ALU.mult))
            e.wait_ge(g_bc, b + 1)
            v.own.add(e.tensor_scalar(c_t[:, :], bc[:, 1, :], 0.5, None, ALU.mult))
            e.wait_ge(g_cum, b + 1)
            rest = dt_v
            v.step(e.tensor_copy(cum_b[:, :, :], cum_t))
            e.wait_ge(g_last, b + 1)
            e.tensor_tensor(dec_tok[:, :, :, :].rearrange(flat_h), bank[6][:, 0:n],
                            cum_tok[:, :, :].rearrange(flat), ALU.subtract).then_inc(g_dec, 1)
            v.step(e.tensor_tensor(rest[:, :, :], cum_t, cum_b[:, :, :], ALU.subtract))
            v.step(e.tensor_copy(low_p[:, :, :], rest[:, :, :]))
            v.own.add(e.tensor_copy(cum_b[FT:2 * FT, :, :], low_p[FT:2 * FT, :, :]))
            v.own.add(e.tensor_tensor(cum_b[2 * FT:P, :, :], rest[2 * FT:P, :, :], low_p[2 * FT:P, :, :],
                                      ALU.subtract))
            e.wait_ge(g_bc_out, b + 1)
            v.own.add(e.tensor_scalar(g_mat[:, :, :].rearrange(flat), bank[7][:, :], 0.25, None, ALU.mult))
            v.own.add(e.tensor_scalar(b_tok[:, :, :].rearrange(flat), bank[2][:, :], 0.5, None, ALU.mult))
            v.together()
            ssm_steps(v, b, ssm_dve_step)
            v.together()
            v.step(e.tensor_scalar(rs[:, 0, :], bank[2][:, 0:TT], 1.0 / (4 * INNER), EPS, ALU.mult, ALU.add))
            v.together()
            v.together()
            rsqrt_dve(v)
            v.step(e.tensor_scalar(rnorm[:, :], rs[:, 2, :], 0.5, None, ALU.mult))
            tail_dve(v, b, (bank[0], bank[1]), 2, True)
            norm_dve(v, b, 1, 1)
            route_dve(v, b, 1)
            v.leave(GROUPS)

    SSM_STEPS = (2 * NORM_STEPS + 2 * (TAPS - 2) + 1 + 2 + 1 + 2 + 1 + 1 + 3 + 2 + 2 + 1 + 5 + 1
                 + TAIL_STEPS + ROUTE_STEPS[1])

    def ssm_pool(q):
        for s in (s_wil, s_wol, s_yg, s_ce, s_acc, s_xdec):
            q.e.drain().then_inc(s, 3)
        q.together()
        q.together()
        with q.e.Fori(0, GROUPS) as b:
            q.enter(b, SSM_MEETS, 0, ONE_GROUP)
            norm_pool(q)
            for _ in range(SSM_PRE):
                q.together()
            ssm_steps(q, b, ssm_pool_step)
            for _ in range(3):
                q.together()
            tail_other(q)
            norm_pool(q)
            route_pool(q)
            q.leave(GROUPS)

    stages = {"attn": ((attn_sync, attn_act, attn_pool, attn_dve, attn_pe), 4 * GROUPS * ATTN_MEETS),
              "moe0": moe(0), "ssm": ((ssm_sync, ssm_act, ssm_pool, ssm_dve, ssm_pe), 4 * (2 + GROUPS * SSM_MEETS)),
              "moe1": moe(1)}
    begins, over = {}, 4 * SETUP_MEETS
    for name in order:
        begins[name], over = over, over + stages[name][1]

    @block.sync
    def _(sync):
        setup_sync(sync)
        for name in order:
            stages[name][0][0](sync, begins[name])
        sync.wait_ge(met, over)
        sync.dma_start(io["out"].rearrange("b (i p) d -> p (b i) d", p=P), x[:, :, :]).then_inc(s_out, 16)
        sync.wait_ge(s_out, 16)

    @block.scalar
    def _(scalar):
        a = Engine(scalar, "act", s_act)
        setup_act(a)
        for name in order:
            stages[name][0][1](a)

    @block.gpsimd
    def _(pool):
        g = Engine(pool, "pool", None)
        setup_pool(g)
        for name in order:
            stages[name][0][2](g)

    @block.vector
    def _(vector):
        v = Engine(vector, "dve", s_dve)
        setup_dve(v)
        for name in order:
            stages[name][0][3](v)

    @block.tensor
    def _(pe):
        t = Engine(pe, "pe", None)
        setup_pe(t)
        for name in order:
            stages[name][0][4](t)


def bf16_bits(table):
    return (table.astype(np.float32).view(np.uint32) >> 16).astype(np.uint16)


def layout(i):
    c = np.ascontiguousarray
    kp = lambda a: a.reshape(KD, P, -1).transpose(1, 0, 2)
    o = {"x": i["L0_attn_x"]}
    o["ct"] = np.stack([kp(i["L0_c"].T), kp(i["L1_c"].T)], axis=2)
    o["wmod0"], o["wmod1"] = kp(i["L0_wmod"]), kp(i["L1_wmod"])
    gw = np.zeros((D, 2 * P), np.float32)
    gw[:, 0:E0] = i["L0_ffn_gate_w"].T
    gw[:, P:P + E1] = i["L1_ffn_gate_w"]
    o["gw"] = kp(gw)
    o["ident"] = np.eye(P, dtype=np.float32)
    o["ident_b"] = bf16_bits(np.eye(P))
    o["iota_e"] = np.broadcast_to(np.arange(E1, dtype=np.float32), (P, TT, E1))
    names = "qkvo"
    o["wt"] = kp(np.concatenate([i[f"L0_attn_W{n}"].T for n in names], axis=1))
    o["la"] = np.stack([i[f"L0_attn_A{n}"].reshape(LORAS * RANK, D) for n in names], axis=1)
    o["lb"] = np.stack([i[f"L0_attn_B{n}"].transpose(0, 2, 1).reshape(LORAS * RANK, D) for n in names], axis=1)
    o["starts"] = i["L0_attn_lora_start_indices"]
    o["own_id"] = np.repeat(np.arange(LORAS, dtype=np.float32), RANK).reshape(-1, 1)
    o["bnum"] = np.broadcast_to(np.arange(GROUPS, dtype=np.float32)[None, :, None], (LORAS * RANK, GROUPS, LORAS))
    inv = (np.float32(10000.0) ** (-np.arange(0, DK, 2, dtype=np.float32) / np.float32(DK))).astype(np.float32)
    ang = (np.arange(SEQ, dtype=np.float32)[:, None] * inv[None, :]).astype(np.float32)
    trig = np.stack([np.cos(ang), np.sin(ang)]).astype(np.float32)
    o["trig"] = trig.reshape(2, TT, P, DK // 2).transpose(2, 0, 1, 3)
    row = np.arange(P)
    o["mask_a"] = bf16_bits(np.where(row[None, :] > row[:, None], NEG, 0.0))

    def tiles(gate, up, down, rows, j):
        w = np.zeros((3, j * P, D), np.float32)
        w[0, :rows], w[1, :rows], w[2, :rows] = gate, up, down
        w = w.reshape(3, j, P, D)
        first = w[0:2].reshape(2, j, P, KD, P).transpose(1, 4, 0, 3, 2).reshape(j, P, 2 * D)
        return np.concatenate([first, w[2]], axis=2)

    f32 = np.float32
    o["cw"] = np.concatenate([i["L1_attn_conv_w"].reshape(FT + 2, P, TAPS),
                              i["L1_attn_conv_b"].reshape(FT + 2, P, 1)], axis=2).transpose(1, 0, 2)
    o["nw"] = i["L1_attn_norm_w"].reshape(FT, P).T
    o["dsk"] = np.repeat(i["L1_attn_D"], SSM_P).reshape(FT, P).T
    by_parity = lambda a: np.tile(a.reshape(FT, 2, *a.shape[1:]), (4, 1) + (1,) * (a.ndim - 1))
    o["a_log"], o["dt_bias"] = by_parity(i["L1_attn_A_log"]), by_parity(i["L1_attn_dt_bias"])
    win = i["L1_attn_in_proj_w"]
    rows = lambda w: w.reshape(-1, P, KD, P).transpose(0, 3, 2, 1).reshape(-1, P, D)
    z, xs = rows(win[0:INNER]), rows(win[INNER:2 * INNER])
    o["wi"] = np.concatenate([z, xs], axis=2)
    o["wo"] = i["L1_attn_out_proj_w"].T.reshape(FT, P, D)
    dt_rows = win[2 * INNER + 2 * SSM_N:]
    o["wb"] = np.stack([*rows(win[2 * INNER:2 * INNER + 2 * SSM_N]), *rows(by_parity(dt_rows).transpose(1, 0, 2).reshape(2 * P, D))],
                       axis=1)
    one = (row[:, None] % FT == np.arange(FT)[None, :]) & (row[:, None] < 3 * FT)
    o["sel_p"] = bf16_bits(np.stack([one * 1.0, one * -1.0], axis=1))
    o["last_f"] = np.broadcast_to((row == P - 1).astype(f32)[:, None], (P, P))
    o["reset"] = np.broadcast_to((np.arange(SEQ) % P != 0).astype(f32), (P, SEQ))
    o["mask_s"] = bf16_bits(np.tile(np.where(row[None, :] < row[:, None], NEG, 0.0), (1, TT)))

    o["w0"] = tiles(i["L0_ffn_w_gate"].reshape(ROWS0, D), i["L0_ffn_w_up"].reshape(ROWS0, D),
                    i["L0_ffn_w_down"].transpose(0, 2, 1).reshape(ROWS0, D), ROWS0, J0)
    cat = np.concatenate
    o["w1"] = tiles(cat([i["L1_ffn_wg"].transpose(0, 2, 1).reshape(-1, D), i["L1_ffn_sg"].T]),
                    cat([i["L1_ffn_wu"].transpose(0, 2, 1).reshape(-1, D), i["L1_ffn_su"].T]),
                    cat([i["L1_ffn_wd"].reshape(-1, D), i["L1_ffn_sd"]]), ROWS1, J1)

    def selector(owner, j):
        s = np.zeros((P, j * P), np.float32)
        for r, e in enumerate(owner):
            for rows in ((e, e + PART, e + 2 * PART) if e < PART else (3 * PART,)):
                s[rows, r] = 1.0
        return bf16_bits(s)

    o["sel0"] = selector(np.repeat(np.arange(E0), I0), J0)
    o["sel1"] = selector(list(np.repeat(np.arange(E1), I1)) + [PART] * SHARED, J1)
    return {k: c(a) for k, a in o.items()}


def kernel(_order=ORDER, **inputs):
    import concourse.bacc as bacc
    from concourse.bass_utils import run_bass_kernel_spmd

    arrays = layout({k: np.asarray(a) for k, a in inputs.items()})
    nc = bacc.Bacc("TRN2", target_bir_lowering=False, num_devices=1)
    io = {k: nc.dram_tensor("in_" + k, a.shape, mybir.dt.from_np(a.dtype), kind="ExternalInput").ap()
          for k, a in arrays.items()}
    out = (GROUPS, SEQ, D)
    io["out"] = nc.dram_tensor("out_x", out, FP32, kind="ExternalOutput").ap()
    for k, a in arrays.items():
        if a.dtype == np.uint16:
            io[k] = io[k].bitcast(BF16)
    build(nc, io, _order)
    r = run_bass_kernel_spmd(nc, [{"in_" + k: a for k, a in arrays.items()}], core_ids=[0])
    return r.results[0]["out_x"]
```

```python
from contextlib import ExitStack

import numpy as np
import concourse.bass as bass
from concourse import mybir

FP32 = mybir.dt.float32
F32R = mybir.dt.float32r
BF16 = mybir.dt.bfloat16
I32 = mybir.dt.int32
U32 = mybir.dt.uint32
ALU = mybir.AluOpType
ACT = mybir.ActivationFunctionType
AX = mybir.AxisListType

P = 128
D = 256
KD = D // P
GROUPS = 4
SEQ = 512
TT = SEQ // P
HEADS, DK = 16, 16
SLOT = 64
RANK, LORAS = 16, 4
EPS = 1e-5
NEG = -3.0e38
SSM_HEADS, SSM_P, SSM_N = 64, 64, 128
INNER = SSM_HEADS * SSM_P
FT = INNER // P
TAPS = 4
E0, TOP0, I0 = 16, 2, 176
E1, TOP1, I1, SHARED = 32, 6, 96, 192
ROWS0 = E0 * I0
ROWS1 = E1 * I1 + SHARED
J0 = ROWS0 // P
J1 = -(-ROWS1 // (2 * P)) * 2
PART = 32


class Tally:

    def __init__(self, sem, base=0):
        self.sem, self.n, self.turn, self.each = sem, base, None, 0

    def add(self, ins):
        self.n += 1
        ins.then_inc(self.sem, 1)

    def now(self):
        return self.n if self.turn is None else self.turn * self.each + self.n

    def enter(self, turn, each):
        self.turn, self.each, self.first = turn, each, self.n

    def leave(self, turns):
        assert self.n - self.first == self.each, (self.n - self.first, self.each)
        self.turn, self.n = None, self.first + turns * self.each


def build(nc, io, order=("attn", "moe0", "ssm", "moe1")):
    ctx = ExitStack()
    with ctx:
        program(nc, io, ctx, order)


def program(nc, io, ctx, order):
    def sb(name, shape, dt=FP32, where=ctx):
        return where.enter_context(nc.sbuf_tensor(name, shape, dt))

    sems = {}

    def sem(name):
        if name not in sems:
            sems[name] = ctx.enter_context(nc.semaphore(name))
        return sems[name]

    bank = [ctx.enter_context(nc.psum_tensor(f"bank{i}", [P, 512], FP32)) for i in range(8)]

    x = sb("x", [P, GROUPS * TT, D])
    ht_hi = sb("ht_hi", [P, KD, GROUPS * SEQ], F32R)
    ht_lo = sb("ht_lo", [P, KD, GROUPS * SEQ], F32R)
    hb_hi = sb("hb_hi", [P, KD, SEQ], F32R)
    hb_lo = sb("hb_lo", [P, KD, SEQ], F32R)
    mod_t = sb("mod_t", [P, 2, 6, KD, GROUPS])
    gates = sb("gates", [P, 4, GROUPS, D])
    comb_t = sb("comb_t", [P, GROUPS * SEQ], BF16)
    ident = sb("ident", [P, P])
    ident_b = sb("ident_b", [P, P], BF16)
    zero_b = sb("zero_b", [P, P], BF16)
    zero_r = sb("zero_r", [P, 512], BF16)
    ones_c = sb("ones_c", [P, 1])
    iota_e = sb("iota_e", [P, E1])
    stats = sb("stats", [P, GROUPS * TT, 6])
    mv = sb("mv", [P, GROUPS * TT, 2])
    rs = sb("rs", [P, 4, GROUPS * TT])
    xn = sb("xn", [P, TT, D])
    h32 = sb("h32", [P, KD, SEQ])
    outs = sb("outs", [P, 4, SEQ])
    tail_tmp = outs[:, KD:4, :].rearrange("p a (c d) -> p (a c) d", d=D)
    rnorm = sb("rnorm", [P, TT])
    NT = GROUPS * TT
    gw = sb("gw", [P, KD, 2 * P])
    gw_hi = sb("gw_hi", [P, KD, 2 * P], F32R)
    gw_lo = sb("gw_lo", [P, KD, 2 * P], F32R)
    lg, pr = [h32[:, n, :].rearrange("p (i e) -> p i e", i=NT) for n in range(2)]
    msk, eq = [xn[:, 2 * n:2 * n + 2, :].rearrange("p a (i e) -> p (a i) e", e=E1) for n in range(2)]
    comb = outs[:, :, :].rearrange("p a (i e) -> p (a i) e", e=P)
    lg_t = outs[0:E1, :, :].rearrange("p a t -> p (a t)")
    part_b = gw[:, :, :].bitcast(BF16).rearrange("p n (i e) -> p n i e", e=E1)
    top = sb("top", [P, NT, 8])
    top_i = sb("top_i", [P, NT, 8], U32)
    top_f = sb("top_f", [P, NT, 8])
    wsum = sb("wsum", [P, 2, NT])

    met, s_dve, s_act, s_pool = sem("met"), sem("dve_chain"), sem("act_chain"), sem("pool_chain")
    s_in, s_out = sem("inputs_in"), sem("x_out")

    class Engine:

        def __init__(self, e, name, chain):
            self.e, self.name, self.meet = e, name, Tally(met)
            self.own = Tally(chain) if chain is not None else None
            self.calls = {stage: Tally(None) for stage in ("norm", "all", "route")}
            self.passes, self.waited = sem("waits_passed_" + name), False

        def together(self):
            if self.waited:
                self.passed()
            self.e.drain().then_inc(met, 1)
            self.meet.n += 4
            self.e.wait_ge(met, self.meet.now())
            self.passed()

        def passed(self):
            self.e.sem_inc(self.passes, 1)
            self.waited = False

        def step(self, ins):
            self.own.add(ins)
            self.e.wait_ge(self.own.sem, self.own.now())
            self.waited = True

        def call(self, stage):
            self.calls[stage].n += 1
            return self.calls[stage].now()

        def enter(self, turn, meets, steps, calls):
            self.meet.enter(turn, 4 * meets)
            for stage, tally in self.calls.items():
                tally.enter(turn, calls[stage])
            if self.own is not None:
                self.own.enter(turn, steps)

        def leave(self, turns):
            self.meet.leave(turns)
            for tally in self.calls.values():
                tally.leave(turns)
            if self.own is not None:
                self.own.leave(turns)

    block = ctx.enter_context(nc.Block())


    n_var, n_root, n_rows, n_turned, n_high, n_full = (
        sem("norm_" + n) for n in ("variance", "root", "rows", "turned", "high", "full"))

    def norm_dve(v, b, layer, meanwhile=None, last=None):
        c = v.call("norm")
        for i in range(TT):
            v.own.add(v.e.bn_stats(stats[:, i, :], x[:, bass.ds(b * TT + i, 1), :]))
        v.e.wait_ge(s_dve, v.own.now())
        v.passed()
        for i in range(TT):
            v.own.add(v.e.bn_aggr(mv[:, i, :], stats[:, i, :]))
        v.e.wait_ge(s_dve, v.own.now())
        v.e.tensor_scalar(rs[:, 0, 0:TT], mv[:, 0:TT, 1], EPS, None, ALU.add).then_inc(n_var, 1)
        v.e.wait_ge(n_root, c)
        rsqrt_dve(v, TT)
        for i in range(TT):
            v.e.tensor_scalar(xn[:, i, :], x[:, bass.ds(b * TT + i, 1), :], mv[:, i, 0:1],
                              rs[:, 2, i:i + 1], ALU.subtract, ALU.mult).then_inc(n_rows, 1)
        if meanwhile:
            meanwhile()
        v.e.wait_ge(n_turned, c)
        for k in (1, 0):
            if k == 0:
                v.e.wait_ge(n_high, c * KD - 1)
            scale, shift = modulation(b, layer, 0, k)
            v.e.tensor_scalar(h32[:, k, :], bank[k][:, :], scale, shift, ALU.mult, ALU.add).then_inc(n_full, 1)
        v.e.wait_ge(n_full, c * KD)
        for k in range(KD):
            v.e.wait_ge(n_high, c * KD + (k + 1 - KD))
            v.own.add(v.e.tensor_tensor(hb_lo[:, k, :], h32[:, k, :], hb_hi[:, k, :].bitcast(FP32), ALU.subtract))
        if last:
            last()
        v.together()

    def modulation(b, layer, half, k):
        return (mod_t[:, layer, 3 * half + 1, k, bass.ds(b, 1)], mod_t[:, layer, 3 * half + 0, k, bass.ds(b, 1)])

    def rsqrt_dve(v, n):
        v.step(v.e.reciprocal(rs[:, 2, 0:n], rs[:, 1, 0:n]))
        v.step(v.e.tensor_tensor(rs[:, 3, 0:n], rs[:, 0, 0:n], rs[:, 2, 0:n], ALU.mult))
        v.step(v.e.tensor_tensor(rs[:, 3, 0:n], rs[:, 3, 0:n], rs[:, 2, 0:n], ALU.mult))
        v.step(v.e.tensor_scalar(rs[:, 3, 0:n], rs[:, 3, 0:n], -0.5, 1.5, ALU.mult, ALU.add))
        v.step(v.e.tensor_tensor(rs[:, 2, 0:n], rs[:, 2, 0:n], rs[:, 3, 0:n], ALU.mult))

    def norm_act(a, b, layer, last=None):
        c = a.call("norm")
        a.e.wait_ge(n_var, c)
        a.e.activation(rs[:, 1, 0:TT], rs[:, 0, 0:TT], ACT.Sqrt).then_inc(n_root, 1)
        a.e.wait_ge(n_turned, c)
        for k in range(KD):
            scale, shift = modulation(b, layer, 0, k)
            if k == 1:
                a.e.wait_ge(n_full, c * KD - 1)
            a.e.activation(hb_hi[:, k, :], bank[k][:, :], ACT.Identity, bias=shift,
                           scale=scale).then_inc(n_high, 1)
        if last:
            last()
        a.together()

    def norm_pe(t):
        c = t.call("norm")
        for i in range(TT):
            t.e.wait_ge(n_rows, c * TT + (i + 1 - TT))
            for k in range(KD):
                mm = t.e.transpose(bank[k][:, i * P:(i + 1) * P], xn[:, i, k * P:(k + 1) * P], ident[:, :])
        mm.then_inc(n_turned, 1)
        t.together()

    def norm_pool(g):
        g.call("norm")
        g.together()

    NORM_MEETS, NORM_STEPS = 1, TT * 2 + 5 + KD

    (a_var, a_root, a_rows, a_turned, a_high, a_full, a_low) = (
        sem("all_norm_" + n) for n in ("variance", "root", "rows", "turned", "high", "full", "low"))
    xn_of = (xn, outs[:, 0:2, :].rearrange("p a (c d) -> p (a c) d", d=D))
    h32_of = (h32, outs[:, 2:4, :])

    def bank_of(b, k):
        return bank[4 + 2 * (b % 2) + k]

    def norm_all_dve(v, layer):
        c, e = v.call("all"), v.e
        for i in range(NT):
            v.own.add(e.bn_stats(stats[:, i, :], x[:, i, :]))
        e.wait_ge(s_dve, v.own.now())
        v.passed()
        for i in range(NT):
            v.own.add(e.bn_aggr(mv[:, i, :], stats[:, i, :]))
        e.wait_ge(s_dve, v.own.now())
        e.tensor_scalar(rs[:, 0, :], mv[:, :, 1], EPS, None, ALU.add).then_inc(a_var, 1)
        e.wait_ge(a_root, c)
        rsqrt_dve(v, NT)

        def rows(b):
            if b >= 2:
                e.wait_ge(a_turned, (c - 1) * GROUPS + b - 1)
            for i in range(b * TT, (b + 1) * TT):
                last = e.tensor_scalar(xn_of[b % 2][:, i - b * TT, :], x[:, i, :], mv[:, i, 0:1], rs[:, 2, i:i + 1],
                                       ALU.subtract, ALU.mult)
            last.then_inc(a_rows, 1)

        rows(0)
        for b in range(GROUPS):
            done_before = (c - 1) * GROUPS + b
            if b + 1 < GROUPS:
                rows(b + 1)
            e.wait_ge(a_turned, done_before + 1)
            if b >= 2:
                e.wait_ge(a_low, KD * (done_before - 1))
            for k in (1, 0):
                if k == 0:
                    e.wait_ge(a_high, KD * done_before + 1)
                scale, shift = modulation(b, layer, 1, k)
                e.tensor_scalar(h32_of[b % 2][:, k, :], bank_of(b, k)[:, :], scale, shift, ALU.mult,
                                ALU.add).then_inc(a_full, 1)

    def norm_all_act(a, layer):
        c, e = a.call("all"), a.e
        e.wait_ge(a_var, c)
        e.activation(rs[:, 1, :], rs[:, 0, :], ACT.Sqrt).then_inc(a_root, 1)
        for b in range(GROUPS):
            done_before = (c - 1) * GROUPS + b
            e.wait_ge(a_turned, done_before + 1)
            for k in range(KD):
                scale, shift = modulation(b, layer, 1, k)
                if k == 1:
                    e.wait_ge(a_full, KD * done_before + 1)
                e.activation(ht_hi[:, k, b * SEQ:(b + 1) * SEQ], bank_of(b, k)[:, :], ACT.Identity, bias=shift,
                             scale=scale).then_inc(a_high, 1)

    def norm_all_pool(g, layer):
        c = g.call("all")
        for b in range(GROUPS):
            done_before = (c - 1) * GROUPS + b
            for k in range(KD):
                cols = slice(b * SEQ, (b + 1) * SEQ)
                g.e.wait_ge(a_full, KD * (done_before + 1))
                g.e.wait_ge(a_high, KD * done_before + k + 1)
                g.e.tensor_tensor(ht_lo[:, k, cols], h32_of[b % 2][:, k, :], ht_hi[:, k, cols].bitcast(FP32),
                                  ALU.subtract).then_inc(a_low, 1)

    def norm_all_pe(t):
        c = t.call("all")
        for b in range(GROUPS):
            done_before = (c - 1) * GROUPS + b
            t.e.wait_ge(a_rows, done_before + 1)
            if b >= 2:
                t.e.wait_ge(a_full, KD * (done_before - 1))
                t.e.wait_ge(a_high, KD * (done_before - 1))
            for i in range(TT):
                for k in range(KD):
                    mm = t.e.transpose(bank_of(b, k)[:, i * P:(i + 1) * P], xn_of[b % 2][:, i, k * P:(k + 1) * P],
                                       ident[:, :])
            mm.then_inc(a_turned, 1)

    r_turn, r_logits, r_out = sem("route_handed_on"), sem("route_logits"), sem("route_logits_out")
    LOGITS, SCORES_IN, SCORES, COMBINE, COMBINE_TURNED = range(1, 6)

    def handed(c, what):
        return (c - 1) * COMBINE_TURNED + what

    def route_pe(t, layer):
        c = t.call("route")
        w = slice(layer * P, (layer + 1) * P)
        for b in range(GROUPS):
            cols, n = slice(b * SEQ, (b + 1) * SEQ), 0
            t.e.wait_ge(a_low, KD * (GROUPS * (c - 1) + b + 1))
            for k in range(KD):
                for l, r in ((gw_hi, ht_hi), (gw_hi, ht_lo), (gw_lo, ht_hi)):
                    mm = t.e.matmul(bank[b][:, :], l[:, k, w], r[:, k, cols], start=(n == 0), stop=(n == 3 * KD - 1))
                    n += 1
            mm.then_inc(r_logits, 1)
        for b in range(GROUPS):
            t.e.wait_ge(r_out, GROUPS * (c - 1) + b + 1)
            t.passed()
            for i in range(b * TT, (b + 1) * TT):
                mm = t.e.transpose(bank[4][:, i * E1:(i + 1) * E1], lg_t[:, i * P:(i + 1) * P], ident[0:E1, 0:E1])
        mm.then_inc(r_turn, 1)
        t.e.wait_ge(r_turn, handed(c, COMBINE))
        for i in range(NT):
            mm = t.e.transpose(bank[1 + i // TT][:, (i % TT) * P:(i % TT + 1) * P], comb[:, i, :], ident[:, :])
        mm.then_inc(r_turn, 1)

    def route_act(a, layer):
        c = a.call("route")
        a.e.wait_ge(a_low, KD * GROUPS * c)
        for b in range(GROUPS):
            a.e.wait_ge(r_logits, GROUPS * (c - 1) + b + 1)
            a.e.activation(lg_t[:, b * SEQ:(b + 1) * SEQ], bank[b][0:E1, :], ACT.Copy).then_inc(r_out, 1)
        a.e.wait_ge(r_turn, handed(c, SCORES_IN))
        ne = (E0, E1)[layer]
        a.e.activation(pr[:, :, 0:ne], lg[:, :, 0:ne], ACT.Exp, scale=(1.0, -1.0)[layer]).then_inc(r_turn, 1)

    def route_dve(v, layer):
        ne, k_top = (E0, TOP0) if layer == 0 else (E1, TOP1)
        e = v.e
        c = v.call("route")

        def every(col):
            return col.unsqueeze(2).broadcast_to([P, NT, ne])

        e.wait_ge(r_turn, handed(c, LOGITS))
        v.step(e.tensor_copy(lg[:, :, :], bank[4][:, :].rearrange("p (i e) -> p i e", i=NT)))
        if layer == 0:
            v.step(e.tensor_reduce(wsum[:, 0, :], lg[:, :, 0:ne], AX.X, ALU.max, negate=True))
            v.step(e.tensor_tensor(lg[:, :, 0:ne], lg[:, :, 0:ne], every(wsum[:, 0, :]), ALU.add))
        v.passed()
        e.sem_inc(r_turn, 1)
        v.step(e.memset(comb[:, :, :], 0.0))
        v.own.add(e.memset(comb[:, :, 3 * PART:3 * PART + 1], 0.5))
        e.wait_ge(r_turn, handed(c, SCORES))
        if layer == 0:
            v.step(e.tensor_reduce(wsum[:, 1, :], pr[:, :, 0:ne], AX.X, ALU.add))
            v.step(e.reciprocal(wsum[:, 1, :], wsum[:, 1, :]))
            v.step(e.tensor_tensor(pr[:, :, 0:ne], pr[:, :, 0:ne], every(wsum[:, 1, :]), ALU.mult))
        else:
            v.step(e.tensor_scalar(pr[:, :, :], pr[:, :, :], 1.0, None, ALU.add))
            v.step(e.reciprocal(pr[:, :, :], pr[:, :, :]))
        v.passed()
        for i in range(NT):
            v.own.add(e.max(top[:, i, :], pr[:, i, 0:ne]))
        e.wait_ge(s_dve, v.own.now())
        v.passed()
        for i in range(NT):
            v.own.add(e.max_index(top_i[:, i, :], top[:, i, :], pr[:, i, 0:ne]))
        e.wait_ge(s_dve, v.own.now())
        v.step(e.tensor_copy(top_f[:, :, :], top_i[:, :, :]))
        v.step(e.tensor_reduce(wsum[:, 1, :], top[:, :, 0:k_top], AX.X, ALU.add))
        v.step(e.tensor_scalar(wsum[:, 1, :], wsum[:, 1, :], 1e-20, None, ALU.add))
        v.step(e.reciprocal(wsum[:, 1, :], wsum[:, 1, :]))
        v.step(e.tensor_scalar(wsum[:, 1, :], wsum[:, 1, :], 0.5, None, ALU.mult))
        experts = iota_e[:, 0:ne].unsqueeze(1).broadcast_to([P, NT, ne])
        for k in range(k_top):
            chosen = top_f[:, :, k:k + 1].broadcast_to([P, NT, ne])
            dst = msk if k == 0 else eq
            v.step(e.tensor_tensor(dst[:, :, 0:ne], experts, chosen, ALU.is_equal))
            if k:
                v.step(e.tensor_tensor(msk[:, :, 0:ne], msk[:, :, 0:ne], eq[:, :, 0:ne], ALU.add))
        v.step(e.tensor_tensor(msk[:, :, 0:ne], msk[:, :, 0:ne], pr[:, :, 0:ne], ALU.mult))
        whole, rest, last = (comb[:, :, n * PART:n * PART + ne] for n in range(3))
        v.step(e.tensor_tensor(whole, msk[:, :, 0:ne], every(wsum[:, 1, :]), ALU.mult))
        v.step(e.tensor_copy(part_b[:, 0, :, 0:ne], whole))
        v.step(e.tensor_tensor(rest, whole, part_b[:, 0, :, 0:ne], ALU.subtract))
        v.step(e.tensor_copy(part_b[:, 1, :, 0:ne], rest))
        e.tensor_tensor(last, rest, part_b[:, 1, :, 0:ne], ALU.subtract).then_inc(r_turn, 1)
        e.wait_ge(r_turn, handed(c, COMBINE_TURNED))
        for b in range(GROUPS):
            v.own.add(e.tensor_copy(comb_t[:, b * SEQ:(b + 1) * SEQ], bank[1 + b][:, :]))

    ROUTE_MEETS = 1

    def token_major(banks, i):
        return banks[i // 2][:, (i % 2) * D:(i % 2 + 1) * D]

    def tail_dve(v, b, acc, gate, scaled):
        for i in range(TT):
            got = token_major(acc, i)
            g = gates[:, gate, bass.ds(b, 1), :]
            if scaled:
                v.own.add(v.e.scalar_tensor_tensor(out=tail_tmp[:, i, :], in0=got, scalar=rnorm[:, i:i + 1],
                                                   in1=g, op0=ALU.mult, op1=ALU.mult))
            else:
                v.own.add(v.e.tensor_tensor(tail_tmp[:, i, :], got, g, ALU.mult))
        v.e.wait_ge(s_dve, v.own.now())
        for i in range(TT):
            xi = x[:, bass.ds(b * TT + i, 1), :]
            v.own.add(v.e.tensor_tensor(xi, xi, tail_tmp[:, i, :], ALU.add))
        v.e.wait_ge(s_dve, v.own.now())

    TAIL_MEETS, TAIL_STEPS = 1, 2 * TT
    ONE_GROUP = {"norm": 1, "all": 0, "route": 0}

    atn = ExitStack()
    wt = sb("wt", [P, KD, 4 * D], where=atn)
    la = sb("la", [LORAS * RANK, 4, D], where=atn)
    lb = sb("lb", [LORAS * RANK, 4, D], where=atn)
    starts_i = sb("starts_i", [LORAS * RANK, LORAS], I32, where=atn)
    own_id = sb("own_id", [LORAS * RANK, 1], where=atn)
    bnum = sb("bnum", [LORAS * RANK, GROUPS, LORAS], where=atn)
    trig = sb("trig", [P, 2, TT, DK // 2], where=atn)
    mask_a = sb("mask_a", [P, P], BF16, where=atn)
    setup = ExitStack()
    ct = sb("ct", [P, KD, 2, GROUPS], where=setup)
    cth = sb("cth", [P, KD, 2, GROUPS], where=setup)
    cs = sb("cs", [P, KD, 2, GROUPS], where=setup)
    csb = sb("csb", [P, KD, 2, GROUPS, P], where=setup)
    wmod = sb("wmod", [P, 2, KD, 6 * D], where=setup)
    ga = sb("ga", [P, 2, GROUPS, D], where=setup)
    gs = sb("gs", [P, GROUPS, D], where=setup)
    setup.close()

    s_wmod = [sem("wmod0_in"), sem("wmod1_in")]
    s_x_in, c_tanh, c_read = sem("x_in"), sem("condition_tanh"), sem("condition_ready")
    m_done, m_out, m_gate = sem("modulation_products"), sem("gates_out_of_psum"), sem("gates_done")
    FEATURES = [0, 1, 3, 4]
    FEATURE_BANK = [bank[0], bank[7]]
    GATE_BANKS = [(bank[1], bank[2]), (bank[3], bank[4]), (bank[5], bank[6]), (bank[1], bank[2])]
    MOD_UNITS = [("features", 0), ("gate", 0), ("gate", 1), ("features", 1), ("gate", 2), ("gate", 3)]

    def setup_sync(e):
        small = [(ct[:, :, :, :], io["ct"]), (gw[:, :, :], io["gw"]), (ident[:, :], io["ident"]),
                 (ident_b[:, :], io["ident_b"]), (iota_e[:, :], io["iota_e"])]
        assert SETUP_IN == 16 * len(small)
        for dst, src in small:
            e.dma_start(dst, src).then_inc(s_in, 16)
        for layer in range(2):
            e.dma_start(wmod[:, layer, :, :], io[f"wmod{layer}"]).then_inc(s_wmod[layer], 16)
        e.dma_start(x[:, :, :], io["x"].rearrange("b (i p) d -> p (b i) d", p=P)).then_inc(s_x_in, 16)

    SETUP_IN = 16 * 5
    SETUP_MEETS = 1

    def setup_dve(v):
        e = v.e
        v.own.add(e.memset(zero_b[:, :], 0.0))
        v.own.add(e.memset(zero_r[:, :], 0.0))
        v.own.add(e.memset(ones_c[:, :], 1.0))
        e.wait_ge(s_dve, v.own.now())
        e.wait_ge(s_in, SETUP_IN)
        e.wait_ge(c_tanh, 1)
        v.step(e.scalar_tensor_tensor(out=cs[:, :, :, :], in0=cth[:, :, :, :], scalar=1.0, in1=ct[:, :, :, :],
                                      op0=ALU.add, op1=ALU.mult))
        v.step(e.tensor_scalar(cs[:, :, :, :], cs[:, :, :, :], 0.5, None, ALU.mult))
        for k in range(KD):
            e.tensor_copy(csb[:, k, :, :, :],
                          cs[:, k, :, :].unsqueeze(3).broadcast_to([P, 2, GROUPS, P])).then_inc(c_read, 1)
        v.step(e.tensor_copy(gw_hi[:, :, :], gw[:, :, :]))
        v.step(e.tensor_tensor(gw_lo[:, :, :], gw[:, :, :], gw_hi[:, :, :].bitcast(FP32), ALU.subtract))
        for unit, (what, n) in enumerate(MOD_UNITS):
            if what == "features":
                e.wait_ge(m_done, unit + 1)
                got = FEATURE_BANK[n][:, 0:6 * KD * GROUPS].rearrange("p (c k b) -> p c k b", c=6, k=KD)
                for c in FEATURES:
                    v.own.add(e.tensor_scalar(mod_t[:, n, c, :, :], got[:, c, :, :],
                                              1.0 if c in (1, 4) else 0.0, None, ALU.add))
            else:
                g1 = ga[:, n % 2, :, :]
                e.wait_ge(m_out, n + 1)
                v.step(e.scalar_tensor_tensor(out=gs[:, :, :], in0=g1, scalar=-1.0, in1=g1,
                                              op0=ALU.mult, op1=ALU.max))
                v.own.add(e.tensor_scalar(gs[:, :, :], gs[:, :, :], 0.25, None, ALU.max))
                v.step(e.tensor_scalar(g1, g1, 0.0, 2.0, ALU.is_ge, ALU.mult))
                e.scalar_tensor_tensor(out=gates[:, n, :, :], in0=g1, scalar=-1.0, in1=gs[:, :, :],
                                       op0=ALU.add, op1=ALU.mult).then_inc(m_gate, 1)
                e.wait_ge(m_gate, n + 1)
        e.wait_ge(s_x_in, 16)
        v.together()

    def setup_act(a):
        e = a.e
        e.wait_ge(s_in, SETUP_IN)
        e.activation(cth[:, :, :, :], ct[:, :, :, :], ACT.Tanh, scale=0.5).then_inc(c_tanh, 1)
        for unit, (what, n) in enumerate(MOD_UNITS):
            if what == "gate":
                e.wait_ge(m_done, unit + 1)
                if n >= 2:
                    e.wait_ge(m_gate, n - 1)
                for b2, src in enumerate(GATE_BANKS[n]):
                    last = e.activation(ga[:, n % 2, 2 * b2:2 * b2 + 2, :],
                                        src[:, :].rearrange("p (b d) -> p b d", b=2), ACT.Copy)
                last.then_inc(m_out, 1)
        a.together()

    def setup_pool(g):
        g.together()

    def setup_pe(t):
        e = t.e
        e.wait_ge(s_in, SETUP_IN)
        e.wait_ge(c_read, KD)
        for what, n in MOD_UNITS:
            if what == "features":
                e.wait_ge(s_wmod[n], 16)
                for c in FEATURES:
                    for m in range(KD):
                        col = (c * KD + m) * GROUPS
                        for k in range(KD):
                            mm = e.matmul(FEATURE_BANK[n][:, col:col + GROUPS],
                                          wmod[:, n, k, c * D + m * P:c * D + (m + 1) * P],
                                          cs[:, k, n, :], start=(k == 0), stop=(k == KD - 1))
            else:
                layer, c = n // 2, (2, 5)[n % 2]
                if n == 3:
                    e.wait_ge(m_out, 1)
                for b in range(GROUPS):
                    dst = GATE_BANKS[n][b // 2][:, (b % 2) * D:(b % 2 + 1) * D]
                    for k in range(KD):
                        mm = e.matmul(dst, csb[:, k, layer, b, :], wmod[:, layer, k, c * D:(c + 1) * D],
                                      start=(k == 0), stop=(k == KD - 1))
            mm.then_inc(m_done, 1)
        t.together()

    QKV = 3 * D
    lbm = h32[0:LORAS * RANK, :, :].rearrange("p a (c d) -> p (a c) d", d=D)
    starts = sb("starts", [LORAS * RANK, LORAS], where=atn)
    cnt = sb("cnt", [LORAS * RANK, GROUPS, LORAS], where=atn)
    pick = sb("pick", [LORAS * RANK, GROUPS], where=atn)
    work = sb("work", [P, 2 * 1280], where=atn)
    we = work[:, 0:KD * 4 * D].rearrange("p (k n) -> p k n", k=KD)
    we_hi = sb("we_hi", [P, KD, 4 * D], F32R, where=atn)
    we_lo = sb("we_lo", [P, KD, 4 * D], F32R, where=atn)
    rot_t = h32[:, :, :].rearrange("p k (n h f) -> p (k n) h f", n=2, f=DK // 2)
    rot = gw[:, :, :].rearrange("p k (h f) -> p (k h) f", f=DK)
    qt = sb("qt", [P, HEADS // 2, SEQ], F32R, where=atn)
    kt = sb("kt", [P, HEADS // 2, SEQ], F32R, where=atn)
    vv = sb("vv", [P, TT, HEADS, 32], where=atn)
    pp = work[:, :].rearrange("p (a n) -> p a n", a=2)
    pt_all = sb("pt_all", [P, 2 * 1280], where=atn)
    pt = pt_all[:, :].rearrange("p (a n) -> p a n", a=2)
    stack = pt_all[:, 0:2 * HEADS * SLOT].rearrange("p (h s) -> p h s", s=SLOT)
    nmax = sb("nmax", [P, HEADS, TT], where=atn)
    ssum = sb("ssum", [P, HEADS, TT], where=atn)
    rsum = sb("rsum", [P, HEADS, TT], where=atn)
    ot = outs
    on = xn
    atn.close()
    s_atn = sem("attention_in")
    ATN_IN = 16 * 8
    w_b, w_ba, w_sum, w_high = (sem("adapter_" + n) for n in ("b_chosen", "product", "added", "high"))
    s_qkv, s_vout, s_qkread = sem("qkv_done"), sem("values_out"), sem("qk_read")
    s_stack, s_tr, s_trout = sem("stack_ready"), sem("stack_turned"), sem("turned_out")
    PROJ = (0, 6)
    s_s, s_max = sem("scores_done"), sem("max_done")
    s_exp, s_turn, s_ptev, s_pv = sem("probs_done"), sem("probs_turned"), sem("probs_out"), sem("pv_done")
    s_otev, s_ohigh = sem("heads_out"), sem("heads_high")

    QOFF = [0, 128, 384, 768]
    UNITS = [[(3, 0)], [(0, 0), (2, 128)], [(1, 0)]]
    TUNITS = [[(0, 0)], [(1, 0), (3, 384)], [(2, 0)]]
    KOFF = {0: 0, 1: 512, 3: 896, 2: 1024}
    TOFF = [(0, 512), (512, 512), (1024, 256)]

    def attn_sync(e, over):
        loads = [(wt[:, :, :], io["wt"]), (la[:, :, :], io["la"]), (lb[:, :, :], io["lb"]),
                 (starts_i[:, :], io["starts"].rearrange("(o n) -> o n", o=1).broadcast_to([LORAS * RANK, LORAS])),
                 (own_id[:, :], io["own_id"]), (bnum[:, :, :], io["bnum"]), (trig[:, :, :, :], io["trig"]),
                 (mask_a[:, :], io["mask_a"])]
        for dst, src in loads:
            e.dma_start(dst, src).then_inc(s_atn, 16)

    def attn_dve(v):
        e = v.e
        e.wait_ge(s_atn, ATN_IN)
        v.step(e.tensor_copy(starts[:, :], starts_i[:, :]))
        v.step(e.tensor_tensor(cnt[:, :, :], bnum[:, :, :],
                               starts[:, :].unsqueeze(1).broadcast_to([LORAS * RANK, GROUPS, LORAS]), ALU.is_ge))
        v.step(e.tensor_reduce(pick[:, :], cnt[:, :, :], AX.X, ALU.add))
        v.step(e.tensor_scalar(pick[:, :], pick[:, :], -1.0, 0.0, ALU.add, ALU.max))
        v.step(e.tensor_scalar(pick[:, :], pick[:, :], own_id[:, 0:1], None, ALU.is_equal))
        v.own.add(e.memset(vv[:, :, :, :], 0.0))
        e.wait_ge(s_dve, v.own.now())
        with e.Fori(0, GROUPS) as b:
            v.enter(b, ATTN_MEETS, ATTN_STEPS, ONE_GROUP)
            e.tensor_scalar(lbm[:, :, :], lb[:, :, :], pick[:, bass.ds(b, 1)], None, ALU.mult).then_inc(w_b, 1)
            v.own.add(e.memset(stack[:, :, 3 * DK:SLOT], 0.0))

            def effective():
                e.wait_ge(w_ba, b + 1)
                for k in range(KD):
                    for n in range(2):
                        last = e.tensor_tensor(we[:, k, n * 512:(n + 1) * 512], bank[2 + 2 * k + n][:, :],
                                               wt[:, k, n * 512:(n + 1) * 512], ALU.add)
                last.then_inc(w_sum, 1)

            def effective_low():
                e.wait_ge(w_high, b + 1)
                v.own.add(e.tensor_tensor(we_lo[:, :, :], we[:, :, :], we_hi[:, :, :].bitcast(FP32), ALU.subtract))

            norm_dve(v, b, 0, effective, effective_low)
            for i in range(TT):
                g = b * TT + i
                qk = bank[PROJ[i % 2]][:, :].rearrange("p (h f two) -> p h f two", f=DK // 2, two=2)
                cos = trig[:, 0, i, :].unsqueeze(1).broadcast_to([P, 2 * HEADS, DK // 2])
                sin = trig[:, 1, i, :].unsqueeze(1).broadcast_to([P, 2 * HEADS, DK // 2])
                e.wait_ge(s_qkv, g + 1)
                e.wait_ge(s_dve, v.own.now())
                for n, (half, fac) in enumerate(((0, cos), (1, sin), (0, sin), (1, cos))):
                    last = e.tensor_tensor(rot_t[:, n, :, :], qk[:, :, :, half], fac, ALU.mult)
                last.then_inc(s_qkread, 1)
                e.wait_ge(s_qkread, g + 1)
                v.own.add(e.tensor_tensor(rot[:, :, 0:DK // 2], rot_t[:, 0, :, :], rot_t[:, 1, :, :], ALU.subtract))
                v.own.add(e.tensor_tensor(rot[:, :, DK // 2:DK], rot_t[:, 2, :, :], rot_t[:, 3, :, :], ALU.add))
                e.wait_ge(s_dve, v.own.now())
                if i:
                    e.wait_ge(s_tr, g)
                v.step(e.tensor_copy(stack[:, :, 0:DK].bitcast(F32R), rot[:, :, :]))
                v.own.add(e.tensor_tensor(stack[:, 0:HEADS, 2 * DK:3 * DK].bitcast(F32R), rot[:, 0:HEADS, :],
                                          stack[:, 0:HEADS, 0:DK], ALU.subtract))
                v.own.add(e.tensor_tensor(stack[:, HEADS:, DK:2 * DK].bitcast(F32R), rot[:, HEADS:, :],
                                          stack[:, HEADS:, 0:DK], ALU.subtract))
                v.own.add(e.tensor_copy(stack[:, 0:HEADS, DK:2 * DK], stack[:, 0:HEADS, 0:DK]))
                last = e.tensor_copy(stack[:, HEADS:, 2 * DK:3 * DK], stack[:, HEADS:, 0:DK])
                last.then_inc(s_stack, 1)
            v.together()
            for h in range(HEADS):
                for u, unit in enumerate(UNITS):
                    n = 3 * h + u
                    e.wait_ge(s_s, b * (3 * HEADS) + n + 1)
                    for q, col in unit:
                        last = e.tensor_reduce(nmax[:, h, q:q + 1], bank[n % 3][:, col:col + P * (q + 1)],
                                               AX.X, ALU.max, negate=True)
                    last.then_inc(s_max, 1)
                if h >= 1:
                    attn_evac(e, b, h - 1, 0)
            attn_evac(e, b, HEADS - 1, 0)
            v.together()
            v.step(e.reciprocal(rsum[:, :, :], ssum[:, :, :]))
            v.together()
            for i in range(TT):
                src = bank[i][:, :].rearrange("p (h s) -> p h s", s=32)[:, :, 0:DK]
                v.own.add(e.tensor_tensor(on[:, i, :].rearrange("p (h s) -> p h s", s=DK), src,
                                          rsum[:, :, i:i + 1].broadcast_to([P, HEADS, DK]), ALU.mult))
            v.together()
            v.together()
            for k in range(KD):
                e.wait_ge(s_ohigh, b * KD + k + 1)
                v.own.add(e.tensor_tensor(hb_lo[:, k, :], bank[4 + k][:, :], hb_hi[:, k, :].bitcast(FP32),
                                          ALU.subtract))
            v.together()
            v.together()
            tail_dve(v, b, (bank[0], bank[1]), 0, False)
            v.leave(GROUPS)
        norm_all_dve(v, 0)
        route_dve(v, 0)

    def attn_evac(e, b, h, who):
        for u in ((0, 2), (1,))[who]:
            n = 3 * h + u
            e.wait_ge(s_turn, b * (3 * HEADS) + n + 1)
            if h >= 2:
                e.wait_ge(s_pv, b * HEADS + h - 1)
            off, size = TOFF[u]
            src, dst = bank[3 + u][:, 0:size], pt[:, h % 2, off:off + size]
            if who == 0:
                e.tensor_copy(dst, src).then_inc(s_ptev, 1)
            else:
                e.activation(dst, src, ACT.Copy).then_inc(sem("probs_out_act"), 1)

    ATTN_MEETS = NORM_MEETS + 1 + 2 + 2 + 1 + TAIL_MEETS
    ATTN_STEPS = (NORM_STEPS + 1 + 1 + TT * (2 + 1 + 3) + 1 + TT + KD
                  + TAIL_STEPS)

    def attn_act(a):
        e = a.e
        with e.Fori(0, GROUPS) as b:
            a.enter(b, ATTN_MEETS, 0, ONE_GROUP)
            def effective_high():
                e.wait_ge(w_sum, b + 1)
                e.activation(we_hi[:, :, :], we[:, :, :], ACT.Copy).then_inc(w_high, 1)

            norm_act(a, b, 0, effective_high)

            def values(i):
                e.wait_ge(s_qkv, b * TT + i + 1)
                e.activation(vv[:, i, :, 0:DK], bank[PROJ[i % 2] + 1][:, 0:D].rearrange("p (h s) -> p h s", s=DK),
                             ACT.Copy).then_inc(s_vout, 1)

            values(0)
            for i in range(TT):
                if i + 1 < TT:
                    values(i + 1)
                e.wait_ge(s_tr, b * TT + i + 1)
                for n in range(2):
                    e.activation(qt[:, 4 * n:4 * n + 4, i * P:(i + 1) * P],
                                 bank[2 + n][:, :].rearrange("p (h t) -> p h t", h=4), ACT.Copy, scale=0.25)
                for n in range(2):
                    last = e.activation(kt[:, 4 * n:4 * n + 4, i * P:(i + 1) * P],
                                        bank[4 + n][:, :].rearrange("p (h t) -> p h t", h=4), ACT.Copy)
                last.then_inc(s_trout, 1)
            a.together()
            for h in range(HEADS):
                if h >= 2:
                    e.wait_ge(s_turn, b * (3 * HEADS) + 3 * (h - 1))
                for u, unit in enumerate(UNITS):
                    e.wait_ge(s_max, b * (3 * HEADS) + 3 * h + u + 1)
                    for q, col in unit:
                        w = P * (q + 1)
                        last = e.activation(pp[:, h % 2, QOFF[q]:QOFF[q] + w], bank[u][:, col:col + w], ACT.Exp,
                                            bias=nmax[:, h, q:q + 1], accum_out=ssum[:, h, q:q + 1])
                    last.then_inc(s_exp, 1)
                if h >= 1:
                    attn_evac(e, b, h - 1, 1)
                if h >= 4 and h % 4 == 2:
                    attn_out(e, b, h // 4 - 1)
            attn_evac(e, b, HEADS - 1, 1)
            attn_out(e, b, HEADS // 4 - 1)
            a.together()
            a.together()
            a.together()
            a.together()
            for k in range(KD):
                e.activation(hb_hi[:, k, :], bank[4 + k][:, :], ACT.Copy).then_inc(s_ohigh, 1)
            a.together()
            a.together()
            a.leave(GROUPS)
        norm_all_act(a, 0)
        route_act(a, 0)

    def attn_out(e, b, g):
        e.wait_ge(s_pv, b * HEADS + 4 * g + 4)
        e.activation(ot[:, g, :], bank[6 + g % 2][:, :], ACT.Copy).then_inc(s_otev, 1)

    def attn_pe(t):
        e = t.e
        with e.Fori(0, GROUPS) as b:
            t.enter(b, ATTN_MEETS, 0, ONE_GROUP)
            e.wait_ge(w_b, b + 1)
            for k in range(KD):
                for n in range(2):
                    for w in range(2):
                        mm = e.matmul(bank[2 + 2 * k + n][:, w * D:(w + 1) * D], la[:, 2 * n + w, k * P:(k + 1) * P],
                                      lbm[:, 2 * n + w, :], start=True, stop=True)
            mm.then_inc(w_ba, 1)
            norm_pe(t)

            def project(i):
                tok = slice(i * P, (i + 1) * P)
                if i >= 2:
                    e.wait_ge(s_qkread, b * TT + i - 1)
                    e.wait_ge(s_vout, b * TT + i - 1)
                for dst, cols in ((bank[PROJ[i % 2]][:, :], slice(0, 512)),
                                  (bank[PROJ[i % 2] + 1][:, 0:D], slice(512, QKV))):
                    n = 0
                    for k in range(KD):
                        for l, r in ((hb_hi, we_hi), (hb_hi, we_lo), (hb_lo, we_hi)):
                            mm = e.matmul(dst, l[:, k, tok], r[:, k, cols], start=(n == 0), stop=(n == 3 * KD - 1))
                            n += 1
                mm.then_inc(s_qkv, 1)

            project(0)
            for i in range(TT):
                if i + 1 < TT:
                    project(i + 1)
                e.wait_ge(s_stack, b * TT + i + 1)
                if i:
                    e.wait_ge(s_trout, b * TT + i)
                for h in range(HEADS):
                    mm = e.transpose(bank[2 + h // 4][:, (h % 4) * P:(h % 4 + 1) * P],
                                     stack[:, 2 * h:2 * h + 2, :].rearrange("p a s -> p (a s)"), ident[:, :])
                mm.then_inc(s_tr, 1)
            t.together()
            for h in range(HEADS + 2):
                if h < HEADS:
                    rows = slice(SLOT * (h % 2), SLOT * (h % 2) + SLOT)
                    for u, unit in enumerate(UNITS):
                        if h >= 1:
                            e.wait_ge(s_exp, b * (3 * HEADS) + 3 * (h - 1) + u + 1)
                        for q, col in unit:
                            w = P * (q + 1)
                            e.matmul(bank[u][:, col:col + w], qt[rows, h // 2, q * P:(q + 1) * P],
                                     kt[rows, h // 2, 0:w], start=True, stop=False)
                            last = e.matmul(bank[u][:, col + w - P:col + w], ident_b[:, :], mask_a[:, :],
                                            start=False, stop=True)
                        last.then_inc(s_s, 1)
                if 1 <= h <= HEADS:
                    g = h - 1
                    for u, unit in enumerate(TUNITS):
                        e.wait_ge(s_exp, b * (3 * HEADS) + 3 * g + 3)
                        if g >= 1:
                            if u == 1:
                                e.wait_ge(sem("probs_out_act"), b * HEADS + g)
                            else:
                                e.wait_ge(s_ptev, b * (2 * HEADS) + 2 * (g - 1) + (1 if u == 0 else 2))
                        for k, col in unit:
                            for q in range(k, TT):
                                last = e.transpose(bank[3 + u][:, col + (q - k) * P:col + (q - k + 1) * P],
                                                   pp[:, g % 2, QOFF[q] + k * P:QOFF[q] + (k + 1) * P], ident[:, :])
                        last.then_inc(s_turn, 1)
                if h >= 2:
                    g = h - 2
                    e.wait_ge(s_ptev, b * (2 * HEADS) + 2 * g + 2)
                    e.wait_ge(sem("probs_out_act"), b * HEADS + g + 1)
                    if g % 4 == 0 and g >= 8:
                        e.wait_ge(s_otev, b * 4 + g // 4 - 1)
                    rows = slice(32 * (g % 4), 32 * (g % 4) + 32)
                    for k in range(TT):
                        last = e.matmul(bank[6 + (g // 4) % 2][rows, k * P:512], vv[:, k, g, :],
                                        pt[:, g % 2, KOFF[k]:KOFF[k] + SEQ - k * P],
                                        start=(k == 0), stop=(k == TT - 1), tile_position=(0, 32 * (g % 4)))
                    last.then_inc(s_pv, 1)
            t.together()
            for i in range(TT):
                for g in range(4):
                    e.transpose(bank[i][:, g * P:(g + 1) * P], ot[:, g, i * P:(i + 1) * P], ident[:, :])
            t.together()
            t.together()
            for k in range(KD):
                for i in range(TT):
                    e.transpose(bank[4 + k][:, i * P:(i + 1) * P], on[:, i, k * P:(k + 1) * P], ident[:, :])
            for _ in range(2):
                t.together()
            for i in range(TT):
                n = 0
                for k in range(KD):
                    for l, r in ((hb_hi, we_hi), (hb_lo, we_hi), (hb_hi, we_lo)):
                        e.matmul(token_major((bank[0], bank[1]), i), l[:, k, i * P:(i + 1) * P], r[:, k, QKV:4 * D],
                                 start=(n == 0), stop=(n == 3 * KD - 1))
                        n += 1
            t.together()
            t.leave(GROUPS)
        norm_all_pe(t)
        route_pe(t, 0)

    def attn_pool(g):
        with g.e.Fori(0, GROUPS) as b:
            g.enter(b, ATTN_MEETS, 0, ONE_GROUP)
            norm_pool(g)
            for _ in range(ATTN_MEETS - NORM_MEETS - TAIL_MEETS):
                g.together()
            g.together()
            g.leave(GROUPS)
        norm_all_pool(g, 0)

    def moe(layer):
        name, J = f"moe{layer}", (J0, J1)[layer]
        JJ = J // 2
        own = ExitStack()
        WC = 2 * D + D
        sel = sb(name + "_sel", [P, J * P], BF16, where=own)
        raw = sb(name + "_raw", [P, 2, WC], where=own)
        w_hi = sb(name + "_whi", [P, 2, WC], F32R, where=own)
        w_lo = sb(name + "_wlo", [P, 2, WC], F32R, where=own)
        th = sb(name + "_th", [P, 2, SEQ], where=own)
        sg = sb(name + "_sg", [P, 2, SEQ], where=own)
        sc = sb(name + "_sc", [P, 2, SEQ], where=own)
        h = sb(name + "_h", [P, 2, SEQ], where=own)
        h_hi = sb(name + "_hhi", [P, 2, SEQ], F32R, where=own)
        h_lo = sb(name + "_hlo", [P, 2, SEQ], F32R, where=own)
        own.close()
        s_sel = sem(name + "_sel_in")
        s_raw = [sem(f"{name}_raw_in{u}") for u in range(2)]
        s_whi, s_wlo = sem(name + "_w_hi"), sem(name + "_w_lo")
        s_g, s_u, s_c = sem(name + "_gate_done"), sem(name + "_up_done"), sem(name + "_comb_done")
        s_th, s_hhi, s_hlo = sem(name + "_tanh"), sem(name + "_h_hi"), sem(name + "_h_lo")
        s_gu, s_cu, s_h = sem(name + "_gate_used"), sem(name + "_comb_used"), sem(name + "_h")
        s_d = sem(name + "_down_done")
        acc = [[bank[0], bank[1]], [bank[2], bank[3]]]
        B_G, B_U, B_C = bank[4], bank[5], bank[6]
        MEETS = 1
        s_tail = sem(name + "_tails_done")

        def sync(e, over):
            e.wait_ge(met, over - 4 * ROUTE_MEETS)
            e.dma_start(sel[:, :], io[f"sel{layer}"]).then_inc(s_sel, 16)
            with e.Fori(0, 2) as half:
                with e.Fori(0, JJ) as jj:
                    for u in range(2):
                        w = (half * JJ + jj) * 2 + u
                        e.wait_ge(s_whi, w + 1)
                        e.wait_ge(s_wlo, w + 1)
                        e.dma_start(raw[:, u, :], io[f"w{layer}"][bass.ds(jj * 2 + u, 1), :, :]
                                    .rearrange("o p n -> p (o n)")).then_inc(s_raw[u], 16)

        def loop(en, body, finish):
            for half in range(2):
                body(half, 0, True, False)
                with en.e.Fori(1, JJ - 1) as jj:
                    body(half, jj, False, False)
                body(half, JJ - 1, False, True)
                finish(half)
            en.together()

        def act(a):
            e = a.e
            e.drain().then_inc(s_whi, 2)

            def high(half, m_step, m):
                e.wait_ge(s_h, m + 3)
                e.wait_ge(s_d, m + 2)
                e.activation(h_hi[:, m_step % 2, :], h[:, m_step % 2, :], ACT.Copy).then_inc(s_hhi, 1)

            def split(pair, u):
                e.wait_ge(s_raw[u], pair * 16 + 16)
                e.wait_ge(s_d, pair * 4 + (2 * u + 1))
                e.activation(w_hi[:, u, :], raw[:, u, :], ACT.Copy).then_inc(s_whi, 1)

            def body(half, jj, first, last):
                for s in range(4):
                    u, tg = s // 2, s % 2
                    m = half * (4 * JJ) + jj * 4 + s
                    if s == 1:
                        split(half * JJ + jj, 1)
                    if s == 3 and not (last and half == 1):
                        split(half * JJ + jj + 1, 0)
                    if not (first and s == 0):
                        high(half, s + 1, m - 1)
                    e.wait_ge(s_g, m + 1)
                    e.wait_ge(s_gu, m + 1)
                    e.activation(th[:, tg, :], B_G[:, :], ACT.Tanh, scale=0.5).then_inc(s_th, 1)

            def finish(half):
                high(half, 3, half * (4 * JJ) + 4 * JJ - 1)

            split(0, 0)
            a.together()
            loop(a, body, finish)

        def pool(g):
            e = g.e
            e.drain().then_inc(s_wlo, 2)

            def split(w, u):
                e.wait_ge(s_whi, w + 3)
                e.tensor_tensor(w_lo[:, u, :], raw[:, u, :], w_hi[:, u, :].bitcast(FP32),
                                ALU.subtract).then_inc(s_wlo, 1)

            def body(half, jj, first, last):
                for u in range(2):
                    if not (first and half == 0 and u == 0):
                        split((half * JJ + jj) * 2 + u, u)

            split(0, 0)
            g.together()

            loop(g, body, lambda half: None)

        def dve(v):
            e = v.e
            e.drain().then_inc(s_gu, 2)
            e.drain().then_inc(s_cu, 2)
            e.drain().then_inc(s_h, 2)
            e.drain().then_inc(s_hlo, 2)
            e.drain().then_inc(s_tail, 1)

            def low(s, m):
                e.wait_ge(s_hhi, m + 1)
                e.wait_ge(s_d, m + 2)
                e.tensor_tensor(h_lo[:, s % 2, :], h[:, s % 2, :], h_hi[:, s % 2, :].bitcast(FP32),
                                ALU.subtract).then_inc(s_hlo, 1)

            def body(half, jj, first, last):
                for s in range(4):
                    tg = s % 2
                    m = half * (4 * JJ) + jj * 4 + s
                    if not (first and s == 0):
                        low(s + 1, m - 1)
                    e.wait_ge(s_th, m + 1)
                    e.wait_ge(s_cu, m + 1)
                    e.scalar_tensor_tensor(out=sg[:, tg, :], in0=th[:, tg, :], scalar=1.0, in1=B_G[:, :],
                                           op0=ALU.add, op1=ALU.mult).then_inc(s_gu, 1)
                    e.wait_ge(s_c, m + 1)
                    e.wait_ge(s_gu, m + 3)
                    e.wait_ge(s_h, m + 1)
                    e.tensor_tensor(sc[:, tg, :], sg[:, tg, :], B_C[:, :], ALU.mult).then_inc(s_cu, 1)
                    e.wait_ge(s_u, m + 1)
                    e.wait_ge(s_cu, m + 3)
                    e.wait_ge(s_hlo, m + 1)
                    e.tensor_tensor(h[:, tg, :], sc[:, tg, :], B_U[:, :], ALU.mult).then_inc(s_h, 1)
                    if first and half == 1 and s == 0:
                        tails(0)

            def tails(half):
                e.wait_ge(s_d, half * (4 * JJ) + 4 * JJ + 3)
                for tg in range(2):
                    tail_dve(v, half * 2 + tg, acc[tg], 2 * layer + 1, False)
                    e.sem_inc(s_tail, 1)

            def finish(half):
                low(3, half * (4 * JJ) + 4 * JJ - 1)
                if half == 1:
                    tails(1)

            v.together()
            loop(v, body, finish)

        def pe(t):
            e = t.e
            e.drain().then_inc(s_d, 3)
            t.together()
            e.wait_ge(s_sel, 16)

            def down(s, m, u, last=False):
                e.wait_ge(s_hhi, m + 1)
                e.wait_ge(s_hlo, m + 3)
                tg = s % 2
                for i in range(TT):
                    rows = slice(i * P, (i + 1) * P)
                    for n, (l, r) in enumerate(((h_hi, w_hi), (h_lo, w_hi), (h_hi, w_lo))):
                        mm = e.matmul(token_major(acc[tg], i), l[:, tg, rows], r[:, u, 2 * D:3 * D],
                                      start=False, stop=last and n == 2, skip_group_check=True)
                mm.then_inc(s_d, 1)

            def body(half, jj, first, last):
                for s in range(4):
                    u, tg = s // 2, s % 2
                    m = half * (4 * JJ) + jj * 4 + s
                    w = (half * JJ + jj) * 2 + u
                    col = half * (2 * SEQ) + tg * SEQ
                    if tg == 0:
                        e.wait_ge(s_whi, w + 3)
                        e.wait_ge(s_wlo, w + 3)
                    for dst, base, used, done in ((B_G, 0, s_gu, s_g), (B_U, D, s_h, s_u)):
                        e.wait_ge(used, m + 2)
                        n = 0
                        for k in range(KD):
                            rh, rl = ht_hi[:, k, bass.ds(col, SEQ)], ht_lo[:, k, bass.ds(col, SEQ)]
                            cols = slice(base + k * P, base + (k + 1) * P)
                            for l, r in ((w_hi, rh), (w_hi, rl), (w_lo, rh)):
                                mm = e.matmul(dst[:, :], l[:, u, cols], r, start=(n == 0), stop=(n == 3 * KD - 1))
                                n += 1
                        mm.then_inc(done, 1)
                    e.wait_ge(s_cu, m + 2)
                    e.matmul(B_C[:, :], sel[:, bass.ds((jj * 2 + u) * P, P)], comb_t[:, bass.ds(col, SEQ)],
                             start=True, stop=True).then_inc(s_c, 1)
                    if first and s == 1:
                        e.wait_ge(s_tail, half * 2 + 1)
                        for a2 in acc:
                            for o in range(KD):
                                e.matmul(a2[o][:, :], zero_b[:, :], zero_r[:, :], start=True, stop=False,
                                         skip_group_check=True)
                    if not (first and s == 0):
                        down(s + 1, m - 1, ((s + 3) % 4) // 2, last and s == 3)

            def finish(half):
                down(3, half * (4 * JJ) + 4 * JJ - 1, 1, True)

            loop(t, body, finish)

        return (sync, act, pool, dve, pe), 4 * MEETS

    cw = sb("cw", [P, FT + 2, TAPS + 1])
    nw = sb("nw", [P, FT])
    dsk = sb("dsk", [P, FT])
    a_neg = sb("a_neg", [P, 2])
    dtb = sb("dtb", [P, 2])
    wb = sb("wb", [P, 4, D])
    sel_p = sb("sel_p", [P, 2, FT], BF16)
    last_f = sb("last_f", [P, P])
    reset = sb("reset", [P, SEQ])
    mask_s = sb("mask_s", [P, SEQ], BF16)
    ssm_mem = ExitStack()

    def sm(name, shape, dt=FP32):
        return sb(name, shape, dt, where=ssm_mem)

    NC = TT
    wb_hi, wb_lo = sm("wb_hi", [P, 4, D], F32R), sm("wb_lo", [P, 4, D], F32R)
    last_r = sm("last_r", [P, P], F32R)
    raw_i, raw_o = sm("raw_i", [P, 2, 2 * D]), sm("raw_o", [P, 2, D])
    wi_hi, wi_lo = sm("wi_hi", [P, 2, 2 * D], F32R), sm("wi_lo", [P, 2, 2 * D], F32R)
    wo_hi, wo_lo = sm("wo_hi", [P, 2, D], F32R), sm("wo_lo", [P, 2, D], F32R)
    cv = sm("cv", [P, 2, SEQ])
    thx, thg = sm("thx", [P, SEQ]), sm("thg", [P, SEQ])
    xc = sm("xc", [P, 2, SEQ])
    sgt = sm("sgt", [P, 2, SEQ])
    bc = sm("bc", [P, 2, SEQ])
    c_t = sm("c_t", [P, SEQ])
    b_tok = sm("b_tok", [P, NC, P])
    g_mat = sm("g_mat", [P, NC, P])
    cum_b = sm("cum_b", [P, 2, SEQ], BF16)
    cum_tok = sm("cum_tok", [P, NC, SSM_HEADS])
    ct_hi, ct_lo = sm("ct_hi", [P, NC, SSM_HEADS], F32R), sm("ct_lo", [P, NC, SSM_HEADS], F32R)
    dt_tok = sm("dt_tok", [P, NC, 2, FT])
    dec_tok = sm("dec_tok", [P, NC, 2, FT])
    e_last = sm("e_last", [P, NC, 2, FT])
    e_in = h32
    l_mat = sm("l_mat", [P, 2, SEQ])
    m_mat = outs[:, :, :].rearrange("p (s h) t -> p s h t", s=2)
    ce = sm("ce", [P, 2, 2, SEQ - P])
    xdt = xn[:, :, :].rearrange("p (s a) (b f) -> p s (a b) f", s=2, f=P)
    xdec = sm("xdec", [P, NC - 1, P])
    st = sm("st", [P, 2, NC - 1, P])
    yd, yg = sm("yd", [P, SEQ]), sm("yg", [P, SEQ])
    y_hi, y_lo = sm("y_hi", [P, 2, SEQ], F32R), sm("y_lo", [P, 2, SEQ], F32R)
    sq, sq_sum = sm("sq", [P, SEQ]), sm("sq_sum", [P, SEQ])
    dt_t, dt_u, dt_v = outs[:, 0:2, :], outs[:, 2:4, :], l_mat
    cum_t = xn[:, :, :].rearrange("p (n a) d -> p n (a d)", n=2)
    low_p = h32[:, :, :].bitcast(BF16)[:, :, 0:SEQ]
    ssm_mem.close()

    s_ssm = sem("mixer_in")
    s_ri = [sem(f"in_weights_in{u}") for u in range(2)]
    s_ro = [sem(f"out_weights_in{u}") for u in range(2)]
    (s_wih, s_wil, s_woh, s_wol, s_x, s_z, s_cb, s_mk, s_cv, s_thx, s_thz, s_xc, s_sg, s_e, s_l, s_m, s_ce, s_t,
     s_xdt, s_xdec, s_ss, s_y, s_yd, s_yg, s_sq, s_acc, s_yhi, s_ylo, s_o) = [sem("mix_" + n) for n in (
         "in_hi", "in_lo", "out_hi", "out_lo", "x", "z", "cum_bcast", "cum_masked", "conv_first", "tanh_x", "tanh_z",
         "x_conv", "silu_z", "decay_in", "decay_mat", "m_mat", "c_decayed", "x_turned", "x_dt", "x_decayed",
         "state_sums", "y", "y_skip", "y_gated", "squares", "squares_summed", "y_hi", "y_lo", "out")]
    s_tap, s_st = sem("mix_taps"), sem("mix_states")
    PSZ, PSX, PCB, PT, PY = bank[2], bank[3], (bank[4], bank[5]), bank[6], bank[7]
    SSM_IN = 16 * 10
    SSM_PRE = 1
    (g_proj, g_dt, g_bias, g_abs, g_log, g_taps, g_tanh, g_cum, g_turned, g_bc, g_bc_out, g_ct, g_last, g_dec) = [
        sem("group_" + n) for n in ("projected", "dt_in", "bc_bias", "minus_abs", "log", "bc_taps", "bc_tanh",
                                    "running_sums", "turned", "bc", "bc_products", "sums_split", "last_sums",
                                    "decays")]
    SSM_POST = 1 + 2 + TAIL_MEETS
    SSM_MEETS = NORM_MEETS + SSM_PRE + SSM_POST
    AHEAD = 3

    def done(g, each=1):
        return each * g + (each + 3)

    class Tile:

        def __init__(self, b, it, u, back, static):
            self.f = it * 2 + (u - back)
            self.slot = (u - back) % 2
            self.half = it + (u - back) // 2
            self.g = b * FT + self.f
            self.one = slice(self.f, self.f + 1) if static else bass.ds(self.f, 1)
            self.live = not static or 0 <= self.f < FT
            self.b = b
            self.last = static and self.f == FT - 1

    def ssm_steps(en, b, step):
        def run(it, u, static):
            step(en, [Tile(b, it, u, back, static) for back in range(AHEAD + 1)])

        for ft in range(4):
            run(ft // 2, ft % 2, True)
        with en.e.Fori(2, FT // 2) as it:
            for u in range(2):
                run(it, u, False)
        for ft in range(FT, FT + AHEAD):
            run(ft // 2, ft % 2, True)

    def ssm_sync(e, over):
        loads = [(cw[:, :, :], io["cw"]), (nw[:, :], io["nw"]), (dsk[:, :], io["dsk"]), (a_neg[:, :], io["a_log"]),
                 (dtb[:, :], io["dt_bias"]), (wb[:, :, :], io["wb"]), (sel_p[:, :, :], io["sel_p"]),
                 (last_f[:, :], io["last_f"]), (reset[:, :], io["reset"]), (mask_s[:, :], io["mask_s"])]
        for dst, src in loads:
            e.dma_start(dst, src).then_inc(s_ssm, 16)
        def step(_, tiles):
            w = tiles[0]
            if w.live:
                e.wait_ge(s_wih, done(w.g - 2))
                e.wait_ge(s_wil, done(w.g - 2))
                e.dma_start(raw_i[:, w.slot, :], io["wi"][w.one, :, :]
                            .rearrange("o p n -> p (o n)")).then_inc(s_ri[w.slot], 16)
            w = tiles[1]
            if w.live:
                e.wait_ge(s_woh, done(w.g - 2))
                e.wait_ge(s_wol, done(w.g - 2))
                e.dma_start(raw_o[:, w.slot, :], io["wo"][w.one, :, :]
                            .rearrange("o p n -> p (o n)")).then_inc(s_ro[w.slot], 16)

        with e.Fori(0, GROUPS) as b:
            ssm_steps(Engine(e, "sync", None), b, step)

    def ssm_pe_step(t, tiles):
        e = t.e

        def project(w, dst, base, sem_done):
            n = 0
            for k in range(KD):
                cols = slice(base + k * P, base + (k + 1) * P)
                for l, r in ((wi_hi, hb_hi), (wi_hi, hb_lo), (wi_lo, hb_hi)):
                    mm = e.matmul(dst[:, :], l[:, w.slot, cols], r[:, k, :], start=(n == 0), stop=(n == 3 * KD - 1))
                    n += 1
            mm.then_inc(sem_done, 1)

        w = tiles[0]
        if w.live:
            e.wait_ge(s_wih, done(w.g))
            e.wait_ge(s_wil, done(w.g))
            e.wait_ge(s_tap, done(w.g - 1, 3))
            project(w, PSX, D, s_x)
        w = tiles[1]
        if w.live:
            e.wait_ge(s_xc, done(w.g))
            e.wait_ge(s_st, done(w.g - 1, 3))
            for c in range(NC):
                mm = e.transpose(PT[:, c * P:(c + 1) * P], xc[:, w.slot, c * P:(c + 1) * P], ident[:, :])
            mm.then_inc(s_t, 1)
        w = tiles[0]
        if w.live:
            e.wait_ge(s_l, done(w.g - 1))
            for hh in range(2):
                mm = e.matmul(PCB[hh][:, :], sel_p[:, 0, bass.ds(w.f, 1)].broadcast_to([P, P]), cum_b[:, hh, :],
                              start=True, stop=False, skip_group_check=True)
            mm.then_inc(s_cb, 1)
        w = tiles[2]
        if w.live:
            e.wait_ge(s_m, done(w.g))
            e.wait_ge(s_ce, done(w.g))
            e.wait_ge(s_st, done(w.g, 3))
            e.wait_ge(s_yd, done(w.g - 1))
            for c in range(NC):
                for hh in range(2):
                    rows = slice(hh * SSM_P, (hh + 1) * SSM_P)
                    mm = e.matmul(PY[rows, c * P:(c + 1) * P], xdt[:, w.slot, c, rows],
                                  m_mat[:, w.slot, hh, c * P:(c + 1) * P],
                                  start=True, stop=(c == 0), skip_group_check=True)
                for hh in range(2):
                    rows = slice(hh * SSM_P, (hh + 1) * SSM_P)
                    if c:
                        mm = e.matmul(PY[rows, c * P:(c + 1) * P], st[:, w.slot, c - 1, rows],
                                      ce[:, w.slot, hh, (c - 1) * P:c * P], start=False, stop=True,
                                      skip_group_check=True)
            mm.then_inc(s_y, 1)
        w = tiles[0]
        if w.live:
            e.wait_ge(s_sg, done(w.g - 1))
            project(w, PSZ, 0, s_z)
        w = tiles[0]
        if w.live:
            e.wait_ge(s_e, done(w.g))
            for hh in range(2):
                for c in range(NC):
                    cols = slice(c * P, (c + 1) * P)
                    e.matmul(PCB[hh][:, cols], cum_b[:, hh, cols],
                             sel_p[:, 1, bass.ds(w.f, 1)].broadcast_to([P, P]), start=False, stop=False,
                             skip_group_check=True)
                mm = e.matmul(PCB[hh][:, :], ident_b[:, :], mask_s[:, :], start=False, stop=True,
                              skip_group_check=True)
            mm.then_inc(s_mk, 1)
        w = tiles[1]
        if w.live:
            e.wait_ge(s_xdec, done(w.g))
            for c in range(NC - 1):
                mm = e.matmul(PT[:, c * P:(c + 1) * P], b_tok[:, c, :], xdec[:, c, :], start=True, stop=True)
            mm.then_inc(s_ss, 1)
        w = tiles[3]
        if w.live:
            e.wait_ge(s_yhi, done(w.g))
            e.wait_ge(s_ylo, done(w.g))
            e.wait_ge(s_woh, done(w.g))
            e.wait_ge(s_wol, done(w.g))
            end = w.last
            for i in range(TT):
                for n, (l, r) in enumerate(((y_hi, wo_hi), (y_lo, wo_hi), (y_hi, wo_lo))):
                    mm = e.matmul(token_major((bank[0], bank[1]), i), l[:, w.slot, i * P:(i + 1) * P],
                                  r[:, w.slot, :], start=False, stop=end and n == 2, skip_group_check=True)
            mm.then_inc(s_o, 1)

    def ssm_act_step(a, tiles):
        e = a.e
        w = tiles[0]
        if w.live:
            e.wait_ge(s_ri[w.slot], (w.b * (FT // 2) + w.half) * 16 + 16)
            e.wait_ge(s_x, done(w.g - 2))
            e.wait_ge(s_z, done(w.g - 2))
            e.activation(wi_hi[:, w.slot, :], raw_i[:, w.slot, :], ACT.Copy).then_inc(s_wih, 1)
        w = tiles[1]
        if w.live:
            e.wait_ge(s_mk, done(w.g))
            e.wait_ge(s_m, done(w.g - 1))
            for hh in range(2):
                last = e.activation(l_mat[:, hh, :], PCB[hh][:, :], ACT.Exp)
            last.then_inc(s_l, 1)
        w = tiles[1]
        if w.live:
            e.wait_ge(s_tap, done(w.g, 3))
            e.wait_ge(s_xc, done(w.g - 1))
            e.activation(thx[:, :], cv[:, w.slot, :], ACT.Tanh, scale=0.5).then_inc(s_thx, 1)
        w = tiles[2]
        if w.live:
            e.wait_ge(s_ro[w.slot], (w.b * (FT // 2) + w.half) * 16 + 16)
            e.wait_ge(s_o, done(w.g - 2))
            e.activation(wo_hi[:, w.slot, :], raw_o[:, w.slot, :], ACT.Copy).then_inc(s_woh, 1)
        w = tiles[3]
        if w.live:
            e.wait_ge(s_yg, done(w.g))
            e.wait_ge(s_acc, done(w.g - 1))
            e.activation(sq[:, :], yg[:, :], ACT.Square).then_inc(s_sq, 1)
        w = tiles[1]
        if w.live:
            e.wait_ge(s_z, done(w.g))
            e.wait_ge(s_sg, done(w.g - 1))
            e.activation(thg[:, :], PSZ[:, :], ACT.Tanh, scale=0.5).then_inc(s_thz, 1)
        w = tiles[3]
        if w.live:
            e.wait_ge(s_yg, done(w.g))
            e.wait_ge(s_o, done(w.g - 2))
            e.activation(y_hi[:, w.slot, :], yg[:, :], ACT.Identity,
                         scale=nw[:, bass.ds(w.f, 1)]).then_inc(s_yhi, 1)
        w = tiles[0]
        if w.live:
            e.wait_ge(s_cb, done(w.g))
            e.wait_ge(s_ce, done(w.g - 1))
            for hh in range(2):
                last = e.activation(e_in[:, hh, P:SEQ], PCB[hh][:, P:SEQ], ACT.Exp)
            last.then_inc(s_e, 1)
        w = tiles[0]
        if w.live:
            e.wait_ge(s_x, done(w.g))
            e.wait_ge(s_xc, done(w.g - 2))
            e.activation(cv[:, w.slot, :], PSX[:, :], ACT.Identity, bias=cw[:, bass.ds(w.f, 1), TAPS],
                         scale=cw[:, bass.ds(w.f, 1), TAPS - 1]).then_inc(s_cv, 1)

    def ssm_dve_step(v, tiles):
        e = v.e
        w = tiles[1]
        if w.live:
            e.wait_ge(s_cv, done(w.g))
            for n in range(1, TAPS):
                if n > 1:
                    e.wait_ge(s_tap, 3 * w.g + 2 + n)
                e.scalar_tensor_tensor(out=cv[:, w.slot, n:SEQ], in0=PSX[:, 0:SEQ - n],
                                       scalar=cw[:, bass.ds(w.f, 1), TAPS - 1 - n], in1=cv[:, w.slot, n:SEQ],
                                       op0=ALU.mult, op1=ALU.add).then_inc(s_tap, 1)
        w = tiles[2]
        if w.live:
            e.wait_ge(s_ss, done(w.g))
            e.wait_ge(s_y, done(w.g - 2))
            e.tensor_copy(st[:, w.slot, 0, :], PT[:, 0:P]).then_inc(s_st, 1)
            for c in (1, 2):
                e.wait_ge(s_st, 3 * w.g + 3 + c)
                for hh in range(2):
                    cols = slice(hh * SSM_P, (hh + 1) * SSM_P)
                    last = e.scalar_tensor_tensor(out=st[:, w.slot, c, cols], in0=st[:, w.slot, c - 1, cols],
                                                  scalar=e_last[:, c, hh, bass.ds(w.f, 1)],
                                                  in1=PT[:, c * P + hh * SSM_P:c * P + (hh + 1) * SSM_P],
                                                  op0=ALU.mult, op1=ALU.add)
                last.then_inc(s_st, 1)
        w = tiles[1]
        if w.live:
            e.wait_ge(s_thx, done(w.g))
            e.wait_ge(s_yd, done(w.g - 2))
            e.scalar_tensor_tensor(out=xc[:, w.slot, :], in0=thx[:, :], scalar=1.0, in1=cv[:, w.slot, :],
                                   op0=ALU.add, op1=ALU.mult).then_inc(s_xc, 1)
        w = tiles[1]
        if w.live:
            e.wait_ge(s_l, done(w.g))
            e.wait_ge(s_y, done(w.g - 2))
            for hh in range(2):
                last = e.tensor_tensor(m_mat[:, w.slot, hh, :], l_mat[:, hh, :],
                                       g_mat[:, :, :].rearrange("p c l -> p (c l)"), ALU.mult)
            last.then_inc(s_m, 1)
        w = tiles[1]
        if w.live:
            e.wait_ge(s_thz, done(w.g))
            e.wait_ge(s_yg, done(w.g - 2))
            e.scalar_tensor_tensor(out=sgt[:, w.slot, :], in0=thg[:, :], scalar=1.0, in1=PSZ[:, :],
                                   op0=ALU.add, op1=ALU.mult).then_inc(s_sg, 1)
        w = tiles[1]
        if w.live:
            e.wait_ge(s_t, done(w.g))
            e.wait_ge(s_y, done(w.g - 2))
            e.tensor_tensor(xdt[:, w.slot, :, :].rearrange("p c (h f) -> p c h f", h=2),
                            PT[:, :].rearrange("p (c h f) -> p c h f", c=NC, h=2),
                            dt_tok[:, :, :, bass.ds(w.f, 1)].broadcast_to([P, NC, 2, SSM_P]),
                            ALU.mult).then_inc(s_xdt, 1)
        w = tiles[3]
        if w.live:
            e.wait_ge(s_yhi, done(w.g))
            e.wait_ge(s_o, done(w.g - 2))
            e.scalar_tensor_tensor(out=y_lo[:, w.slot, :], in0=yg[:, :], scalar=nw[:, bass.ds(w.f, 1)],
                                   in1=y_hi[:, w.slot, :].bitcast(FP32), op0=ALU.mult,
                                   op1=ALU.subtract).then_inc(s_ylo, 1)
        w = tiles[2]
        if w.live:
            e.wait_ge(s_y, done(w.g))
            e.wait_ge(s_yg, done(w.g - 1))
            e.scalar_tensor_tensor(out=yd[:, :], in0=xc[:, w.slot, :], scalar=dsk[:, bass.ds(w.f, 1)], in1=PY[:, :],
                                   op0=ALU.mult, op1=ALU.add).then_inc(s_yd, 1)

    def ssm_pool_step(q, tiles):
        e = q.e
        w = tiles[0]
        if w.live:
            e.wait_ge(s_wih, done(w.g))
            e.tensor_tensor(wi_lo[:, w.slot, :], raw_i[:, w.slot, :], wi_hi[:, w.slot, :].bitcast(FP32),
                            ALU.subtract).then_inc(s_wil, 1)
        w = tiles[3]
        if w.live:
            e.wait_ge(s_yd, done(w.g))
            e.wait_ge(s_sg, done(w.g))
            e.wait_ge(s_sq, done(w.g - 1))
            e.wait_ge(s_ylo, done(w.g - 1))
            e.tensor_tensor(yg[:, :], yd[:, :], sgt[:, w.slot, :], ALU.mult).then_inc(s_yg, 1)
        w = tiles[1]
        if w.live:
            e.wait_ge(s_e, done(w.g))
            e.wait_ge(s_y, done(w.g - 2))
            for hh in range(2):
                last = e.tensor_tensor(ce[:, w.slot, hh, :], e_in[:, hh, P:SEQ], c_t[:, P:SEQ], ALU.mult)
            last.then_inc(s_ce, 1)
        w = tiles[1]
        if w.live:
            e.wait_ge(s_xdt, done(w.g))
            e.wait_ge(s_ss, done(w.g - 1))
            e.tensor_tensor(xdec[:, :, :].rearrange("p c (h f) -> p c h f", h=2),
                            xdt[:, w.slot, 0:NC - 1, :].rearrange("p c (h f) -> p c h f", h=2),
                            dec_tok[:, 0:NC - 1, :, bass.ds(w.f, 1)].broadcast_to([P, NC - 1, 2, SSM_P]),
                            ALU.mult).then_inc(s_xdec, 1)
        w = tiles[2]
        if w.live:
            e.wait_ge(s_woh, done(w.g))
            e.tensor_tensor(wo_lo[:, w.slot, :], raw_o[:, w.slot, :], wo_hi[:, w.slot, :].bitcast(FP32),
                            ALU.subtract).then_inc(s_wol, 1)
        w = tiles[3]
        if w.live:
            e.wait_ge(s_sq, done(w.g))
            e.wait_ge(s_acc, done(w.g - 1))
            e.tensor_tensor(sq_sum[:, :], sq_sum[:, :], sq[:, :], ALU.add).then_inc(s_acc, 1)

    def three_products(e, dst, pairs, start, stop):
        for n, (l, r) in enumerate(pairs):
            mm = e.matmul(dst, l, r, start=start and n == 0, stop=stop and n == len(pairs) - 1)
        return mm

    def ssm_pe(t):
        e = t.e
        for s in (s_x, s_z, s_cb, s_mk, s_t, s_ss, s_y, s_o):
            e.drain().then_inc(s, 3)
        t.together()
        t.together()
        with e.Fori(0, GROUPS) as b:
            t.enter(b, SSM_MEETS, 0, ONE_GROUP)
            norm_pe(t)
            for w in (2, 3, 0, 1):
                pairs = [(l[:, w, k * P:(k + 1) * P], r[:, k, :]) for k in range(KD)
                         for l, r in ((wb_hi, hb_hi), (wb_hi, hb_lo), (wb_lo, hb_hi))]
                three_products(e, bank[2 + w][:, :], pairs, True, True).then_inc(g_proj, 1)
            for o in range(KD):
                e.matmul(bank[o][:, :], zero_b[:, :], zero_r[:, :], start=True, stop=False, skip_group_check=True)
            e.wait_ge(g_cum, b + 1)
            t.passed()
            for c in range(NC):
                cols = slice(c * P, (c + 1) * P)
                for hh in range(2):
                    hc = slice((c * 2 + hh) * FT, (c * 2 + hh + 1) * FT)
                    e.transpose(bank[5][:, hc], cum_t[0:FT, hh, cols], ident[0:FT, 0:FT])
                    mm = e.transpose(bank[4][:, hc], dt_t[0:FT, hh, cols], ident[0:FT, 0:FT])
            mm.then_inc(g_turned, 1)
            e.wait_ge(g_bc, b + 1)
            for c in range(NC):
                cols = slice(c * P, (c + 1) * P)
                e.matmul(bank[7][:, cols], bc[:, 0, cols], bc[:, 1, cols], start=True, stop=True)
                mm = e.transpose(bank[2][:, cols], bc[:, 0, cols], ident[:, :])
            mm.then_inc(g_bc_out, 1)
            e.wait_ge(g_ct, b + 1)
            three_products(e, bank[6][:, 0:NC * SSM_HEADS],
                           [(last_r[:, :], part[:, :, :].rearrange("p c h -> p (c h)")) for part in (ct_hi, ct_lo)],
                           True, True).then_inc(g_last, 1)
            t.together()
            ssm_steps(t, b, ssm_pe_step)
            e.wait_ge(s_acc, done(b * FT + (FT - 1)))
            for i in range(TT):
                e.matmul(bank[2][:, i:i + 1], sq_sum[:, i * P:(i + 1) * P], ones_c[:, :], start=True, stop=True)
            for _ in range(3):
                t.together()
            t.together()
            t.leave(GROUPS)
        norm_all_pe(t)
        route_pe(t, 1)

    def ssm_act(a):
        e = a.e
        for s in (s_wih, s_woh, s_e, s_l, s_cv, s_thx, s_thz, s_sq, s_yhi):
            e.drain().then_inc(s, 3)
        e.wait_ge(s_ssm, SSM_IN)
        a.step(e.activation(a_neg[:, :], a_neg[:, :], ACT.Exp))
        e.activation(wb_hi[:, :, :], wb[:, :, :], ACT.Copy)
        a.together()
        a.together()
        with e.Fori(0, GROUPS) as b:
            a.enter(b, SSM_MEETS, 1, ONE_GROUP)
            norm_act(a, b, 1)
            for n in range(2):
                e.wait_ge(g_proj, b * 4 + n + 1)
                e.activation(dt_u[:, n, :], bank[4 + n][:, :], ACT.Identity, bias=dtb[:, n:n + 1]).then_inc(g_dt, 1)
            for n in range(2):
                e.wait_ge(g_proj, b * 4 + n + 3)
                e.activation(bc[:, n, :], bank[2 + n][:, :], ACT.Identity, bias=cw[:, FT + n, TAPS:TAPS + 1],
                             scale=cw[:, FT + n, TAPS - 1:TAPS]).then_inc(g_bias, 1)
            e.wait_ge(g_abs, b + 1)
            a.step(e.activation(dt_v[:, :, :], dt_v[:, :, :], ACT.Exp))
            e.activation(dt_v[:, :, :], dt_v[:, :, :], ACT.Ln, bias=1.0).then_inc(g_log, 1)
            e.wait_ge(g_taps, b + 1)
            for n, th in enumerate((thx, thg)):
                e.activation(th[:, :], bc[:, n, :], ACT.Tanh, scale=0.5).then_inc(g_tanh, 1)
            e.wait_ge(g_dec, b + 1)
            e.activation(e_last[:, :, :, :].rearrange("p c h f -> p (c h f)"), bank[6][:, 0:NC * SSM_HEADS], ACT.Exp)
            e.activation(dec_tok[:, :, :, :], dec_tok[:, :, :, :], ACT.Exp)
            a.together()
            ssm_steps(a, b, ssm_act_step)
            a.together()
            a.together()
            e.activation(rs[:, 1, 0:TT], rs[:, 0, 0:TT], ACT.Sqrt)
            a.together()
            a.together()
            a.leave(GROUPS)
        norm_all_act(a, 1)
        route_act(a, 1)

    def ssm_dve(v):
        e = v.e
        for s in (s_tap, s_st, s_sg, s_yd, s_xc, s_m, s_xdt, s_ylo):
            e.drain().then_inc(s, 3)
        e.wait_ge(s_ssm, SSM_IN)
        v.together()
        e.tensor_scalar(a_neg[:, :], a_neg[:, :], -1.0, None, ALU.mult)
        e.tensor_scalar(dsk[:, :], dsk[:, :], 0.5, None, ALU.mult)
        e.tensor_tensor(wb_lo[:, :, :], wb[:, :, :], wb_hi[:, :, :].bitcast(FP32), ALU.subtract)
        e.tensor_copy(last_r[:, :], last_f[:, :])
        v.together()
        with e.Fori(0, GROUPS) as b:
            v.enter(b, SSM_MEETS, SSM_STEPS, ONE_GROUP)
            norm_dve(v, b, 1)
            e.wait_ge(g_dt, b * 2 + 2)
            e.scalar_tensor_tensor(out=dt_v[:, :, :], in0=dt_u[:, :, :], scalar=-1.0, in1=dt_u[:, :, :],
                                   op0=ALU.mult, op1=ALU.min).then_inc(g_abs, 1)
            e.wait_ge(g_bias, b * 2 + 2)
            for n in range(1, TAPS):
                for w in range(2):
                    last = e.scalar_tensor_tensor(out=bc[:, w, n:SEQ], in0=bank[2 + w][:, 0:SEQ - n],
                                                  scalar=cw[:, FT + w, TAPS - 1 - n:TAPS - n],
                                                  in1=bc[:, w, n:SEQ], op0=ALU.mult, op1=ALU.add)
                    if n < TAPS - 1:
                        v.own.add(last)
                if n < TAPS - 1:
                    e.wait_ge(s_dve, v.own.now())
            last.then_inc(g_taps, 1)
            e.wait_ge(g_log, b + 1)
            v.step(e.scalar_tensor_tensor(out=dt_t[:, :, :], in0=dt_u[:, :, :], scalar=0.0, in1=dt_v[:, :, :],
                                          op0=ALU.max, op1=ALU.add))
            for hh in range(2):
                v.own.add(e.tensor_scalar(dt_u[:, hh, :], dt_t[:, hh, :], a_neg[:, hh:hh + 1], None, ALU.mult))
            e.wait_ge(s_dve, v.own.now())
            for hh in range(2):
                last = e.tensor_tensor_scan(cum_t[:, hh, :], reset[:, :], dt_u[:, hh, :], 0.0, ALU.mult, ALU.add)
            last.then_inc(g_cum, 1)
            for w, th in enumerate((thx, thg)):
                e.wait_ge(g_tanh, b * 2 + w + 1)
                last = e.scalar_tensor_tensor(out=bc[:, w, :], in0=th[:, :], scalar=1.0, in1=bc[:, w, :],
                                              op0=ALU.add, op1=ALU.mult)
            last.then_inc(g_bc, 1)
            v.own.add(e.memset(sq_sum[:, :], 0.0))
            flat, flat_h = "p c h -> p (c h)", "p c h f -> p (c h f)"
            n = NC * SSM_HEADS
            e.wait_ge(g_turned, b + 1)
            v.step(e.tensor_copy(cum_tok[:, :, :].rearrange(flat), bank[5][:, 0:n]))
            v.step(e.tensor_copy(ct_hi[:, :, :], cum_tok[:, :, :]))
            e.tensor_tensor(ct_lo[:, :, :], cum_tok[:, :, :], ct_hi[:, :, :].bitcast(FP32),
                            ALU.subtract).then_inc(g_ct, 1)
            v.own.add(e.tensor_scalar(dt_tok[:, :, :, :].rearrange(flat_h), bank[4][:, 0:n], 0.5, None, ALU.mult))
            e.wait_ge(g_bc, b + 1)
            v.own.add(e.tensor_scalar(c_t[:, :], bc[:, 1, :], 0.5, None, ALU.mult))
            e.wait_ge(g_cum, b + 1)
            rest = dt_v
            v.step(e.tensor_copy(cum_b[:, :, :], cum_t))
            e.wait_ge(g_last, b + 1)
            e.tensor_tensor(dec_tok[:, :, :, :].rearrange(flat_h), bank[6][:, 0:n],
                            cum_tok[:, :, :].rearrange(flat), ALU.subtract).then_inc(g_dec, 1)
            v.step(e.tensor_tensor(rest[:, :, :], cum_t, cum_b[:, :, :], ALU.subtract))
            v.step(e.tensor_copy(low_p[:, :, :], rest[:, :, :]))
            v.own.add(e.tensor_copy(cum_b[FT:2 * FT, :, :], low_p[FT:2 * FT, :, :]))
            v.own.add(e.tensor_tensor(cum_b[2 * FT:P, :, :], rest[2 * FT:P, :, :], low_p[2 * FT:P, :, :],
                                      ALU.subtract))
            e.wait_ge(g_bc_out, b + 1)
            v.own.add(e.tensor_scalar(g_mat[:, :, :].rearrange(flat), bank[7][:, :], 0.25, None, ALU.mult))
            v.own.add(e.tensor_scalar(b_tok[:, :, :].rearrange(flat), bank[2][:, :], 0.5, None, ALU.mult))
            v.together()
            ssm_steps(v, b, ssm_dve_step)
            v.together()
            v.step(e.tensor_scalar(rs[:, 0, 0:TT], bank[2][:, 0:TT], 1.0 / (4 * INNER), EPS, ALU.mult, ALU.add))
            v.together()
            v.together()
            rsqrt_dve(v, TT)
            v.step(e.tensor_scalar(rnorm[:, :], rs[:, 2, 0:TT], 0.5, None, ALU.mult))
            v.together()
            tail_dve(v, b, (bank[0], bank[1]), 2, True)
            v.leave(GROUPS)
        norm_all_dve(v, 1)
        route_dve(v, 1)

    SSM_STEPS = (NORM_STEPS + 2 * (TAPS - 2) + 1 + 2 + 1 + 2 + 1 + 1 + 3 + 2 + 2 + 1 + 5 + 1
                 + TAIL_STEPS)

    def ssm_pool(q):
        for s in (s_wil, s_wol, s_yg, s_ce, s_acc, s_xdec):
            q.e.drain().then_inc(s, 3)
        q.together()
        q.together()
        with q.e.Fori(0, GROUPS) as b:
            q.enter(b, SSM_MEETS, 0, ONE_GROUP)
            norm_pool(q)
            for _ in range(SSM_PRE):
                q.together()
            ssm_steps(q, b, ssm_pool_step)
            for _ in range(3):
                q.together()
            q.together()
            q.leave(GROUPS)
        norm_all_pool(q, 1)

    stages = {"attn": ((attn_sync, attn_act, attn_pool, attn_dve, attn_pe), 4 * (GROUPS * ATTN_MEETS + ROUTE_MEETS)),
              "moe0": moe(0), "ssm": ((ssm_sync, ssm_act, ssm_pool, ssm_dve, ssm_pe), 4 * (2 + GROUPS * SSM_MEETS + ROUTE_MEETS)),
              "moe1": moe(1)}
    begins, over = {}, 4 * SETUP_MEETS
    for name in order:
        begins[name], over = over, over + stages[name][1]

    @block.sync
    def _(sync):
        setup_sync(sync)
        for name in order:
            stages[name][0][0](sync, begins[name])
        sync.wait_ge(met, over)
        sync.dma_start(io["out"].rearrange("b (i p) d -> p (b i) d", p=P), x[:, :, :]).then_inc(s_out, 16)
        sync.wait_ge(s_out, 16)

    @block.scalar
    def _(scalar):
        a = Engine(scalar, "act", s_act)
        setup_act(a)
        for name in order:
            stages[name][0][1](a)

    @block.gpsimd
    def _(pool):
        g = Engine(pool, "pool", None)
        setup_pool(g)
        for name in order:
            stages[name][0][2](g)

    @block.vector
    def _(vector):
        v = Engine(vector, "dve", s_dve)
        setup_dve(v)
        for name in order:
            stages[name][0][3](v)

    @block.tensor
    def _(pe):
        t = Engine(pe, "pe", None)
        setup_pe(t)
        for name in order:
            stages[name][0][4](t)


def bf16_bits(table):
    return (table.astype(np.float32).view(np.uint32) >> 16).astype(np.uint16)


def layout(i):
    c = np.ascontiguousarray
    kp = lambda a: a.reshape(KD, P, -1).transpose(1, 0, 2)
    o = {"x": i["L0_attn_x"]}
    o["ct"] = np.stack([kp(i["L0_c"].T), kp(i["L1_c"].T)], axis=2)
    o["wmod0"], o["wmod1"] = kp(i["L0_wmod"]), kp(i["L1_wmod"])
    gw = np.zeros((D, 2 * P), np.float32)
    gw[:, 0:E0] = i["L0_ffn_gate_w"].T
    gw[:, P:P + E1] = i["L1_ffn_gate_w"]
    o["gw"] = kp(gw)
    o["ident"] = np.eye(P, dtype=np.float32)
    o["ident_b"] = bf16_bits(np.eye(P))
    o["iota_e"] = np.broadcast_to(np.arange(E1, dtype=np.float32), (P, E1))
    names = "qkvo"
    o["wt"] = kp(np.concatenate([i[f"L0_attn_W{n}"].T for n in names], axis=1))
    o["la"] = np.stack([i[f"L0_attn_A{n}"].reshape(LORAS * RANK, D) for n in names], axis=1)
    o["lb"] = np.stack([i[f"L0_attn_B{n}"].transpose(0, 2, 1).reshape(LORAS * RANK, D) for n in names], axis=1)
    o["starts"] = i["L0_attn_lora_start_indices"]
    o["own_id"] = np.repeat(np.arange(LORAS, dtype=np.float32), RANK).reshape(-1, 1)
    o["bnum"] = np.broadcast_to(np.arange(GROUPS, dtype=np.float32)[None, :, None], (LORAS * RANK, GROUPS, LORAS))
    inv = (np.float32(10000.0) ** (-np.arange(0, DK, 2, dtype=np.float32) / np.float32(DK))).astype(np.float32)
    ang = (np.arange(SEQ, dtype=np.float32)[:, None] * inv[None, :]).astype(np.float32)
    trig = np.stack([np.cos(ang), np.sin(ang)]).astype(np.float32)
    o["trig"] = trig.reshape(2, TT, P, DK // 2).transpose(2, 0, 1, 3)
    row = np.arange(P)
    o["mask_a"] = bf16_bits(np.where(row[None, :] > row[:, None], NEG, 0.0))

    def tiles(gate, up, down, rows, j):
        w = np.zeros((3, j * P, D), np.float32)
        w[0, :rows], w[1, :rows], w[2, :rows] = gate, up, down
        w = w.reshape(3, j, P, D)
        first = w[0:2].reshape(2, j, P, KD, P).transpose(1, 4, 0, 3, 2).reshape(j, P, 2 * D)
        return np.concatenate([first, w[2]], axis=2)

    f32 = np.float32
    o["cw"] = np.concatenate([i["L1_attn_conv_w"].reshape(FT + 2, P, TAPS),
                              i["L1_attn_conv_b"].reshape(FT + 2, P, 1)], axis=2).transpose(1, 0, 2)
    o["nw"] = i["L1_attn_norm_w"].reshape(FT, P).T
    o["dsk"] = np.repeat(i["L1_attn_D"], SSM_P).reshape(FT, P).T
    by_parity = lambda a: np.tile(a.reshape(FT, 2, *a.shape[1:]), (4, 1) + (1,) * (a.ndim - 1))
    o["a_log"], o["dt_bias"] = by_parity(i["L1_attn_A_log"]), by_parity(i["L1_attn_dt_bias"])
    win = i["L1_attn_in_proj_w"]
    rows = lambda w: w.reshape(-1, P, KD, P).transpose(0, 3, 2, 1).reshape(-1, P, D)
    z, xs = rows(win[0:INNER]), rows(win[INNER:2 * INNER])
    o["wi"] = np.concatenate([z, xs], axis=2)
    o["wo"] = i["L1_attn_out_proj_w"].T.reshape(FT, P, D)
    dt_rows = win[2 * INNER + 2 * SSM_N:]
    o["wb"] = np.stack([*rows(win[2 * INNER:2 * INNER + 2 * SSM_N]), *rows(by_parity(dt_rows).transpose(1, 0, 2).reshape(2 * P, D))],
                       axis=1)
    one = (row[:, None] % FT == np.arange(FT)[None, :]) & (row[:, None] < 3 * FT)
    o["sel_p"] = bf16_bits(np.stack([one * 1.0, one * -1.0], axis=1))
    o["last_f"] = np.broadcast_to((row == P - 1).astype(f32)[:, None], (P, P))
    o["reset"] = np.broadcast_to((np.arange(SEQ) % P != 0).astype(f32), (P, SEQ))
    o["mask_s"] = bf16_bits(np.tile(np.where(row[None, :] < row[:, None], NEG, 0.0), (1, TT)))

    o["w0"] = tiles(i["L0_ffn_w_gate"].reshape(ROWS0, D), i["L0_ffn_w_up"].reshape(ROWS0, D),
                    i["L0_ffn_w_down"].transpose(0, 2, 1).reshape(ROWS0, D), ROWS0, J0)
    cat = np.concatenate
    o["w1"] = tiles(cat([i["L1_ffn_wg"].transpose(0, 2, 1).reshape(-1, D), i["L1_ffn_sg"].T]),
                    cat([i["L1_ffn_wu"].transpose(0, 2, 1).reshape(-1, D), i["L1_ffn_su"].T]),
                    cat([i["L1_ffn_wd"].reshape(-1, D), i["L1_ffn_sd"]]), ROWS1, J1)

    def selector(owner, j):
        s = np.zeros((P, j * P), np.float32)
        for r, e in enumerate(owner):
            for rows in ((e, e + PART, e + 2 * PART) if e < PART else (3 * PART,)):
                s[rows, r] = 1.0
        return bf16_bits(s)

    o["sel0"] = selector(np.repeat(np.arange(E0), I0), J0)
    o["sel1"] = selector(list(np.repeat(np.arange(E1), I1)) + [PART] * SHARED, J1)
    return {k: c(a) for k, a in o.items()}


def kernel(**inputs):
    import concourse.bacc as bacc
    from concourse.bass_utils import run_bass_kernel_spmd

    arrays = layout({k: np.asarray(a) for k, a in inputs.items()})
    nc = bacc.Bacc("TRN2", target_bir_lowering=False, num_devices=1)
    io = {k: nc.dram_tensor("in_" + k, a.shape, mybir.dt.from_np(a.dtype), kind="ExternalInput").ap()
          for k, a in arrays.items()}
    out = (GROUPS, SEQ, D)
    io["out"] = nc.dram_tensor("out_x", out, FP32, kind="ExternalOutput").ap()
    for k, a in arrays.items():
        if a.dtype == np.uint16:
            io[k] = io[k].bitcast(BF16)
    build(nc, io)
    r = run_bass_kernel_spmd(nc, [{"in_" + k: a for k, a in arrays.items()}], core_ids=[0])
    return r.results[0]["out_x"]
```
